# Optimizing a Trainium2 kernel written in Bass

```python
import numpy as np
import jax
import jax.numpy as jnp

def _softmax(x, axis=-1):
    return jax.nn.softmax(x, axis=axis)

def _gelu(x):
    return jax.nn.gelu(x, approximate=True)

def _silu(x):
    return jax.nn.silu(x)

def _sigmoid(x):
    return jax.nn.sigmoid(x)

def _layernorm(x, axis=-1, eps=1e-05):
    m = jnp.mean(x, axis=axis, keepdims=True)
    v = jnp.var(x, axis=axis, keepdims=True)
    return (x - m) / jnp.sqrt(v + eps)

def _scatter_add(tgt, idx, src, axis=0):
    return tgt.at[idx].add(src)

def _segment_sum(src, seg, n):
    return jax.ops.segment_sum(src, seg, n)
kernel_name = 'mk_adaln_d1_jaxref_r4_af8d38'

def setup_inputs(seed: int=0):
    np.random.seed(seed)
    _w = jnp.asarray

    def _L0_attn_setup():
        import math
        import jax, jax.numpy as jnp
        import numpy as np
        E = 256
        H = 16
        D = E // H

        def _l2norm(t, eps=1e-12):
            n = jnp.sqrt(jnp.sum(t * t, axis=-1, keepdims=True))
            return t / jnp.maximum(n, eps)
        key = jax.random.key(seed)
        ks = jax.random.split(key, 10)
        s = 0.02
        x = jax.random.normal(ks[0], (2, 1024, E), dtype=jnp.float32)
        Wq = jax.random.normal(ks[1], (E, E), dtype=jnp.float32) * s
        Wk = jax.random.normal(ks[2], (E, E), dtype=jnp.float32) * s
        Wv = jax.random.normal(ks[3], (E, E), dtype=jnp.float32) * s
        Walpha = jax.random.normal(ks[4], (E, H), dtype=jnp.float32) * s
        Wbeta = jax.random.normal(ks[5], (E, H), dtype=jnp.float32) * s
        A_log = jnp.linspace(0.0, math.log(16.0), H).astype(jnp.float32)
        dt_bias = jnp.zeros((H,), dtype=jnp.float32)
        Wgate = jax.random.normal(ks[6], (E, E), dtype=jnp.float32) * s
        Wout = jax.random.normal(ks[7], (E, E), dtype=jnp.float32) * s
        rms_w = jnp.ones((D,), dtype=jnp.float32)
        return {'x': x, 'Wq': Wq, 'Wk': Wk, 'Wv': Wv, 'Walpha': Walpha, 'Wbeta': Wbeta, 'A_log': A_log, 'dt_bias': dt_bias, 'Wgate': Wgate, 'Wout': Wout, 'rms_w': rms_w}
    _L0_attn_in = _L0_attn_setup()

    def _L0_ffn_setup():
        import jax, jax.numpy as jnp
        import numpy as np
        DIM = 256
        NUM_EXPERTS = 8
        HIDDEN = 1024
        CAP_FACTOR = 2.0
        B, S = (4, 512)
        key = jax.random.key(seed)
        ks = jax.random.split(key, 6)
        scale_r = 1.0 / np.sqrt(DIM)
        scale_1 = 1.0 / np.sqrt(DIM)
        scale_2 = 1.0 / np.sqrt(HIDDEN)
        return {'x': jax.random.normal(ks[0], (B, S, DIM), dtype=jnp.float32), 'router_w': jax.random.uniform(ks[1], (NUM_EXPERTS, DIM), jnp.float32, -scale_r, scale_r), 'w1': jax.random.uniform(ks[2], (NUM_EXPERTS, DIM, HIDDEN), jnp.float32, -scale_1, scale_1), 'b1': jax.random.uniform(ks[3], (NUM_EXPERTS, HIDDEN), jnp.float32, -scale_1, scale_1), 'w2': jax.random.uniform(ks[4], (NUM_EXPERTS, HIDDEN, DIM), jnp.float32, -scale_2, scale_2), 'b2': jax.random.uniform(ks[5], (NUM_EXPERTS, DIM), jnp.float32, -scale_2, scale_2)}
    _L0_ffn_in = _L0_ffn_setup()
    _L0_c = _w((lambda *s: np.random.randn(*s).astype(np.float32) * 0.05)(8, 256))
    _L0_wmod = _w((lambda *s: np.random.randn(*s).astype(np.float32) * 0.05)(256, 6 * 256) * 256 ** (-0.5))
    _d = {'L0_attn_x': _L0_attn_in['x'], 'L0_attn_Wq': _L0_attn_in['Wq'], 'L0_attn_Wk': _L0_attn_in['Wk'], 'L0_attn_Wv': _L0_attn_in['Wv'], 'L0_attn_Walpha': _L0_attn_in['Walpha'], 'L0_attn_Wbeta': _L0_attn_in['Wbeta'], 'L0_attn_A_log': _L0_attn_in['A_log'], 'L0_attn_dt_bias': _L0_attn_in['dt_bias'], 'L0_attn_Wgate': _L0_attn_in['Wgate'], 'L0_attn_Wout': _L0_attn_in['Wout'], 'L0_attn_rms_w': _L0_attn_in['rms_w'], 'L0_ffn_router_w': _L0_ffn_in['router_w'], 'L0_ffn_w1': _L0_ffn_in['w1'], 'L0_ffn_b1': _L0_ffn_in['b1'], 'L0_ffn_w2': _L0_ffn_in['w2'], 'L0_ffn_b2': _L0_ffn_in['b2'], 'L0_c': _L0_c, 'L0_wmod': _L0_wmod}
    _x0 = _d['L0_attn_x']
    _d['L0_attn_x'] = jax.random.normal(jax.random.fold_in(jax.random.key(seed), 1), (8, 1024, 256), dtype=_x0.dtype)
    del _x0
    return _d

def reference(L0_attn_x, L0_attn_Wq, L0_attn_Wk, L0_attn_Wv, L0_attn_Walpha, L0_attn_Wbeta, L0_attn_A_log, L0_attn_dt_bias, L0_attn_Wgate, L0_attn_Wout, L0_attn_rms_w, L0_ffn_router_w, L0_ffn_w1, L0_ffn_b1, L0_ffn_w2, L0_ffn_b2, L0_c, L0_wmod):

    def _L0_attn_ref(x, Wq, Wk, Wv, Walpha, Wbeta, A_log, dt_bias, Wgate, Wout, rms_w):
        import math
        import jax, jax.numpy as jnp
        import numpy as np
        E = 256
        H = 16
        D = E // H

        def _l2norm(t, eps=1e-12):
            n = jnp.sqrt(jnp.sum(t * t, axis=-1, keepdims=True))
            return t / jnp.maximum(n, eps)
        b, s, _ = x.shape
        q = (x @ Wq).reshape(b, s, H, D)
        k = (x @ Wk).reshape(b, s, H, D)
        v = (x @ Wv).reshape(b, s, H, D)
        q = _l2norm(q) / math.sqrt(D)
        k = _l2norm(k)
        dt = jax.nn.softplus(x @ Walpha + dt_bias)
        alpha = jnp.exp(-jnp.exp(A_log) * dt)
        beta = jax.nn.sigmoid(x @ Wbeta)
        qT = jnp.moveaxis(q, 1, 0)
        kT = jnp.moveaxis(k, 1, 0)
        vT = jnp.moveaxis(v, 1, 0)
        aT = jnp.moveaxis(alpha, 1, 0)
        bT = jnp.moveaxis(beta, 1, 0)
        state0 = jnp.zeros((b, H, D, D), dtype=x.dtype)

        def step(state, inp):
            q_t, k_t, v_t, a_t, b_t = inp
            state = a_t[..., None, None] * state
            stored = jnp.einsum('bhij,bhj->bhi', state, k_t)
            delta = b_t[..., None] * (v_t - stored)
            state = state + jnp.einsum('bhi,bhj->bhij', delta, k_t)
            o_t = jnp.einsum('bhij,bhj->bhi', state, q_t)
            return (state, o_t)
        qs = jnp.swapaxes(qT, 1, 2).swapaxes(1, 1)
        _, outs = jax.lax.scan(step, state0, (qT, kT, vT, aT, bT))
        out = jnp.moveaxis(outs, 0, 1)
        var = jnp.mean(out * out, axis=-1, keepdims=True)
        out = out * jax.lax.rsqrt(var + 1e-06) * rms_w
        out = out.reshape(b, s, E)
        gate = jax.nn.silu(x @ Wgate)
        return out * gate @ Wout

    def _L0_ffn_ref(x, router_w, w1, b1, w2, b2):
        import jax, jax.numpy as jnp
        import numpy as np
        DIM = 256
        NUM_EXPERTS = 8
        HIDDEN = 1024
        CAP_FACTOR = 2.0
        B, S = (4, 512)
        Bz, Sz, Dz = x.shape
        E = router_w.shape[0]
        capacity = max(1, int(Sz * CAP_FACTOR / E) + 1)
        scores = jax.nn.softmax(jnp.einsum('bsd,ed->bse', x, router_w), axis=-1)
        scores_t = jnp.swapaxes(scores, 1, 2)
        gate_vals, sel_idx = jax.lax.top_k(scores_t, capacity)
        b_idx = jnp.arange(Bz)[:, None, None]
        tokens = x[b_idx, sel_idx]
        h = jnp.einsum('becd,edh->bech', tokens, w1) + b1[None, :, None, :]
        h = jax.nn.gelu(h, approximate=False)
        y = jnp.einsum('bech,ehd->becd', h, w2) + b2[None, :, None, :]
        gated = y * gate_vals[..., None]
        out = jnp.zeros_like(x).at[b_idx, sel_idx].add(gated)
        return out
    x = L0_attn_x
    mod = (_silu(L0_c) @ L0_wmod).reshape(L0_c.shape[0], 6, 1, -1)
    sa, ca, ga, sb, cb, gb = (mod[:, 0], mod[:, 1], mod[:, 2], mod[:, 3], mod[:, 4], mod[:, 5])
    ga = (2 * (ga >= 0) - 1) * jnp.maximum(jnp.abs(ga), 0.25)
    gb = (2 * (gb >= 0) - 1) * jnp.maximum(jnp.abs(gb), 0.25)
    h = _layernorm(x, axis=-1) * (1 + ca) + sa
    x = x + ga * _L0_attn_ref(h, L0_attn_Wq, L0_attn_Wk, L0_attn_Wv, L0_attn_Walpha, L0_attn_Wbeta, L0_attn_A_log, L0_attn_dt_bias, L0_attn_Wgate, L0_attn_Wout, L0_attn_rms_w)
    h = _layernorm(x, axis=-1) * (1 + cb) + sb
    x = x + gb * _L0_ffn_ref(h, L0_ffn_router_w, L0_ffn_w1, L0_ffn_b1, L0_ffn_w2, L0_ffn_b2)
    return x

_drawn_inputs = setup_inputs


def setup_inputs(seed=0):
    import zlib

    import numpy as np

    out = dict(_drawn_inputs(seed))
    spreads = {'L0_attn_dt_bias': (0.0, 0.8), 'L0_attn_rms_w': (1.0, 0.6)}
    factors = {'L0_attn_Wq': 4.333,
     'L0_attn_Wk': 4.303,
     'L0_attn_Wv': 4.293,
     'L0_attn_Walpha': 8.0,
     'L0_attn_Wbeta': 8.0,
     'L0_attn_A_log': 8.0,
     'L0_attn_Wgate': 4.356,
     'L0_attn_Wout': 4.311,
     'L0_ffn_router_w': 3.985,
     'L0_ffn_w1': 3.728,
     'L0_ffn_b1': 8.0,
     'L0_ffn_w2': 3.497,
     'L0_ffn_b2': 8.0,
     'L0_c': 2.715,
     'L0_wmod': 2.701}
    for name, (base, spread) in spreads.items():
        noise = np.random.default_rng([zlib.crc32(name.encode()), seed]).standard_normal(out[name].shape)
        drawn = base * np.exp(spread * noise) if base else spread * noise
        out[name] = jnp.asarray(drawn.astype(out[name].dtype))
    for name, factor in factors.items():
        out[name] = (out[name] * factor).astype(out[name].dtype)
    return out
```

```python
from contextlib import ExitStack

import concourse.bass as bass
from concourse import mybir

F32 = mybir.dt.float32
U32 = mybir.dt.uint32
ALU = mybir.AluOpType
ACT = mybir.ActivationFunctionType
AX = mybir.AxisListType

P = 128
B, T, E, H, D = 8, 1024, 256, 16, 16
C = 16
NCH = T // C
HG = H * D // P
HP = H // HG
U = HG * B
KC = E // P
NE = 8
HID = 1024
CAP = T * 2 // NE + 1
ROUNDS = -(-CAP // 8)
UNROLL = 4
WIDE = 96
PAD = WIDE // C - 1

LAG_PROJ, LAG_GRAM, LAG_REC, LAG_OUT, LAG_ROUTE, LAG_SCORE = 1, 2, 5, 6, 7, 8
STEPS = NCH + LAG_SCORE
HEAD = 12

LOG1P = [1.0 / k for k in range(13, 1, -2)]


def bcast(ap, shape):
    return ap.to_broadcast(shape)


def program(nc, x, wq, wk, wv, walpha, wbeta, a_log, dt_bias, wgate, wout, rms_w,
            router_w, w1, b1, w2, b2, cond, wmod, out, debug=None):
    with ExitStack() as ctx:
        def sb(name, shape, dt=F32):
            return ctx.enter_context(nc.sbuf_tensor(name, shape, dt))

        def sem(name):
            return ctx.enter_context(nc.semaphore(name))

        def sems(names):
            return {n: sem(n) for n in names.split()}

        h2_dram = nc.dram_tensor("h2_rows", (B * T, E), F32).ap()
        score_dram = nc.dram_tensor("scores", (NE, B, T), F32).ap()

        ident = sb("ident", [P, P])
        head_mask = sb("head_mask", [P, HP])
        ident_rep = sb("ident_rep", [P, U, C])
        head_ones = sb("head_ones", [P, P])
        eps_ln = sb("eps_ln", [P, 1])
        eps_rms = sb("eps_rms", [P, 1])
        one = sb("one", [P, 1])
        zero = sb("zero", [P, 1])
        mod = sb("mod", [P, 6, E])
        SA, CA, GA, SB_, CB, GB = range(6)
        gb_col = sb("gb_col", [P, KC, B])
        neg_rate = sb("neg_rate", [P, H])
        dtb = sb("dtb", [P, 2 * H])
        w_in = {n: sb(f"w_{n}", [P, KC, E]) for n in ("q", "k", "v", "g")}
        w_ab = sb("w_ab", [P, KC, 2 * H])
        w_out = sb("w_out", [P, HG, E])
        rms_col = sb("rms_col", [P, 1])
        router_t = sb("router_t", [P, KC, NE])

        banks = [ctx.enter_context(nc.psum_tensor(f"bank{i}", [P, 512], F32)) for i in range(4)]
        gram = ctx.enter_context(nc.psum_tensor("gram", [P, U, 2 * C], F32))
        chain = ctx.enter_context(nc.psum_tensor("chain", [P, 2, 2 * U, C], F32))
        obank = ctx.enter_context(nc.psum_tensor("obank", [P, 2, E], F32))
        zbank, qkbank, vgbank, tbank = banks

        K = sems("c_pool c_vec c_act c_pe c_in")

        x_v = x.rearrange("b (n i) e -> n b i e", i=C)
        out_v = out.rearrange("b (n i) e -> n b i e", i=C)
        h2_v = h2_dram.rearrange("(b n i) e -> n b i e", b=B, i=C)
        score_v = score_dram.rearrange("e b (n i) -> n e b i", i=C)

        def rows(ap):
            return ap

        with ExitStack() as mixer:
            def mb(name, shape, dt=F32):
                return mixer.enter_context(nc.sbuf_tensor(name, shape, dt))

            x4 = mb("x4", [P, 4, E])
            stats = mb("stats", [P, 6])
            mv = mb("mv", [P, 2])
            rstd = mb("rstd", [P, 2])
            xn = mb("xn", [P, E])
            h = mb("h", [P, E])
            hT2 = mb("hT2", [P, 2, KC, P])
            sqk = mb("sqk", [P, 4, P])
            inv_norm = mb("inv_norm", [P, 4, P])
            kq2 = mb("kq2", [P, 2, U, 2 * C])
            head_side = mb("head_side", [P, 2])
            kv_pair = mb("kv_pair", [P, 2, U, 2, C])
            kv_turn = mb("kv_turn", [P, 2, U, 2, C])
            k_diag4 = mb("k_diag4", [P, 4, U, HP, C])
            kt_diag = mb("kt_diag", [P, U, HP, C])
            gate8 = mb("gate8", [P, 8, HG, P])
            sig = mb("sig", [P, 3, E])
            z32 = mb("z32", [P, 2 * H])
            w32 = mb("w32", [P, 2 * H])
            u32 = mb("u32", [P, 2 * H])
            den = mb("den", [P, 2 * H])
            rec = mb("rec", [P, 2 * H])
            ser = mb("ser", [P, 6, H])
            decay_rep = mb("decay_rep", [P, 2, H, C])
            alpha0 = mb("alpha0", [P, U, C])
            start0 = mb("start0", [P, U, C])
            beta4 = mb("beta4", [P, 4, U, C])
            dec4 = mb("dec4", [P, 4, U, C])
            gam4 = mb("gam4", [P, 4, U, C])
            gq4 = mb("gq4", [P, 4, U + PAD, C])
            gtmp = mb("gtmp", [P, U, C])
            gcol4 = mb("gcol4", [P, 4, U])
            ap4 = mb("ap4", [P, 4, U + PAD, 2, C])
            kv4 = mb("kv4", [P, 4, U, 2, C])
            low = mb("low", [P, 2, 2 * P * 2])
            solved = mb("solved", [P, C, 2, C])
            solved_b = mb("solved_b", [P, C, 2, C])
            prod = mb("prod", [P, 2 * C * C])
            t2 = mb("t2", [P, 2, 2, U, C])
            t_diag2 = mb("t_diag2", [P, 2, U, HP, C])
            s2 = mb("s2", [P, 2, U + PAD, C])
            s_diag = mb("s_diag", [P, U, HP, C])
            sg = mb("sg", [P, U, C])
            rhs = mb("rhs", [P, 2, U + PAD, C])
            delta = mb("delta", [P, 2, U + PAD, C])
            d_diag = mb("d_diag", [P, U, HP, C])
            o_c = mb("o_c", [P, E])
            o_sq = mb("o_sq", [P, E])
            o_r = mb("o_r", [P, 2, E])
            og = mb("og", [P, 2, HG, P])
            xr2 = mb("xr2", [P, 2, E])
            x2_2 = mb("x2_2", [P, 2, E])
            xn2 = mb("xn2", [P, E])
            h2_2 = mb("h2_2", [P, 2, E])
            stats2 = mb("stats2", [P, 6])
            mv2 = mb("mv2", [P, 2])
            rstd2 = mb("rstd2", [P, 2])
            tick = mb("tick", [P, 1])
            h2T = mb("h2T", [P, KC, P])
            logit = mb("logit", [P, NE])
            nmax = mb("nmax", [P, 1])
            esum = mb("esum", [P, 2])
            expl = mb("expl", [P, NE])
            sc = mb("sc", [P, NE])
            scT4 = mb("scT4", [NE, 4, P])

            wm = k_diag4[:, 0:2].rearrange("p r u g c -> p (r u g c)")[:, 0:KC * 6 * E] \
                .rearrange("p (k n) -> p k n", k=KC)
            cT = sqk[:, 0:KC, :]

            XS = [sem(f"x_loaded{i}") for i in range(4)]
            XR = [sem(f"residual_loaded{i}") for i in range(4)]
            XO = [sem(f"x2_stored{i}") for i in range(4)]
            HO = [sem(f"h2_stored{i}") for i in range(4)]
            SO = [sem(f"scores_stored{i}") for i in range(4)]
            M = sems("stats_done mean_done ln_rstd rstd_done xn_done hmul_done h_done xt_done hT_done "
                     "proj_done z_done sq_done kpair_done vpair_done kvturn_done gate_e gate_l gate_s gate_done ss_done lnss_done "
                     "inv_done k_done q_done decay_steps expz_done alpha_done beta_done ab_done "
                     "alpha0_done start0_done beta_copied dec_done gam_done gtmp_done gcol_done gq_done "
                     "kdiag_done gram_done ap_done kv_done ktdiag_done lanes_steps t_done tdiag_done "
                     "ks_done gks_done rhs_done delta_mm delta_done ddelta_done ddiag_done sg_done "
                     "su_done state_done sdiag_done o_mm oc_done osq_done ms_done lnms_done rms_done "
                     "og1_done og_done y_done yga_done x2_done stats2_done mean2_done ln_rstd2 "
                     "rstd2_done xn2_done h2mul_done h2_done h2t_mm h2T_done rl_done logit_done "
                     "max_done expl_done esum_done sc_done st_done scT_done")

            def act_on(c):
                return not isinstance(c, int) or 0 <= c < NCH

            def wait(eng, name, c, per=1, plus=None):
                if isinstance(c, int) and c < 0:
                    return
                eng.wait_ge(M[name], c * per + (per if plus is None else plus))

            def wait_ring(eng, ring, c, slot):
                if isinstance(c, int) and c < 0:
                    return
                eng.wait_ge(ring[slot], (c - slot) * 4 + 16)

            def run(eng, step):
                for n in range(HEAD):
                    step(n, n % UNROLL)
                with eng.Fori(HEAD // UNROLL, NCH // UNROLL) as m:
                    for k in range(UNROLL):
                        step(m * UNROLL + k, k)
                for n in range(NCH, STEPS):
                    step(n, n % UNROLL)

            def slot(k, lag, size=4):
                return (k - lag) % size

            DECAY = 12 + len(LOG1P)
            LANES = 4 + 2 * (C - 1)
            LOADS = 12 + HP
            SETUP_POOL = 18
            SETUP_ACT = 5
            SILU_VEC = 4 + C + HG + 3
            COND_VEC = SILU_VEC + 2 * KC
            SETUP_VEC = COND_VEC + 12

            with nc.Block() as block:
                @block.sync
                def _(sp):
                    loads = [(w_in["q"], wq), (w_in["k"], wk), (w_in["v"], wv), (w_in["g"], wgate)]
                    sp.dma_start(wm, wmod.rearrange("(k p) n -> p k n", p=P)).then_inc(K["c_in"], 16)
                    for dst, src in loads:
                        sp.dma_start(dst[:], src.rearrange("(k p) n -> p k n", p=P)).then_inc(K["c_in"], 16)
                    sp.dma_start(w_ab[:, :, 0:H], walpha.rearrange("(k p) n -> p k n", p=P)).then_inc(K["c_in"], 16)
                    sp.dma_start(w_ab[:, :, H:2 * H], wbeta.rearrange("(k p) n -> p k n", p=P)).then_inc(K["c_in"], 16)
                    sp.dma_start(w_out[:], wout.rearrange("(g p) n -> p g n", p=P)).then_inc(K["c_in"], 16)
                    sp.dma_start(z32[:, 0:H], a_log.partition_broadcast(P)).then_inc(K["c_in"], 16)
                    sp.dma_start(dtb[:, 0:H], dt_bias.partition_broadcast(P)).then_inc(K["c_in"], 16)
                    for g in range(HP):
                        sp.dma_start(rms_col[g * D:(g + 1) * D, :], rms_w.unsqueeze(1)).then_inc(K["c_in"], 16)
                    sp.dma_start(xn[0:NE, :], router_w).then_inc(K["c_in"], 16)
                    sp.dma_start(h[0:B, :], cond).then_inc(K["c_in"], 16)

                    sp.wait_ge(K["c_vec"], SETUP_VEC)

                    def step(n, k):
                        if act_on(n):
                            wait(sp, "xn_done", n - 4)
                            sp.dma_start(rows(x4[:, k, :]), x_v[n]).then_inc(XS[k], 16)
                        o, ko = n - LAG_OUT + 1, slot(k, LAG_OUT - 1)
                        if act_on(o):
                            wait(sp, "x2_done", o - 2)
                            sp.dma_start(rows(xr2[:, ko % 2, :]), x_v[o]).then_inc(XR[ko], 16)
                        o, ko = n - LAG_ROUTE, slot(k, LAG_ROUTE)
                        if act_on(o):
                            wait(sp, "x2_done", o)
                            sp.dma_start(out_v[o], rows(x2_2[:, ko % 2, :])).then_inc(XO[ko], 16)
                            wait(sp, "h2_done", o)
                            sp.dma_start(h2_v[o], rows(h2_2[:, ko % 2, :])).then_inc(HO[ko], 16)
                        o, ko = n - LAG_SCORE, slot(k, LAG_SCORE)
                        if act_on(o):
                            wait(sp, "scT_done", o)
                            sp.dma_start(score_v[o], scT4[:, ko, :].rearrange("e (b i) -> e b i", i=C)) \
                                .then_inc(SO[ko], 16)
                    run(sp, step)
                    for ring in (XO, HO, SO):
                        for s in ring:
                            sp.wait_ge(s, 16 * (NCH // 4))

                @block.gpsimd
                def _(pool):
                    count = [0]

                    def link(ins):
                        count[0] += 1
                        ins.then_inc(K["c_pool"], 1)
                        pool.wait_ge(K["c_pool"], count[0])

                    link(pool.memset(ident[:], 0.0))
                    link(pool.memset(head_mask[:], 1.0))
                    link(pool.affine_select(out=ident[:], in_=ident[:], compare_op=ALU.not_equal, fill=1.0,
                                            base=0, pattern=[[-1, P]], channel_multiplier=1))
                    link(pool.affine_select(out=head_mask[:], in_=head_mask[:], compare_op=ALU.is_ge, fill=0.0,
                                            base=0, pattern=[[-D, HP]], channel_multiplier=1))
                    link(pool.affine_select(out=head_mask[:], in_=head_mask[:], compare_op=ALU.is_ge, fill=0.0,
                                            base=D - 1, pattern=[[D, HP]], channel_multiplier=-1))
                    link(pool.tensor_copy(head_ones[:].rearrange("p (h r) -> p h r", r=D),
                                          bcast(head_mask[:].unsqueeze(2), [P, HP, D])))
                    for tile, value in ((eps_ln, 1e-5), (eps_rms, 1e-6), (one, 1.0), (zero, 0.0)):
                        link(pool.memset(tile[:], value))
                    link(pool.memset(dtb[:, H:], 0.0))
                    for tile in (alpha0, start0, s2, gq4, ap4, rhs, delta):
                        link(pool.memset(tile[:], 0.0))

                    def diag(dst, src):
                        return pool.tensor_tensor(
                            out=dst, in0=bcast(src.unsqueeze(2), [P, U, HP, C]),
                            in1=bcast(head_mask[:].unsqueeze(1).unsqueeze(3), [P, U, HP, C]), op=ALU.mult)

                    def step(n, k):
                        r, kr = n - LAG_REC, slot(k, LAG_REC)
                        if act_on(r):
                            wait(pool, "state_done", r - 1)
                            wait(pool, "o_mm", r - 1)
                            diag(s_diag[:], s2[:, kr % 2, 0:U]).then_inc(M["sdiag_done"], 1)
                        g, kg = n - LAG_GRAM, slot(k, LAG_GRAM)
                        if act_on(g):
                            wait(pool, "gam_done", g)
                            wait(pool, "q_done", g)
                            wait(pool, "o_mm", g - 4)
                            pool.tensor_tensor(out=gq4[:, kg, 0:U], in0=gam4[:, kg], in1=kq2[:, kg % 2, 0:U, C:2 * C],
                                               op=ALU.mult).then_inc(M["gq_done"], 1)
                        o, ko = n - LAG_OUT, slot(k, LAG_OUT)
                        if act_on(o):
                            wait(pool, "oc_done", o)
                            wait(pool, "gate_done", o)
                            wait(pool, "og_done", o - 1)
                            g8 = gate8[:, o % 8].rearrange("p g t -> p (g t)")
                            pool.tensor_tensor(out=o_r[:, 1, :], in0=o_c[:], in1=g8, op=ALU.mult) \
                                .then_inc(M["og1_done"], 1)
                        r, kr = n - LAG_REC + 1, slot(k, LAG_REC - 1)
                        if act_on(r):
                            pool.wait_ge(M["t_done"], r - kr % 2 + 2)
                            wait(pool, "delta_mm", r - 2)
                            diag(t_diag2[:, kr % 2], t2[:, kr // 2, kr % 2]).then_inc(M["tdiag_done"], 1)
                        if act_on(o):
                            wait(pool, "rms_done", o)
                            wait(pool, "og1_done", o)
                            wait(pool, "y_done", o - 2)
                            pool.tensor_tensor(out=og[:, ko % 2].rearrange("p g t -> p (g t)"), in0=o_r[:, 1, :],
                                               in1=o_r[:, 0, :], op=ALU.mult).then_inc(M["og_done"], 1)
                        if act_on(n):
                            wait(pool, "xn_done", n)
                            wait(pool, "xt_done", n - 1)
                            pool.tensor_tensor(out=h[:], in0=xn[:], in1=mod[:, CA, :], op=ALU.mult) \
                                .then_inc(M["hmul_done"], 1)
                            wait(pool, "hmul_done", n)
                            pool.tensor_tensor(out=h[:], in0=h[:], in1=mod[:, SA, :], op=ALU.add) \
                                .then_inc(M["h_done"], 1)
                        c, kc_ = n - LAG_PROJ, slot(k, LAG_PROJ)
                        if act_on(c):
                            wait(pool, "k_done", c)
                            wait(pool, "ks_done", c - 4)
                            diag(k_diag4[:, kc_], kq2[:, kc_ % 2, 0:U, 0:C]).then_inc(M["kdiag_done"], 1)
                        if act_on(o):
                            wait(pool, "xn2_done", o)
                            wait_ring(pool, HO, o - 2, (ko + 2) % 4)
                            wait(pool, "h2t_mm", o - 2)
                            pool.tensor_tensor(out=h2_2[:, ko % 2, :], in0=xn2[:], in1=mod[:, CB, :], op=ALU.mult) \
                                .then_inc(M["h2mul_done"], 1)
                            wait(pool, "h2mul_done", o)
                            pool.tensor_tensor(out=h2_2[:, ko % 2, :], in0=h2_2[:, ko % 2, :], in1=mod[:, SB_, :], op=ALU.add) \
                                .then_inc(M["h2_done"], 1)

                    pool.wait_ge(K["c_vec"], SETUP_VEC)
                    run(pool, step)

                @block.scalar
                def _(act):
                    count = [0]

                    def link(ins):
                        count[0] += 1
                        ins.then_inc(K["c_act"], 1)
                        act.wait_ge(K["c_act"], count[0])

                    act.preload_act_table_set("natural_log_exp_and_others")
                    act.wait_ge(K["c_pool"], SETUP_POOL)
                    act.wait_ge(K["c_in"], LOADS * 16)
                    link(act.activation(x4[0:B, 0, :], h[0:B, :], ACT.Exp, scale=-1.0, bias=zero[0:B, :]))
                    link(act.activation(neg_rate[:], z32[:, 0:H], ACT.Exp, bias=zero[:]))
                    act.wait_ge(K["c_pe"], 3)
                    for m in range(3):
                        link(act.activation(mod[:, 2 * m:2 * m + 2, :].rearrange("p m e -> p (m e)"),
                                            [zbank, qkbank, vgbank][m][:, :], ACT.Copy))

                    def diag(dst, src, done):
                        for g in range(HP):
                            ins = act.activation(dst[:, :, g, :], src, ACT.Copy, scale=head_mask[:, g:g + 1])
                        ins.then_inc(M[done], 1)

                    def pair(a, src, done):
                        for g in range(2):
                            ins = act.activation(kv_pair[:, a, :, g, :], src, ACT.Copy, scale=head_side[:, g:g + 1])
                        ins.then_inc(M[done], 1)

                    def step(n, k):
                        o, ko = n - LAG_OUT, slot(k, LAG_OUT)
                        e = n - LAG_ROUTE
                        if act_on(e):
                            wait(act, "h2t_mm", e)
                            wait(act, "rl_done", e - 1)
                            act.activation(h2T[:].rearrange("p k t -> p (k t)"), tbank[:, 0:E], ACT.Copy) \
                                .then_inc(M["h2T_done"], 1)
                        c, kc_ = n - LAG_PROJ, slot(k, LAG_PROJ)
                        if act_on(c):
                            wait(act, "xt_done", c)
                            wait(act, "proj_done", c - 2)
                            act.activation(hT2[:, kc_ % 2].rearrange("p k t -> p (k t)"), tbank[:, 0:E], ACT.Copy) \
                                .then_inc(M["hT_done"], 1)
                        if act_on(o):
                            wait(act, "o_mm", o)
                            wait(act, "og1_done", o - 1)
                            act.activation(o_c[:], obank[:, 0, :], ACT.Copy, scale=D ** -0.5) \
                                .then_inc(M["oc_done"], 1)
                            wait(act, "oc_done", o)
                            wait(act, "ms_done", o - 1)
                            act.activation(o_sq[:], o_c[:], ACT.Square, bias=zero[:]).then_inc(M["osq_done"], 1)
                        if act_on(n):
                            wait(act, "mean_done", n)
                            wait(act, "xn_done", n - 1)
                            act.activation(rstd[:, 1:2], mv[:, 1:2], ACT.Ln, bias=eps_ln[:]).then_inc(M["ln_rstd"], 1)
                            wait(act, "ln_rstd", n)
                            act.activation(rstd[:, 0:1], rstd[:, 1:2], ACT.Exp, scale=-0.5, bias=zero[:]) \
                                .then_inc(M["rstd_done"], 1)
                        if act_on(o):
                            wait(act, "ms_done", o)
                            wait(act, "og_done", o - 1)
                            act.activation(o_sq[:], obank[:, 1, :], ACT.Ln, scale=1.0 / D, bias=eps_rms[:]) \
                                .then_inc(M["lnms_done"], 1)
                            wait(act, "lnms_done", o)
                            act.activation(o_r[:, 0, :], o_sq[:], ACT.Exp, scale=-0.5, bias=zero[:]) \
                                .then_inc(M["rms_done"], 1)
                        r, kr = n - LAG_REC, slot(k, LAG_REC)
                        if act_on(r):
                            wait(act, "kv_done", r)
                            wait(act, "su_done", r - 1)
                            diag(kt_diag[:], kv4[:, kr, :, 0, :], "ktdiag_done")
                        if act_on(c):
                            wait(act, "proj_done", c)
                            wait(act, "inv_done", c - 1)
                            act.activation(sqk[:].rearrange("p m t -> p (m t)"), qkbank[:, :], ACT.Square,
                                           bias=zero[:]).then_inc(M["sq_done"], 1)
                            wait(act, "kvturn_done", c - 1)
                            pair(1, vgbank[:, 0:E].rearrange("p (u t) -> p u t", t=C), "vpair_done")
                            wait(act, "gate_done", c - 1)
                            act.activation(sig[:, 0, :], vgbank[:, E:2 * E], ACT.Exp, scale=-1.0, bias=zero[:]) \
                                .then_inc(M["gate_e"], 1)
                            wait(act, "gate_e", c)
                            act.activation(sig[:, 1, :], sig[:, 0, :], ACT.Ln, bias=one[:]).then_inc(M["gate_l"], 1)
                            wait(act, "gate_l", c)
                            act.activation(sig[:, 2, :], sig[:, 1, :], ACT.Exp, scale=-1.0, bias=zero[:]) \
                                .then_inc(M["gate_s"], 1)
                            wait(act, "decay_steps", c, DECAY, 3)
                            act.activation(u32[:], w32[:], ACT.Exp, bias=zero[:]).then_inc(M["expz_done"], 1)
                            wait(act, "ss_done", c)
                            act.activation(sqk[:].rearrange("p m t -> p (m t)"), tbank[:, :], ACT.Ln,
                                           bias=zero[:]).then_inc(M["lnss_done"], 1)
                            wait(act, "lnss_done", c)
                            wait(act, "q_done", c - 1)
                            act.activation(inv_norm[:], sqk[:], ACT.Exp, scale=-0.5, bias=zero[:]) \
                                .then_inc(M["inv_done"], 1)
                            wait(act, "decay_steps", c, DECAY, DECAY)
                            wait(act, "ab_done", c - 1)
                            act.activation(decay_rep[:, 0], bcast(ser[:, 5, :].unsqueeze(2), [P, H, C]), ACT.Exp,
                                           bias=zero[:]).then_inc(M["alpha_done"], 1)
                            act.activation(decay_rep[:, 1], bcast(rec[:, H:].unsqueeze(2), [P, H, C]), ACT.Copy) \
                                .then_inc(M["beta_done"], 1)
                        if act_on(o):
                            wait(act, "mean2_done", o)
                            wait(act, "xn2_done", o - 1)
                            act.activation(rstd2[:, 1:2], mv2[:, 1:2], ACT.Ln, bias=eps_ln[:]) \
                                .then_inc(M["ln_rstd2"], 1)
                            wait(act, "ln_rstd2", o)
                            act.activation(rstd2[:, 0:1], rstd2[:, 1:2], ACT.Exp, scale=-0.5, bias=zero[:]) \
                                .then_inc(M["rstd2_done"], 1)
                        if act_on(e):
                            wait(act, "max_done", e)
                            wait(act, "sc_done", e - 1)
                            act.activation(expl[:], logit[:], ACT.Exp, bias=nmax[:], accum_out=esum[:, 0:1]) \
                                .then_inc(M["expl_done"], 1)
                        if act_on(c):
                            wait(act, "k_done", c)
                            pair(0, kq2[:, kc_ % 2, 0:U, 0:C], "kpair_done")
                            wait(act, "ab_done", c)
                            wait(act, "gam_done", c - 1)
                            ab = tbank[:, 0:2 * E].rearrange("p (a u i) -> p a u i", a=2, i=C)
                            act.activation(alpha0[:, :, 1:C], ab[:, 0, :, 1:C], ACT.Copy) \
                                .then_inc(M["alpha0_done"], 1)
                            act.activation(start0[:, :, 0:1], ab[:, 0, :, 0:1], ACT.Copy) \
                                .then_inc(M["start0_done"], 1)
                            act.activation(beta4[:, kc_], ab[:, 1], ACT.Copy).then_inc(M["beta_copied"], 1)
                    run(act, step)

                @block.vector
                def _(v):
                    count = [0]

                    def link(ins):
                        count[0] += 1
                        ins.then_inc(K["c_vec"], 1)
                        v.wait_ge(K["c_vec"], count[0])

                    v.wait_ge(K["c_pool"], SETUP_POOL)
                    v.wait_ge(K["c_in"], LOADS * 16)
                    link(v.tensor_reduce(ident_rep[:, 0, :], ident[:].rearrange("p (h r) -> p r h", r=D), AX.X, ALU.add))
                    link(v.tensor_copy(ident_rep[:, 1:, :], bcast(ident_rep[:, 0:1, :], [P, U - 1, C])))
                    link(v.tensor_reduce(head_side[:], head_mask[:].rearrange("p (a b) -> p b a", b=2), AX.X, ALU.add))
                    link(v.memset(solved[:], 0.0))
                    for i in range(C):
                        link(v.memset(solved[:, i, :, i:i + 1], 1.0))
                    for g in range(HG):
                        link(v.tensor_scalar(w_out[:, g, :], w_out[:, g, :], rms_col[:, 0:1], None, ALU.mult))
                    v.wait_ge(K["c_act"], 1)
                    link(v.tensor_scalar(x4[0:B, 1, :], x4[0:B, 0, :], 1.0, None, ALU.add))
                    link(v.reciprocal(x4[0:B, 2, :], x4[0:B, 1, :]))
                    link(v.tensor_tensor(out=x4[0:B, 3, :], in0=x4[0:B, 2, :], in1=h[0:B, :], op=ALU.mult))
                    v.wait_ge(K["c_pe"], 1)
                    for kc in range(KC):
                        link(v.tensor_copy(cT[:, kc, :].rearrange("p (b i) -> p b i", i=C),
                                           bcast(tbank[:, kc * P:kc * P + B].unsqueeze(2), [P, B, C])))
                        link(v.tensor_copy(router_t[:, kc, :], tbank[:, (2 + kc) * P:(2 + kc) * P + NE]))
                    v.wait_ge(K["c_act"], SETUP_ACT)
                    link(v.tensor_scalar(neg_rate[:], neg_rate[:], -1.0, None, ALU.mult))
                    for m in (CA, CB):
                        link(v.tensor_scalar(mod[:, m, :], mod[:, m, :], 1.0, None, ALU.add))
                    for m in (GA, GB):
                        link(v.tensor_scalar(xr2[:, 0, :], mod[:, m, :], 0.0, 2.0, ALU.is_ge, ALU.mult))
                        link(v.scalar_tensor_tensor(out=xr2[:, 1, :], in0=mod[:, m, :], scalar=-1.0,
                                                    in1=mod[:, m, :], op0=ALU.mult, op1=ALU.max))
                        link(v.tensor_scalar(xr2[:, 1, :], xr2[:, 1, :], 0.25, None, ALU.max))
                        link(v.scalar_tensor_tensor(out=mod[:, m, :], in0=xr2[:, 0, :], scalar=-1.0,
                                                    in1=xr2[:, 1, :], op0=ALU.add, op1=ALU.mult))
                    v.wait_ge(K["c_pe"], 4)
                    link(v.tensor_copy(gb_col[:], tbank[:, 0:2 * P].rearrange("p (k b i) -> p k b i", k=KC, i=C)[:, :, :, 0]))
                    assert count[0] == SETUP_VEC, count[0]

                    def solve_row(even, i):
                        base = LANES // 2 * even
                        a = low[:, 0, :].rearrange("p (i h l) -> p i h l", h=2, l=C)[:, i, :, 0:i]
                        t = solved[:, 0:i, :, 0:i].rearrange("p l h j -> p h j l")
                        pr = prod[:, 0:2 * i * i].rearrange("p (h j l) -> p h j l", h=2, l=i)
                        v.wait_ge(M["lanes_steps"], base + 3 + 2 * (i - 1))
                        v.tensor_tensor(out=pr, in0=bcast(a.unsqueeze(2), [P, 2, i, i]), in1=t, op=ALU.mult) \
                            .then_inc(M["lanes_steps"], 1)
                        v.wait_ge(M["lanes_steps"], base + 4 + 2 * (i - 1))
                        v.tensor_reduce(solved[:, i, :, 0:i], pr, AX.X, ALU.add, negate=True) \
                            .then_inc(M["lanes_steps"], 1)

                    def lanes_in(even, s):
                        lane = low[:].rearrange("p a (i c) -> p a i c", c=32)
                        v.transpose(lane[:, 0].rearrange("p i (c u) -> p i c u", c=2),
                                    ap4[:, s:s + 2, 0:U, 0, :].rearrange("p c u i -> p i c u")) \
                            .then_inc(M["lanes_steps"], 1)
                        v.transpose(lane[:, 1], beta4[:, s:s + 2].rearrange("p c u i -> p i (c u)")) \
                            .then_inc(M["lanes_steps"], 1)
                        v.wait_ge(M["lanes_steps"], LANES // 2 * even + 2)
                        v.tensor_tensor(out=low[:, 0, :], in0=low[:, 0, :], in1=low[:, 1, :], op=ALU.mult) \
                            .then_inc(M["lanes_steps"], 1)

                    def lanes_out(even, s):
                        v.wait_ge(M["lanes_steps"], LANES // 2 * even + 3 + 2 * (C - 1))
                        beta = low[:, 1, :].rearrange("p (j h r) -> p j h r", h=2, r=C)[:, :, :, 0] \
                            .rearrange("p j h -> p h j")
                        v.tensor_tensor(out=solved_b[:], in0=solved[:],
                                        in1=bcast(beta.unsqueeze(1), [P, C, 2, C]), op=ALU.mult) \
                            .then_inc(M["lanes_steps"], 1)
                        v.wait_ge(M["lanes_steps"], LANES // 2 * even + 4 + 2 * (C - 1))
                        wait(v, "tdiag_done", even + 1 - 4)
                        v.transpose(t2[:, s].rearrange("p c u i -> p i (c u)"),
                                    solved_b[:].rearrange("p i h j -> p i (h j)")).then_inc(M["t_done"], 2)

                    def step(n, k):
                        r, kr = n - LAG_REC, slot(k, LAG_REC)
                        o, ko = n - LAG_OUT, slot(k, LAG_OUT)
                        g, kg = n - LAG_GRAM, slot(k, LAG_GRAM)
                        c, kc_ = n - LAG_PROJ, slot(k, LAG_PROJ)
                        e = n - LAG_ROUTE
                        w, kw = n - LAG_SCORE, slot(k, LAG_SCORE)
                        first = k % 2 == 1
                        lag = LAG_GRAM + 1 if first else LAG_GRAM + 2
                        even, ps = n - lag, slot(k, lag)
                        solving = act_on(even)

                        if act_on(r):
                            wait(v, "ks_done", r)
                            wait(v, "delta_mm", r - 1)
                            v.tensor_tensor(out=rhs[:, 1, 0:U], in0=chain[:, 0, 0:U],
                                            in1=bcast(gcol4[:, kr].unsqueeze(2), [P, U, C]), op=ALU.mult) \
                                .then_inc(M["gks_done"], 1)
                            wait(v, "gks_done", r)
                            v.tensor_tensor(out=rhs[:, 0, 0:U], in0=kv4[:, kr, :, 1, :], in1=rhs[:, 1, 0:U], op=ALU.subtract) \
                                .then_inc(M["rhs_done"], 1)
                        if act_on(w):
                            wait(v, "st_done", w)
                            wait_ring(v, SO, w - 4, kw)
                            v.tensor_copy(scT4[:, kw, :], zbank[0:NE, 384:512]).then_inc(M["scT_done"], 1)
                        if act_on(n):
                            wait_ring(v, XS, n, k)
                            wait(v, "mean_done", n - 1)
                            v.bn_stats(stats[:], x4[:, k, :]).then_inc(M["stats_done"], 1)
                            wait(v, "rstd_done", n - 1)
                            wait(v, "xn_done", n - 1)
                            wait(v, "stats_done", n)
                        if act_on(r):
                            v.tensor_tensor(out=sg[:], in0=s2[:, kr % 2, 0:U],
                                            in1=bcast(gam4[:, kr, :, C - 1:C], [P, U, C]), op=ALU.mult) \
                                .then_inc(M["sg_done"], 1)
                        if act_on(n):
                            v.bn_aggr(mv[:], stats[:]).then_inc(M["mean_done"], 1)
                        if solving and not first:
                            for i in range(9, C - 3):
                                solve_row(even, i)
                        if act_on(g):
                            wait(v, "gram_done", g)
                            wait(v, "dec_done", g)
                            wait(v, "o_mm", g - 4)
                            v.tensor_tensor(out=ap4[:, kg, 0:U], in0=gram[:].rearrange("p u (a i) -> p u a i", a=2),
                                            in1=bcast(dec4[:, kg].unsqueeze(2), [P, U, 2, C]), op=ALU.mult) \
                                .then_inc(M["ap_done"], 1)
                            wait(v, "kpair_done", g)
                            wait(v, "vpair_done", g)
                            wait(v, "kv_done", g - 1)
                            v.transpose(kv_turn[:].rearrange("p a u s c -> p (a u s c)"),
                                        kv_pair[:].rearrange("p a u s c -> p (a u s c)")).then_inc(M["kvturn_done"], 1)
                            wait(v, "kvturn_done", g)
                            turned = kv_turn[:].rearrange("p a u s c -> p u a s c")
                            v.tensor_tensor(out=kv4[:, kg], in0=turned[:, :, :, 0, :], in1=turned[:, :, :, 1, :],
                                            op=ALU.add).then_inc(M["kv_done"], 1)
                        if act_on(r):
                            wait(v, "delta_mm", r)
                            wait(v, "su_done", r - 1)
                            wait(v, "ddiag_done", r - 1)
                            v.tensor_copy(delta[:, 0, 0:U], chain[:, 1, 0:U]).then_inc(M["delta_done"], 1)
                            wait(v, "delta_done", r)
                            v.tensor_tensor(out=delta[:, 1, 0:U], in0=delta[:, 0, 0:U],
                                            in1=bcast(dec4[:, kr, :, C - 1:C], [P, U, C]), op=ALU.mult) \
                                .then_inc(M["ddelta_done"], 1)
                        if solving and not first:
                            for i in range(C - 3, C):
                                solve_row(even, i)
                            lanes_out(even, ps // 2)
                        if solving and first:
                            wait(v, "ap_done", even + 1)
                            wait(v, "beta_copied", even + 1)
                            wait(v, "t_done", even - 1)
                            lanes_in(even, ps)
                        if act_on(n):
                            wait(v, "rstd_done", n)
                            wait(v, "h_done", n - 1)
                            v.tensor_scalar(xn[:], x4[:, k, :], mv[:, 0:1], rstd[:, 0:1], ALU.subtract, ALU.mult) \
                                .then_inc(M["xn_done"], 1)
                        base = c * DECAY if act_on(c) else None
                        if act_on(c):
                            wait(v, "z_done", c)
                            wait(v, "expz_done", c - 1)
                            v.tensor_tensor(out=z32[:], in0=zbank[:, 0:2 * H], in1=dtb[:], op=ALU.add) \
                                .then_inc(M["decay_steps"], 1)
                            v.wait_ge(M["decay_steps"], base + 1)
                            v.scalar_tensor_tensor(out=w32[:, 0:H], in0=z32[:, 0:H], scalar=-1.0, in1=z32[:, 0:H],
                                                   op0=ALU.mult, op1=ALU.min) \
                                .then_inc(M["decay_steps"], 1)
                            v.tensor_scalar(w32[:, H:], z32[:, H:], -1.0, None, ALU.mult) \
                                .then_inc(M["decay_steps"], 1)
                        if act_on(r):
                            wait(v, "o_mm", r - 1)
                            v.tensor_tensor(out=d_diag[:], in0=bcast(delta[:, 0, 0:U].unsqueeze(2), [P, U, HP, C]),
                                            in1=bcast(head_mask[:].unsqueeze(1).unsqueeze(3), [P, U, HP, C]),
                                            op=ALU.mult).then_inc(M["ddiag_done"], 1)
                            wait(v, "su_done", r)
                            wait(v, "sg_done", r)
                            wait(v, "sdiag_done", r - 1)
                            v.tensor_tensor(out=s2[:, (kr + 1) % 2, 0:U], in0=sg[:], in1=chain[:, 0, 0:U], op=ALU.add) \
                                .then_inc(M["state_done"], 1)
                        if solving and first:
                            for i in range(1, 5):
                                solve_row(even, i)
                        if act_on(o):
                            wait(v, "y_done", o)
                            wait(v, "h2mul_done", o - 1)
                            v.tensor_tensor(out=xn2[:], in0=zbank[:, 128:128 + E], in1=mod[:, GA, :], op=ALU.mult) \
                                .then_inc(M["yga_done"], 1)
                            wait(v, "yga_done", o)
                            wait_ring(v, XR, o, ko)
                            wait_ring(v, XO, o - 2, (ko + 2) % 4)
                            v.tensor_tensor(out=x2_2[:, ko % 2, :], in0=xn2[:], in1=xr2[:, ko % 2, :], op=ALU.add) \
                                .then_inc(M["x2_done"], 1)
                            wait(v, "x2_done", o)
                            v.bn_stats(stats2[:], x2_2[:, ko % 2, :]).then_inc(M["stats2_done"], 1)
                            wait(v, "stats2_done", o)
                            wait(v, "xn2_done", o - 1)
                            v.tensor_copy(tick[:], zero[:])
                            v.bn_aggr(mv2[:], stats2[:]).then_inc(M["mean2_done"], 1)
                        if act_on(c):
                            wait(v, "gate_s", c)
                            wait(v, "og1_done", c - 8)
                            v.tensor_tensor(out=gate8[:, c % 8].rearrange("p g t -> p (g t)"), in0=vgbank[:, E:],
                                            in1=sig[:, 2, :], op=ALU.mult).then_inc(M["gate_done"], 1)
                            wait(v, "inv_done", c)
                            wait(v, "gram_done", c - 2)
                            wait(v, "kdiag_done", c - 2)
                            wait(v, "gq_done", c - 2)
                            for m, name in ((1, "k_done"), (0, "q_done")):
                                v.scalar_tensor_tensor(
                                    out=kq2[:, kc_ % 2, 0:U, (1 - m) * C:(2 - m) * C],
                                    in0=inv_norm[:, 2 * m:2 * m + 2, :].rearrange("p g (b i) -> p (g b) i", i=C),
                                    scalar=1e12,
                                    in1=qkbank[:, m * E:(m + 1) * E].rearrange("p (u i) -> p u i", i=C),
                                    op0=ALU.min, op1=ALU.mult).then_inc(M[name], 1)
                        if solving and first:
                            for i in range(5, 7):
                                solve_row(even, i)
                        if act_on(c):
                            wait(v, "expz_done", c)
                            j = [3]

                            def decay(ins):
                                j[0] += 1
                                ins.then_inc(M["decay_steps"], 1)
                                v.wait_ge(M["decay_steps"], base + j[0])
                            wait(v, "beta_done", c - 1)
                            decay(v.tensor_scalar(den[:, 0:H], u32[:, 0:H], 2.0, None, ALU.add))
                            decay(v.tensor_scalar(den[:, H:], u32[:, H:], 1.0, None, ALU.add))
                            decay(v.reciprocal(rec[:], den[:]))
                            decay(v.tensor_tensor(out=ser[:, 0, :], in0=u32[:, 0:H], in1=rec[:, 0:H], op=ALU.mult))
                            decay(v.tensor_tensor(out=ser[:, 1, :], in0=ser[:, 0, :], in1=ser[:, 0, :], op=ALU.mult))
                            decay(v.tensor_scalar(ser[:, 2, :], ser[:, 1, :], LOG1P[0], None, ALU.mult))
                            for m, coef in enumerate(LOG1P[1:]):
                                decay(v.scalar_tensor_tensor(out=ser[:, 3 - m % 2, :], in0=ser[:, 2 + m % 2, :],
                                                             scalar=coef, in1=ser[:, 1, :], op0=ALU.add, op1=ALU.mult))
                            decay(v.scalar_tensor_tensor(out=ser[:, 4, :], in0=ser[:, 3, :], scalar=1.0,
                                                         in1=ser[:, 0, :], op0=ALU.add, op1=ALU.mult))
                            decay(v.tensor_scalar(ser[:, 2, :], z32[:, 0:H], 0.0, None, ALU.max))
                            decay(v.scalar_tensor_tensor(out=ser[:, 3, :], in0=ser[:, 4, :], scalar=2.0,
                                                         in1=ser[:, 2, :], op0=ALU.mult, op1=ALU.add))
                            decay(v.tensor_tensor(out=ser[:, 5, :], in0=ser[:, 3, :], in1=neg_rate[:], op=ALU.mult))
                            assert j[0] == DECAY, j
                        if act_on(o):
                            wait(v, "rstd2_done", o)
                            wait(v, "h2mul_done", o - 1)
                            v.tensor_scalar(xn2[:], x2_2[:, ko % 2, :], mv2[:, 0:1], rstd2[:, 0:1], ALU.subtract, ALU.mult) \
                                .then_inc(M["xn2_done"], 1)
                        if act_on(e):
                            wait(v, "rl_done", e)
                            wait(v, "expl_done", e - 1)
                            v.tensor_copy(logit[:], zbank[:, 32:32 + NE]).then_inc(M["logit_done"], 1)
                            wait(v, "logit_done", e)
                            v.tensor_reduce(nmax[:], logit[:], AX.X, ALU.max, negate=True).then_inc(M["max_done"], 1)
                        if solving and first:
                            for i in range(7, 9):
                                solve_row(even, i)
                        if act_on(e):
                            wait(v, "expl_done", e)
                            v.reciprocal(esum[:, 1:2], esum[:, 0:1]).then_inc(M["esum_done"], 1)
                            wait(v, "esum_done", e)
                            wait(v, "st_done", e - 1)
                            v.tensor_scalar(sc[:], expl[:], esum[:, 1:2], None, ALU.mult).then_inc(M["sc_done"], 1)
                        if act_on(c):
                            wait(v, "beta_copied", c)
                            for name in ("ap_done", "ddelta_done", "sg_done", "gks_done", "gq_done"):
                                wait(v, name, c - 4)
                            v.tensor_tensor_scan(dec4[:, kc_].rearrange("p u i -> p (u i)"),
                                                 alpha0[:].rearrange("p u i -> p (u i)"),
                                                 ident_rep[:].rearrange("p u i -> p (u i)"), 0.0, ALU.mult, ALU.add) \
                                .then_inc(M["dec_done"], 1)
                            v.tensor_tensor_scan(gam4[:, kc_].rearrange("p u i -> p (u i)"),
                                                 alpha0[:].rearrange("p u i -> p (u i)"),
                                                 start0[:].rearrange("p u i -> p (u i)"), 0.0, ALU.mult, ALU.add) \
                                .then_inc(M["gam_done"], 1)
                            wait(v, "gam_done", c)
                            wait(v, "gcol_done", c - 1)
                            v.tensor_tensor(out=gtmp[:], in0=gam4[:, kc_], in1=ident_rep[:], op=ALU.mult) \
                                .then_inc(M["gtmp_done"], 1)
                            wait(v, "gtmp_done", c)
                            v.tensor_reduce(gcol4[:, kc_], gtmp[:], AX.X, ALU.add).then_inc(M["gcol_done"], 1)
                    run(v, step)

                @block.tensor
                def _(pe):
                    pe.wait_ge(K["c_pool"], SETUP_POOL)
                    pe.wait_ge(K["c_in"], LOADS * 16)
                    pe.wait_ge(K["c_vec"], SILU_VEC)
                    for kc in range(KC):
                        pe.transpose(tbank[:, kc * P:kc * P + B], x4[0:B, 3, kc * P:(kc + 1) * P], ident[0:B, 0:B])
                    for kc in range(KC):
                        ins = pe.transpose(tbank[:, (2 + kc) * P:(2 + kc) * P + NE], xn[0:NE, kc * P:(kc + 1) * P],
                                           ident[0:NE, 0:NE])
                    ins.then_inc(K["c_pe"], 1)
                    pe.wait_ge(K["c_vec"], COND_VEC)
                    for m in range(3):
                        for kc in range(KC):
                            ins = pe.matmul([zbank, qkbank, vgbank][m][:, :], cT[:, kc, :],
                                            wm[:, kc, m * 512:(m + 1) * 512], start=(kc == 0), stop=(kc == KC - 1))
                    ins.then_inc(K["c_pe"], 2)
                    pe.wait_ge(K["c_vec"], SETUP_VEC - 1)
                    for kc in range(KC):
                        ins = pe.transpose(tbank[:, kc * P:(kc + 1) * P], mod[:, GB, kc * P:(kc + 1) * P], ident[:])
                    ins.then_inc(K["c_pe"], 1)
                    pe.wait_ge(K["c_vec"], SETUP_VEC)

                    o_units = obank[:].rearrange("p a (u c) -> p (a u) c", c=C)

                    def window(ap, u, end=None):
                        per = ap.shape[-1]
                        stop = u + WIDE // per
                        return ap[:, u:stop if end is None else min(stop, end)]

                    def step(n, k):
                        r, kr = n - LAG_REC, slot(k, LAG_REC)
                        o, ko = n - LAG_OUT, slot(k, LAG_OUT)
                        g, kg = n - LAG_GRAM, slot(k, LAG_GRAM)
                        c, kc_ = n - LAG_PROJ, slot(k, LAG_PROJ)
                        e = n - LAG_ROUTE
                        w = n - LAG_SCORE
                        if act_on(r):
                            wait(pe, "state_done", r - 1)
                            for u in range(U):
                                ins = pe.matmul(window(chain[:, 0], u), k_diag4[:, kr, u].rearrange("p g i -> p (g i)"),
                                                window(s2[:, kr % 2], u), start=True, stop=True)
                            ins.then_inc(M["ks_done"], 1)
                        if act_on(w):
                            wait(pe, "sc_done", w)
                            wait(pe, "logit_done", w)
                            pe.transpose(zbank[0:NE, 384:512], sc[:], ident[:]).then_inc(M["st_done"], 1)
                        if act_on(c):
                            wait(pe, "h_done", c)
                            wait(pe, "h2T_done", n - LAG_ROUTE if act_on(e) else -1)
                            wait(pe, "beta_copied", c - 1)
                            for kc in range(KC):
                                ins = pe.transpose(tbank[:, kc * P:(kc + 1) * P], h[:, kc * P:(kc + 1) * P], ident[:])
                            ins.then_inc(M["xt_done"], 1)
                        if act_on(o):
                            wait(pe, "osq_done", o)
                            pe.matmul(obank[:, 1, :], head_ones[:], o_sq[:], start=True, stop=True) \
                                .then_inc(M["ms_done"], 1)
                        if act_on(g):
                            wait(pe, "kdiag_done", g)
                            wait(pe, "q_done", g)
                            wait(pe, "ap_done", g - 1)
                            for u in range(U):
                                ins = pe.matmul(window(gram, u, U), k_diag4[:, kg, u].rearrange("p g i -> p (g i)"),
                                                window(kq2[:, kg % 2], u, U), start=True, stop=True)
                            ins.then_inc(M["gram_done"], 1)
                        if act_on(r):
                            wait(pe, "rhs_done", r)
                            wait(pe, "tdiag_done", r)
                            for u in range(U):
                                ins = pe.matmul(window(chain[:, 1], u), t_diag2[:, kr % 2, u].rearrange("p g i -> p (g i)"),
                                                window(rhs[:, 0], u), start=True, stop=True)
                            ins.then_inc(M["delta_mm"], 1)
                        if act_on(c):
                            wait(pe, "hT_done", c)
                            wait(pe, "q_done", c - 1)
                            wait(pe, "gate_done", c - 1)
                            for m, name in enumerate("qkvg"):
                                bank = qkbank if m < 2 else vgbank
                                for hg in range(HG):
                                    for kc in range(KC):
                                        col = (m % 2) * E + hg * P
                                        ins = pe.matmul(bank[:, col:col + P], w_in[name][:, kc, hg * P:(hg + 1) * P],
                                                        hT2[:, kc_ % 2, kc, :], start=(kc == 0), stop=(kc == KC - 1))
                            ins.then_inc(M["proj_done"], 1)
                            wait(pe, "scT_done", w if act_on(w) else -1)
                            for kc in range(KC):
                                ins = pe.matmul(zbank[:, 0:2 * H], hT2[:, kc_ % 2, kc, :], w_ab[:, kc, :],
                                                start=(kc == 0), stop=(kc == KC - 1))
                            ins.then_inc(M["z_done"], 1)
                        if act_on(r):
                            wait(pe, "ddelta_done", r)
                            wait(pe, "ktdiag_done", r)
                            for u in range(U):
                                ins = pe.matmul(window(chain[:, 0], u), kt_diag[:, u].rearrange("p g i -> p (g i)"),
                                                window(delta[:, 1], u), start=True, stop=True)
                            ins.then_inc(M["su_done"], 1)
                        if act_on(o):
                            wait(pe, "og_done", o)
                            if act_on(c):
                                wait(pe, "decay_steps", c, DECAY, 1)
                            if act_on(w):
                                wait(pe, "scT_done", w)
                            for hg in range(HG):
                                ins = pe.matmul(zbank[:, 128:128 + E], og[:, ko % 2, hg, :], w_out[:, hg, :],
                                                start=(hg == 0), stop=(hg == HG - 1))
                            ins.then_inc(M["y_done"], 1)
                        if act_on(c):
                            wait(pe, "sq_done", c)
                            pe.matmul(tbank[:, :], head_ones[:], sqk[:].rearrange("p m t -> p (m t)"),
                                      start=True, stop=True).then_inc(M["ss_done"], 1)
                        if act_on(r):
                            wait(pe, "sdiag_done", r)
                            wait(pe, "ddiag_done", r)
                            wait(pe, "gq_done", r)
                            if act_on(o):
                                wait(pe, "lnms_done", o)
                            for u in range(U):
                                pe.matmul(window(o_units, u), s_diag[:, u].rearrange("p g i -> p (g i)"),
                                          window(gq4[:, kr], u), start=True, stop=False)
                                ins = pe.matmul(window(o_units, u), d_diag[:, u].rearrange("p g i -> p (g i)"),
                                                window(ap4[:, kr, :, 1, :], u), start=False, stop=True)
                            ins.then_inc(M["o_mm"], 1)
                        if act_on(e):
                            wait(pe, "h2T_done", e)
                            if act_on(o):
                                wait(pe, "yga_done", o)
                            elif act_on(w):
                                wait(pe, "scT_done", w)
                            for kc in range(KC):
                                ins = pe.matmul(zbank[:, 32:32 + NE], h2T[:, kc, :], router_t[:, kc, :],
                                                start=(kc == 0), stop=(kc == KC - 1))
                            ins.then_inc(M["rl_done"], 1)
                        if act_on(c):
                            wait(pe, "alpha_done", c)
                            wait(pe, "beta_done", c)
                            wait(pe, "lnss_done", c)
                            for a in range(2):
                                for hg in range(HG):
                                    src = decay_rep[:, a, hg * HP:(hg + 1) * HP, :].rearrange("p h r -> p (h r)")
                                    ins = pe.transpose(tbank[:, (2 * a + hg) * P:(2 * a + hg + 1) * P], src, ident[:])
                            ins.then_inc(M["ab_done"], 1)
                        if act_on(o):
                            wait(pe, "h2_done", o)
                            if act_on(c):
                                wait(pe, "beta_copied", c)
                            for kc in range(KC):
                                ins = pe.transpose(tbank[:, kc * P:(kc + 1) * P], h2_2[:, ko % 2, kc * P:(kc + 1) * P],
                                                   ident[:])
                            ins.then_inc(M["h2t_mm"], 1)
                    run(pe, step)


        PAIRS = NE * B
        NT = 3
        TR = -(-CAP // NT)
        width = [min(TR, CAP - t * TR) for t in range(NT)]

        experts = ctx.enter_context(ExitStack())

        def eb(name, shape, dt=F32):
            return experts.enter_context(nc.sbuf_tensor(name, shape, dt))

        score = eb("score", [PAIRS, T])
        best = eb("best", [PAIRS, ROUNDS * 8])
        place = eb("place", [PAIRS, ROUNDS * 8])
        best8 = eb("best8", [PAIRS, 8])
        place8 = eb("place8", [PAIRS, 8], U32)
        batch_hot = eb("batch_hot", [PAIRS, B])
        batch_row = eb("batch_row", [P, B])
        batch_int = eb("batch_int", [P, B], U32)
        batch_base = eb("batch_base", [PAIRS, 1])
        gate_col = eb("gate_col", [TR, NT, PAIRS])
        row_col = eb("row_col", [TR, NT, PAIRS + 2], U32)
        b1_rows = eb("b1_rows", [NE * HID // P, P])
        b2_rows = eb("b2_rows", [NE * KC, P])
        b1_col = eb("b1_col", [P, NE * HID // P])
        b2_col = eb("b2_col", [P, NE * KC])
        w1_2 = eb("w1_2", [P, 2, KC, HID])
        w2_2 = eb("w2_2", [P, 2, HID // P, E])
        b1_now = eb("b1_now", [P, 2, HID // P])
        carry = eb("carry", [P, 128])
        from_row = eb("from_row", [TR, 2, NT], U32)
        to_row = eb("to_row", [TR, 2, NT], U32)
        tok2 = eb("tok2", [TR, 2, NT, E])
        tokT2 = eb("tokT2", [P, 2, KC, CAP])
        act2 = eb("act2", [P, 2, HID // P, CAP])
        yT2 = eb("yT2", [P, 2, KC, CAP])
        ys2 = eb("ys2", [TR, 2, NT, E])

        N = sems("scores_in biases_in round_max round_place round_next round_kept best_ready place_ready hot_steps "
                 "lists_turned lists_ready rows_zeroed biases_turned biases_ready b1_picked from_picked to_picked tokT_mm "
                 "tokT_ready up_mm gelu_done down_mm yT_ready back_mm ys_ready")
        W1 = [sem(f"w1_loaded{i}") for i in range(2)]
        W2 = [sem(f"w2_loaded{i}") for i in range(2)]
        GATHERED = [sem(f"gathered{i}") for i in range(2)]
        ADDED = [sem(f"added{i}") for i in range(2)]
        HC = HID // P

        with nc.Block() as block:
            place_of = [-1]

            def settle(eng):
                place_of[0] += 1
                col = slice(place_of[0], place_of[0] + 1)
                if eng is nc.gpsimd:
                    eng.tensor_tensor(out=carry[:, col], in0=zero[:], in1=zero[:], op=ALU.add)
                elif eng is nc.scalar:
                    eng.activation(carry[:, col], zero[:], ACT.Copy)
                else:
                    eng.tensor_copy(carry[:, col], zero[:])

            def wait_added(eng, q, j):
                if isinstance(q, int) and q < 2:
                    return
                eng.wait_ge(ADDED[j], (q - j) * (8 * NT))

            def back(t):
                return [vgbank[0:width[0], 0:E], vgbank[0:width[1], E:2 * E], tbank[0:width[2], 0:E]][t]

            def chain_bank(kc):
                return [chain[:, 0].rearrange("p u c -> p (u c)"), obank[:].rearrange("p a c -> p (a c)")][kc][:, 0:CAP]

            def side_bank(j):
                return [gram[:], chain[:, 1]][j].rearrange("p u c -> p (u c)")

            def up_bank(m):
                return side_bank(m % 2)[:, 0:CAP]

            def each_unit(eng, unit):
                unit(0, 0, 0, 0, 0, finish=False)
                unit(1, 1, 0, 0, 1)
                with eng.Fori(1, B // 2) as b2_:
                    for j in range(2):
                        unit(b2_ * 2 + j, b2_ * 2 + j, 0, 0, j)
                with eng.Fori(0, B // 2) as b2_:
                    for j in range(2):
                        unit(b2_ * 2 + (B + j), b2_ * 2 + j, 1, 1, j)
                with eng.Fori(1, NE // 2) as e2:
                    for par in range(2):
                        with eng.Fori(0, B // 2) as b2_:
                            for j in range(2):
                                unit(e2 * (2 * B) + b2_ * 2 + (par * B + j), b2_ * 2 + j, e2 * 2 + par, par, j)

            def load_weights(sp, e, par):
                sp.dma_start(w1_2[:, par], w1[e].rearrange("(k p) n -> p k n", p=P)).then_inc(W1[par], 16)
                sp.dma_start(w2_2[:, par], w2[e].rearrange("(j p) n -> p j n", p=P)).then_inc(W2[par], 16)

            @block.sync
            def _(sp):
                sp.dma_start(score[:], score_dram.rearrange("e b t -> (e b) t")).then_inc(N["scores_in"], 16)
                sp.dma_start(b1_rows[:], b1.rearrange("e (j p) -> (e j) p", p=P)).then_inc(N["biases_in"], 16)
                sp.dma_start(b2_rows[:], b2.rearrange("e (k p) -> (e k) p", p=P)).then_inc(N["biases_in"], 16)
                for par in range(2):
                    load_weights(sp, par, par)
                with sp.Fori(1, NE // 2) as e2:
                    for par in range(2):
                        sp.wait_ge(N["down_mm"], (e2 * 2 + par - 1) * B)
                        load_weights(sp, e2 * 2 + par, par)

            @block.vector
            def _(v):
                steps = [0]

                def link(ins):
                    steps[0] += 1
                    ins.then_inc(N["hot_steps"], 1)
                    v.wait_ge(N["hot_steps"], steps[0])

                link(v.memset(row_col[:], 0))
                link(v.tensor_reduce(batch_hot[:], ident[0:PAIRS, 0:PAIRS].rearrange("p (e b) -> p b e", b=B),
                                     AX.X, ALU.add))
                v.wait_ge(N["rows_zeroed"], 1)
                link(v.tensor_copy(batch_row[:], batch_int[:]))
                link(v.tensor_tensor(out=batch_hot[:], in0=batch_hot[:], in1=batch_row[0:PAIRS, :], op=ALU.mult))
                link(v.tensor_reduce(batch_base[:], batch_hot[:], AX.X, ALU.add))
                v.wait_ge(N["scores_in"], 16)
                def best_eight(r):
                    if not isinstance(r, int):
                        v.wait_ge(N["round_next"], r)
                        v.wait_ge(N["round_kept"], r * 2)
                        settle(v)
                    v.max(best8[:], score[:]).then_inc(N["round_max"], 1)
                    v.wait_ge(N["round_max"], r + 1)
                    v.tensor_scalar(best[:, bass.ds(r * 8, 8)], best8[:], 1.0, None, ALU.mult) \
                        .then_inc(N["round_kept"], 1)
                    v.max_index(place8[:], best8[:], score[:]).then_inc(N["round_place"], 1)
                    v.wait_ge(N["round_place"], r + 1)
                    v.tensor_scalar(place[:, bass.ds(r * 8, 8)], place8[:], batch_base[:, 0:1], None, ALU.add) \
                        .then_inc(N["round_kept"], 1)
                    v.match_replace(score[:], best8[:], score[:], -1.0).then_inc(N["round_next"], 1)

                best_eight(0)
                with v.Fori(1, ROUNDS) as r:
                    best_eight(r)
                v.wait_ge(N["lists_turned"], 1)
                for src, dst in ((0, gate_col), (1, row_col)):
                    for t in range(NT):
                        w = width[t]
                        v.tensor_copy(dst[0:w, t, 0:PAIRS], side_bank(src)[0:w, t * PAIRS:(t + 1) * PAIRS]) \
                            .then_inc(N["lists_ready"], 1)
                v.wait_ge(N["biases_turned"], 1)
                v.tensor_copy(b1_col[:], chain[:, 0].rearrange("p u c -> p (u c)")[:, 0:NE * HC]) \
                    .then_inc(N["biases_ready"], 1)
                v.tensor_copy(b2_col[:], chain[:, 0].rearrange("p u c -> p (u c)")[:, P:P + NE * KC]) \
                    .then_inc(N["biases_ready"], 1)

                def unit(q, b, e, par, j, turn_next=True, finish=True, start=True):
                    if turn_next:
                        v.wait_ge(N["tokT_mm"], q + 2)
                        for kc in range(KC):
                            v.tensor_copy(tokT2[:, (j + 1) % 2, kc, :], [zbank, qkbank][kc][:, 0:CAP]) \
                                .then_inc(N["tokT_ready"], 1)
                    if finish:
                        v.wait_ge(N["back_mm"], q)
                        wait_added(v, q - 1, (j + 1) % 2)
                        for t in range(NT):
                            col = gate_col[0:width[t], t, bass.ds(q - 1, 1)]
                            v.tensor_scalar(ys2[0:width[t], (j + 1) % 2, t, :], back(t), col, None, ALU.mult) \
                                .then_inc(N["ys_ready"], 1)
                    if start:
                        v.wait_ge(N["down_mm"], q + 1)
                        for kc in range(KC):
                            v.tensor_scalar(yT2[:, j, kc, :], chain_bank(kc), b2_col[:, bass.ds(e * KC + kc, 1)],
                                            gb_col[:, kc, bass.ds(b, 1)], ALU.add, ALU.mult) \
                                .then_inc(N["yT_ready"], 1)

                v.wait_ge(N["tokT_mm"], 1)
                for kc in range(KC):
                    v.tensor_copy(tokT2[:, 0, kc, :], [zbank, qkbank][kc][:, 0:CAP]).then_inc(N["tokT_ready"], 1)
                each_unit(v, unit)
                unit(PAIRS, 0, 0, 0, 0, turn_next=False, start=False)

            @block.scalar
            def _(act):
                act.wait_ge(N["biases_ready"], 2)

                def unit(q, b, e, par, j, finish=True):
                    act_free = q - 1
                    if not isinstance(q, int) or q >= 2:
                        act.wait_ge(N["down_mm"], act_free)
                        settle(act)
                    act.activation(b1_now[:, j, :], b1_col[:, bass.ds(e * HC, HC)], ACT.Copy) \
                        .then_inc(N["b1_picked"], 1)
                    act.wait_ge(N["b1_picked"], q + 1)
                    for m in range(HC):
                        act.wait_ge(N["up_mm"], q * HC + (m + 1))
                        act.activation(act2[:, j, m, :], up_bank(m), ACT.Gelu,
                                       bias=b1_now[:, j, m:m + 1]).then_inc(N["gelu_done"], 1)
                each_unit(act, unit)

            @block.tensor
            def _(pe):
                pe.wait_ge(N["biases_in"], 32)
                flat = chain[:, 0].rearrange("p u c -> p (u c)")
                pe.transpose(flat[:, 0:NE * HC], b1_rows[:], ident[0:NE * HC, 0:NE * HC])
                pe.transpose(flat[:, P:P + NE * KC], b2_rows[:], ident[0:NE * KC, 0:NE * KC]) \
                    .then_inc(N["biases_turned"], 1)
                pe.wait_ge(N["round_kept"], ROUNDS * 2)
                for src, rows_ in ((0, best), (1, place)):
                    for t in range(NT):
                        ins = pe.transpose(side_bank(src)[0:width[t], t * PAIRS:(t + 1) * PAIRS],
                                           rows_[:, t * TR:t * TR + width[t]], ident[0:PAIRS, 0:PAIRS])
                ins.then_inc(N["lists_turned"], 1)

                def turn(q, j):
                    pe.wait_ge(GATHERED[j % 2], (q - j % 2) * (8 * NT) + 16 * NT)
                    if not isinstance(q, int) or q > 0:
                        pe.wait_ge(N["tokT_ready"], q * KC)
                    for kc in range(KC):
                        for t in range(NT):
                            ins = pe.transpose([zbank, qkbank][kc][:, t * TR:t * TR + width[t]],
                                               tok2[0:width[t], j, t, kc * P:(kc + 1) * P],
                                               ident[0:width[t], 0:width[t]])
                    ins.then_inc(N["tokT_mm"], 1)

                def back_rows(q, j):
                    pe.wait_ge(N["yT_ready"], q * KC + KC)
                    if not isinstance(q, int) or q > 0:
                        pe.wait_ge(N["ys_ready"], q * NT)
                    for t in range(NT):
                        for kc in range(KC):
                            ins = pe.transpose(back(t)[:, kc * P:(kc + 1) * P],
                                               yT2[:, j, kc, t * TR:t * TR + width[t]], ident[:])
                    ins.then_inc(N["back_mm"], 1)

                def unit(q, b, e, par, j, finish=True):
                    if j == 0:
                        pe.wait_ge(W1[par], (e - par) * 8 + 16)
                        pe.wait_ge(W2[par], (e - par) * 8 + 16)
                    pe.wait_ge(N["tokT_ready"], q * KC + KC)
                    for m in range(HC):
                        if m < 2 and isinstance(q, int) and q == 0:
                            pe.wait_ge(N["lists_ready"], 2 * NT)
                        else:
                            pe.wait_ge(N["gelu_done"], q * HC + (m - 1))
                        for kc in range(KC):
                            ins = pe.matmul(up_bank(m), w1_2[:, par, kc, m * P:(m + 1) * P], tokT2[:, j, kc, :],
                                            start=(kc == 0), stop=(kc == KC - 1))
                        ins.then_inc(N["up_mm"], 1)
                    turn(q + 1, (j + 1) % 2)
                    if finish:
                        back_rows(q - 1, (j + 1) % 2)
                    if not isinstance(q, int) or q > 0:
                        pe.wait_ge(N["yT_ready"], q * KC)
                    else:
                        pe.wait_ge(N["biases_ready"], 2)
                    for kc in range(KC):
                        for m in range(HC):
                            if kc == 0:
                                pe.wait_ge(N["gelu_done"], q * HC + (m + 1))
                            ins = pe.matmul(chain_bank(kc), w2_2[:, par, m, kc * P:(kc + 1) * P], act2[:, j, m, :],
                                            start=(m == 0), stop=(m == HC - 1))
                    ins.then_inc(N["down_mm"], 1)

                turn(0, 0)
                each_unit(pe, unit)
                back_rows(PAIRS - 1, 1)

            @block.gpsimd
            def _(pool):
                pool.iota(batch_int[:], pattern=[[T, B]], base=0, channel_multiplier=0).then_inc(N["rows_zeroed"], 1)
                pool.wait_ge(N["lists_ready"], 2 * NT)

                def gather(q, j):
                    if not isinstance(q, int) or q >= 2:
                        pool.wait_ge(N["tokT_mm"], q - 1)
                    settle(pool)
                    pool.tensor_copy(from_row[:, j, :], row_col[:, :, bass.ds(q, 1)].rearrange("p t o -> p (t o)")) \
                        .then_inc(N["from_picked"], 1)
                    pool.wait_ge(N["from_picked"], q + 1)
                    settle(pool)
                    for t in range(NT):
                        pool.indirect_dma_start(tok2[0:width[t], j, t, :], None, h2_dram,
                                                bass.IndirectOffsetOnAxis(ap=from_row[0:width[t], j, t:t + 1], axis=0)) \
                            .then_inc(GATHERED[j], 16)

                def scatter(q, j):
                    wait_added(pool, q, j)
                    settle(pool)
                    pool.tensor_copy(to_row[:, j, :], row_col[:, :, bass.ds(q, 1)].rearrange("p t o -> p (t o)")) \
                        .then_inc(N["to_picked"], 1)
                    pool.wait_ge(N["to_picked"], q + 1)
                    pool.wait_ge(N["ys_ready"], q * NT + NT)
                    if not isinstance(q, int) or q > 0:
                        other = (j + 1) % 2
                        pool.wait_ge(ADDED[other], (q - 1 - other) * (8 * NT) + 16 * NT)
                    settle(pool)
                    for t in range(NT):
                        pool.indirect_dma_start(out_rows, bass.IndirectOffsetOnAxis(ap=to_row[0:width[t], j, t:t + 1], axis=0),
                                                ys2[0:width[t], j, t, :], None, compute_op=ALU.add) \
                            .then_inc(ADDED[j], 16)

                out_rows = out.rearrange("b t e -> (b t) e")

                gather(0, 0)
                gather(1, 1)

                def unit(q, b, e, par, j, finish=True):
                    gather(q + 2, j)
                    scatter(q, j)
                each_unit(pool, unit)
                for j in range(2):
                    pool.wait_ge(ADDED[j], PAIRS * 8 * NT)
                    pool.wait_ge(GATHERED[j], (PAIRS + 2) * 8 * NT)


_INS = ["L0_attn_x", "L0_attn_Wq", "L0_attn_Wk", "L0_attn_Wv", "L0_attn_Walpha", "L0_attn_Wbeta", "L0_attn_A_log",
        "L0_attn_dt_bias", "L0_attn_Wgate", "L0_attn_Wout", "L0_attn_rms_w", "L0_ffn_router_w", "L0_ffn_w1",
        "L0_ffn_b1", "L0_ffn_w2", "L0_ffn_b2", "L0_c", "L0_wmod"]
_OUTS = [((B, T, E), "float32")]


def kernel(**inputs):
    import numpy as _np
    import concourse.bacc as _bacc
    from concourse import mybir as _mybir
    from concourse.bass_utils import run_bass_kernel_spmd as _run

    nc = _bacc.Bacc("TRN2", target_bir_lowering=False, num_devices=1)
    arrays, args = {}, []
    for name in _INS:
        a = _np.ascontiguousarray(inputs[name])
        arrays[f"in_{name}_dram"] = a
        args.append(nc.dram_tensor(f"in_{name}_dram", a.shape, _mybir.dt.from_np(a.dtype), kind="ExternalInput").ap())
    for i, (shape, dtype) in enumerate(_OUTS):
        dt = _mybir.dt.from_np(_np.dtype(dtype))
        args.append(nc.dram_tensor(f"out_{i}_dram", shape, dt, kind="ExternalOutput").ap())
    program(nc, *args)
    r = _run(nc, [arrays], core_ids=[0])
    got = tuple(r.results[0][f"out_{i}_dram"] for i in range(len(_OUTS)))
    return got[0]
```

```python
from contextlib import ExitStack

import concourse.bass as bass
from concourse import mybir

F32 = mybir.dt.float32
U32 = mybir.dt.uint32
ALU = mybir.AluOpType
ACT = mybir.ActivationFunctionType
AX = mybir.AxisListType

P = 128
B, T, E, H, D = 8, 1024, 256, 16, 16
C = 16
NCH = T // C
HG = H * D // P
HP = H // HG
U = HG * B
KC = E // P
NE = 8
HID = 1024
CAP = T * 2 // NE + 1
ROUNDS = -(-CAP // 8)
UNROLL = 4
WIDE = 96
PAD = WIDE // C - 1
HU = U // 2

LAG_PROJ, LAG_GRAM, LAG_REC, LAG_OUT, LAG_ROUTE, LAG_SCORE = 1, 2, 5, 6, 7, 8
STEPS = NCH + LAG_SCORE
HEAD = 12

LOG1P = [1.0 / k for k in range(13, 1, -2)]


def bcast(ap, shape):
    return ap.to_broadcast(shape)


def program(nc, x, wq, wk, wv, walpha, wbeta, a_log, dt_bias, wgate, wout, rms_w,
            router_w, w1, b1, w2, b2, cond, wmod, out, debug=None):
    with ExitStack() as ctx:
        def sb(name, shape, dt=F32):
            return ctx.enter_context(nc.sbuf_tensor(name, shape, dt))

        def sem(name):
            return ctx.enter_context(nc.semaphore(name))

        def sems(names):
            return {n: sem(n) for n in names.split()}

        h2_dram = nc.dram_tensor("h2_rows", (B * T, E), F32).ap()
        score_dram = nc.dram_tensor("scores", (NE, B, T), F32).ap()

        ident = sb("ident", [P, P])
        head_mask = sb("head_mask", [P, HP])
        ident_rep = sb("ident_rep", [P, U, C])
        head_ones = sb("head_ones", [P, P])
        eps_ln = sb("eps_ln", [P, 1])
        eps_rms = sb("eps_rms", [P, 1])
        one = sb("one", [P, 1])
        zero = sb("zero", [P, 1])
        mod = sb("mod", [P, 6, E])
        SA, CA, GA, SB_, CB, GB = range(6)
        gb_col = sb("gb_col", [P, KC, B])
        neg_rate = sb("neg_rate", [P, H])
        dtb = sb("dtb", [P, 2 * H])
        w_in = {n: sb(f"w_{n}", [P, KC, E]) for n in ("q", "k", "v", "g")}
        w_ab = sb("w_ab", [P, KC, 2 * H])
        w_out = sb("w_out", [P, HG, E])
        rms_col = sb("rms_col", [P, 1])
        router_t = sb("router_t", [P, KC, NE])

        banks = [ctx.enter_context(nc.psum_tensor(f"bank{i}", [P, 512], F32)) for i in range(4)]
        gram = ctx.enter_context(nc.psum_tensor("gram", [P, U, 2 * C], F32))
        rec_banks = ctx.enter_context(nc.psum_tensor("rec_banks", [P, 2, 512], F32))
        obank = ctx.enter_context(nc.psum_tensor("obank", [P, 2, E], F32))
        zbank, qkbank, vgbank, tbank = banks

        K = sems("c_pool c_vec c_act c_pe c_in")

        x_v = x.rearrange("b (n i) e -> n b i e", i=C)
        out_v = out.rearrange("b (n i) e -> n b i e", i=C)
        h2_v = h2_dram.rearrange("(b n i) e -> n b i e", b=B, i=C)
        score_v = score_dram.rearrange("e b (n i) -> n e b i", i=C)

        def rows(ap):
            return ap

        with ExitStack() as mixer:
            def mb(name, shape, dt=F32):
                return mixer.enter_context(nc.sbuf_tensor(name, shape, dt))

            x4 = mb("x4", [P, 4, E])
            stats = mb("stats", [P, 6])
            mv = mb("mv", [P, 2])
            rstd = mb("rstd", [P, 2])
            xn = mb("xn", [P, E])
            h = mb("h", [P, E])
            hT2 = mb("hT2", [P, 2, KC, P])
            sqk = mb("sqk", [P, 4, P])
            inv_norm = mb("inv_norm", [P, 4, P])
            mk4 = mb("mk4", [P, 4, U, 4, C])
            GQ, GI, KF, QF = range(4)
            head_side = mb("head_side", [P, 2])
            pair_mask = mb("pair_mask", [P, HP // 2])
            k_pair = mb("k_pair", [P, U, 2, C])
            k_turn = mb("k_turn", [P, U, 2, C])
            k_tok = mb("k_tok", [P, U, C])
            k_diag2 = mb("k_diag2", [P, 2, U, HP, C])
            v4 = mb("v4", [P, 4, U, C])
            gate8 = mb("gate8", [P, 8, HG, P])
            sig = mb("sig", [P, 3, E])
            z32 = mb("z32", [P, 2 * H])
            w32 = mb("w32", [P, 2 * H])
            u32 = mb("u32", [P, 2 * H])
            den = mb("den", [P, 2 * H])
            rec = mb("rec", [P, 2 * H])
            ser = mb("ser", [P, 6, H])
            decay_rep = mb("decay_rep", [P, 2, H, C])
            alpha0 = mb("alpha0", [P, U, C])
            start0 = mb("start0", [P, U, C])
            beta4 = mb("beta4", [P, 4, U, C])
            dec4 = mb("dec4", [P, 4, U, C])
            gam4 = mb("gam4", [P, 4, U, C])
            ap4 = mb("ap4", [P, 4, U + 1, 3, C])
            low = mb("low", [P, 2, 2 * P * 2])
            solved = mb("solved", [P, C, 2, C])
            solved_b = mb("solved_b", [P, C, 2, C])
            prod = mb("prod", [P, 2 * C * C])
            t2 = mb("t2", [P, 2, 2, U, C])
            t_diag2 = mb("t_diag2", [P, 2, U, HP, C])
            s_pair = mb("s_pair", [P, U, 2, C])
            s_turn = mb("s_turn", [P, U, 2, C])
            s_diag = mb("s_diag", [P, U, HP, C])
            held = mb("held", [P, U, 2, C])
            os = mb("os", [P, U, 2, C])
            rhs_g = mb("rhs_g", [P, U, C])
            rhs_f = mb("rhs_f", [P, U, C])
            r_pair = mb("r_pair", [P, U, 2, C])
            r_turn = mb("r_turn", [P, U, 2, C])
            rhs = mb("rhs", [P, U + PAD, C])
            d_diag = mb("d_diag", [P, U, HP, C])
            o_sq = mb("o_sq", [P, E])
            o_r = mb("o_r", [P, 2, E])
            og = mb("og", [P, 2, HG, P])
            xr2 = mb("xr2", [P, 2, E])
            x2_2 = mb("x2_2", [P, 2, E])
            xn2 = mb("xn2", [P, E])
            h2_2 = mb("h2_2", [P, 2, E])
            stats2 = mb("stats2", [P, 6])
            mv2 = mb("mv2", [P, 2])
            rstd2 = mb("rstd2", [P, 2])
            tick = mb("tick", [P, 2])
            h2T = mb("h2T", [P, KC, P])
            logit = mb("logit", [P, NE])
            nmax = mb("nmax", [P, 1])
            esum = mb("esum", [P, 2])
            expl = mb("expl", [P, NE])
            sc = mb("sc", [P, NE])
            scT4 = mb("scT4", [NE, 4, P])

            wm = k_diag2[:, 0:2].rearrange("p r u g c -> p (r u g c)")[:, 0:KC * 6 * E] \
                .rearrange("p (k n) -> p k n", k=KC)
            cT = sqk[:, 0:KC, :]

            XS = [sem(f"x_loaded{i}") for i in range(4)]
            XR = [sem(f"residual_loaded{i}") for i in range(4)]
            XO = [sem(f"x2_stored{i}") for i in range(4)]
            HO = [sem(f"h2_stored{i}") for i in range(4)]
            SO = [sem(f"scores_stored{i}") for i in range(4)]
            M = sems("stats_done mean_done ln_rstd rstd_done xn_done hmul_done h_done xt_done hT_done "
                     "proj_done z_done sq_done vcopy_done gate_e gate_l gate_s gate_done ss_done lnss_done "
                     "inv_done k_done q_done decay_steps expz_done alpha_done beta_done ab_done "
                     "alpha0_done start0_done beta_copied dec_done gam_done gq_done gi_done kdiag_done "
                     "kpair_done kturn_done ktok_done dk_done gram_done ap_done lanes_steps t_done tdiag_done "
                     "read_mm gks_done rhsf_done rpair_done rturn_done rhs_done delta_mm ddiag_done "
                     "add_mm held_done sum_done spair_done sturn_done sdiag_done osq_done ms_done lnms_done rms_done "
                     "og1_done og_done y_done yga_done x2_done stats2_done mean2_done ln_rstd2 "
                     "rstd2_done xn2_done h2mul_done h2_done h2t_mm h2T_done rl_done logit_done "
                     "max_done expl_done esum_done sc_done st_done scT_done")

            def act_on(c):
                return not isinstance(c, int) or 0 <= c < NCH

            def wait(eng, name, c, per=1, plus=None):
                if isinstance(c, int) and c < 0:
                    return
                eng.wait_ge(M[name], c * per + (per if plus is None else plus))

            def wait_ring(eng, ring, c, slot):
                if isinstance(c, int) and c < 0:
                    return
                eng.wait_ge(ring[slot], (c - slot) * 4 + 16)

            def run(eng, step):
                for n in range(HEAD):
                    step(n, n % UNROLL)
                with eng.Fori(HEAD // UNROLL, NCH // UNROLL) as m:
                    for k in range(UNROLL):
                        step(m * UNROLL + k, k)
                for n in range(NCH, STEPS):
                    step(n, n % UNROLL)

            def half(c, h):
                return c, 2, h + 1

            def units(h):
                return slice(h * HU, (h + 1) * HU)

            OT, ST, KST = range(3)
            rec_block = [rec_banks[:, h, 0:(HU + 1) * 3 * C].rearrange("p (u n) -> p u n", n=3 * C) for h in range(2)]

            def banked(h, part, end=None):
                return rec_block[h][:, 0:HU, part * C:(part + 1 if end is None else end) * C]

            small_z, small_rl, small_st = obank[:, 1, 0:2 * H], obank[:, 1, 2 * H:2 * H + NE], obank[0:NE, 1, P:2 * P]

            def slot(k, lag, size=4):
                return (k - lag) % size

            DECAY = 12 + len(LOG1P)
            EARLY_DECAY = 8
            LANES = 4 + 2 * (C - 1)
            LOADS = 12 + HP
            SETUP_POOL = 16
            SETUP_ACT = 5
            SILU_VEC = 5 + C + HG + 3
            COND_VEC = SILU_VEC + 2 * KC
            SETUP_VEC = COND_VEC + 12

            with nc.Block() as block:
                @block.sync
                def _(sp):
                    loads = [(w_in["q"], wq), (w_in["k"], wk), (w_in["v"], wv), (w_in["g"], wgate)]
                    sp.dma_start(wm, wmod.rearrange("(k p) n -> p k n", p=P)).then_inc(K["c_in"], 16)
                    for dst, src in loads:
                        sp.dma_start(dst[:], src.rearrange("(k p) n -> p k n", p=P)).then_inc(K["c_in"], 16)
                    sp.dma_start(w_ab[:, :, 0:H], walpha.rearrange("(k p) n -> p k n", p=P)).then_inc(K["c_in"], 16)
                    sp.dma_start(w_ab[:, :, H:2 * H], wbeta.rearrange("(k p) n -> p k n", p=P)).then_inc(K["c_in"], 16)
                    sp.dma_start(w_out[:], wout.rearrange("(g p) n -> p g n", p=P)).then_inc(K["c_in"], 16)
                    sp.dma_start(z32[:, 0:H], a_log.partition_broadcast(P)).then_inc(K["c_in"], 16)
                    sp.dma_start(dtb[:, 0:H], dt_bias.partition_broadcast(P)).then_inc(K["c_in"], 16)
                    for g in range(HP):
                        sp.dma_start(rms_col[g * D:(g + 1) * D, :], rms_w.unsqueeze(1)).then_inc(K["c_in"], 16)
                    sp.dma_start(xn[0:NE, :], router_w).then_inc(K["c_in"], 16)
                    sp.dma_start(h[0:B, :], cond).then_inc(K["c_in"], 16)

                    sp.wait_ge(K["c_vec"], SETUP_VEC)

                    def step(n, k):
                        if act_on(n):
                            wait(sp, "xn_done", n - 4)
                            sp.dma_start(rows(x4[:, k, :]), x_v[n]).then_inc(XS[k], 16)
                        o, ko = n - LAG_OUT + 1, slot(k, LAG_OUT - 1)
                        if act_on(o):
                            wait(sp, "x2_done", o - 2)
                            sp.dma_start(rows(xr2[:, ko % 2, :]), x_v[o]).then_inc(XR[ko], 16)
                        o, ko = n - LAG_ROUTE, slot(k, LAG_ROUTE)
                        if act_on(o):
                            wait(sp, "x2_done", o)
                            sp.dma_start(out_v[o], rows(x2_2[:, ko % 2, :])).then_inc(XO[ko], 16)
                            wait(sp, "h2_done", o)
                            sp.dma_start(h2_v[o], rows(h2_2[:, ko % 2, :])).then_inc(HO[ko], 16)
                        o, ko = n - LAG_SCORE, slot(k, LAG_SCORE)
                        if act_on(o):
                            wait(sp, "scT_done", o)
                            sp.dma_start(score_v[o], scT4[:, ko, :].rearrange("e (b i) -> e b i", i=C)) \
                                .then_inc(SO[ko], 16)
                    run(sp, step)
                    for ring in (XO, HO, SO):
                        for s in ring:
                            sp.wait_ge(s, 16 * (NCH // 4))

                @block.gpsimd
                def _(pool):
                    count = [0]

                    def link(ins):
                        count[0] += 1
                        ins.then_inc(K["c_pool"], 1)
                        pool.wait_ge(K["c_pool"], count[0])

                    link(pool.memset(ident[:], 0.0))
                    link(pool.memset(head_mask[:], 1.0))
                    link(pool.affine_select(out=ident[:], in_=ident[:], compare_op=ALU.not_equal, fill=1.0,
                                            base=0, pattern=[[-1, P]], channel_multiplier=1))
                    link(pool.affine_select(out=head_mask[:], in_=head_mask[:], compare_op=ALU.is_ge, fill=0.0,
                                            base=0, pattern=[[-D, HP]], channel_multiplier=1))
                    link(pool.affine_select(out=head_mask[:], in_=head_mask[:], compare_op=ALU.is_ge, fill=0.0,
                                            base=D - 1, pattern=[[D, HP]], channel_multiplier=-1))
                    link(pool.tensor_copy(head_ones[:].rearrange("p (h r) -> p h r", r=D),
                                          bcast(head_mask[:].unsqueeze(2), [P, HP, D])))
                    for tile, value in ((eps_ln, 1e-5), (eps_rms, 1e-6), (one, 1.0), (zero, 0.0)):
                        link(pool.memset(tile[:], value))
                    link(pool.memset(dtb[:, H:], 0.0))
                    for tile in (alpha0, start0, s_diag, ap4, rhs):
                        link(pool.memset(tile[:], 0.0))

                    def diag(dst, src):
                        return pool.tensor_tensor(
                            out=dst, in0=bcast(src.unsqueeze(2), [P, U, HP, C]),
                            in1=bcast(head_mask[:].unsqueeze(1).unsqueeze(3), [P, U, HP, C]), op=ALU.mult)

                    def step(n, k):
                        r, kr = n - LAG_REC, slot(k, LAG_REC)
                        if act_on(r):
                            pool.wait_ge(M["t_done"], r - kr % 2 + 2)
                            wait(pool, "delta_mm", r - 2)
                            diag(t_diag2[:, kr % 2], t2[:, kr // 2, kr % 2]).then_inc(M["tdiag_done"], 1)
                        e, ke = n - LAG_ROUTE, slot(k, LAG_ROUTE)
                        if act_on(e):
                            wait(pool, "xn2_done", e)
                            wait_ring(pool, HO, e - 2, (ke + 2) % 4)
                            wait(pool, "h2t_mm", e - 2)
                            pool.tensor_tensor(out=h2_2[:, ke % 2, :], in0=xn2[:], in1=mod[:, CB, :], op=ALU.mult) \
                                .then_inc(M["h2mul_done"], 1)
                            wait(pool, "h2mul_done", e)
                            pool.tensor_tensor(out=h2_2[:, ke % 2, :], in0=h2_2[:, ke % 2, :], in1=mod[:, SB_, :], op=ALU.add) \
                                .then_inc(M["h2_done"], 1)
                        g, kg = n - LAG_GRAM, slot(k, LAG_GRAM)
                        if act_on(g):
                            wait(pool, "gam_done", g)
                            wait(pool, "q_done", g)
                            wait(pool, "read_mm", g - 4, 2)
                            pool.tensor_tensor(out=mk4[:, kg, :, GQ, :], in0=gam4[:, kg], in1=mk4[:, kg, :, QF, :],
                                               op=ALU.mult).then_inc(M["gq_done"], 1)
                            pool.tensor_tensor(out=mk4[:, kg, :, GI, :], in0=ident_rep[:],
                                               in1=bcast(gam4[:, kg, :, C - 1:C], [P, U, C]), op=ALU.mult) \
                                .then_inc(M["gi_done"], 1)
                        o, ko = n - LAG_OUT, slot(k, LAG_OUT)
                        if act_on(o):
                            wait(pool, "sum_done", o, 2)
                            wait(pool, "gate_done", o)
                            wait(pool, "og_done", o - 1)
                            g8 = gate8[:, o % 8].rearrange("p g (b i) -> p (g b) i", i=C)
                            pool.tensor_tensor(out=o_r[:, 1, :].rearrange("p (u i) -> p u i", i=C), in0=os[:, :, 0, :],
                                               in1=g8, op=ALU.mult) \
                                .then_inc(M["og1_done"], 1)
                            wait(pool, "rms_done", o)
                            wait(pool, "og1_done", o)
                            wait(pool, "y_done", o - 2)
                            pool.tensor_tensor(out=og[:, ko % 2].rearrange("p g t -> p (g t)"), in0=o_r[:, 1, :],
                                               in1=o_r[:, 0, :], op=ALU.mult).then_inc(M["og_done"], 1)
                        if act_on(g):
                            wait(pool, "kturn_done", g)
                            wait(pool, "dk_done", g - 1)
                            pool.tensor_tensor(out=k_tok[:], in0=k_turn[:, :, 0, :], in1=k_turn[:, :, 1, :],
                                               op=ALU.add).then_inc(M["ktok_done"], 1)
                            wait(pool, "ktok_done", g)
                            wait(pool, "add_mm", g - 4, 2)
                            pool.tensor_tensor(out=ap4[:, kg, 0:U, 2, :], in0=k_tok[:],
                                               in1=bcast(dec4[:, kg, :, C - 1:C], [P, U, C]), op=ALU.mult) \
                                .then_inc(M["dk_done"], 1)
                        if act_on(n):
                            wait(pool, "xn_done", n)
                            wait(pool, "xt_done", n - 1)
                            pool.tensor_tensor(out=h[:], in0=xn[:], in1=mod[:, CA, :], op=ALU.mult) \
                                .then_inc(M["hmul_done"], 1)
                            wait(pool, "hmul_done", n)
                            pool.tensor_tensor(out=h[:], in0=h[:], in1=mod[:, SA, :], op=ALU.add) \
                                .then_inc(M["h_done"], 1)
                        c, kc_ = n - LAG_PROJ, slot(k, LAG_PROJ)
                        if act_on(c):
                            wait(pool, "k_done", c)
                            wait(pool, "gram_done", c - 2)
                            diag(k_diag2[:, kc_ % 2], mk4[:, kc_, :, KF, :]).then_inc(M["kdiag_done"], 1)

                    pool.wait_ge(K["c_vec"], SETUP_VEC)
                    run(pool, step)

                @block.scalar
                def _(act):
                    count = [0]

                    def link(ins):
                        count[0] += 1
                        ins.then_inc(K["c_act"], 1)
                        act.wait_ge(K["c_act"], count[0])

                    act.preload_act_table_set("natural_log_exp_and_others")
                    act.wait_ge(K["c_pool"], SETUP_POOL)
                    act.wait_ge(K["c_in"], LOADS * 16)
                    link(act.activation(x4[0:B, 0, :], h[0:B, :], ACT.Exp, scale=-1.0, bias=zero[0:B, :]))
                    link(act.activation(neg_rate[:], z32[:, 0:H], ACT.Exp, bias=zero[:]))
                    act.wait_ge(K["c_pe"], 3)
                    for m in range(3):
                        link(act.activation(mod[:, 2 * m:2 * m + 2, :].rearrange("p m e -> p (m e)"),
                                            [zbank, qkbank, vgbank][m][:, :], ACT.Copy))

                    def pair(dst, src):
                        for s in range(2):
                            ins = act.activation(dst[:, :, s, :], src, ACT.Copy, scale=head_side[:, s:s + 1])
                        return ins

                    def step(n, k):
                        o, ko = n - LAG_OUT, slot(k, LAG_OUT)
                        e = n - LAG_ROUTE
                        if act_on(o):
                            wait(act, "sum_done", o, 2)
                            wait(act, "rms_done", o - 1)
                            act.activation(o_sq[:].rearrange("p (u c) -> p u c", c=C), os[:, :, 0, :], ACT.Square,
                                           bias=zero[:]).then_inc(M["osq_done"], 1)
                        r = n - LAG_REC
                        if act_on(r):
                            for h_ in range(2):
                                wait(act, "read_mm", *half(r, h_))
                                wait(act, "gks_done", *half(r, h_))
                                wait(act, "sum_done", *half(r - 1, h_))
                                act.activation(held[:, units(h_)].rearrange("p u a c -> p u (a c)"), banked(h_, OT, ST + 1),
                                               ACT.Copy).then_inc(M["held_done"], 1)
                        g, kg = n - LAG_GRAM, slot(k, LAG_GRAM)
                        if act_on(g):
                            wait(act, "ab_done", g)
                            wait(act, "gam_done", g - 1)
                            ab = tbank[:, 0:2 * E].rearrange("p (a u i) -> p a u i", a=2, i=C)
                            act.activation(alpha0[:, :, 1:C], ab[:, 0, :, 1:C], ACT.Copy) \
                                .then_inc(M["alpha0_done"], 1)
                            act.activation(start0[:, :, 0:1], ab[:, 0, :, 0:1], ACT.Copy) \
                                .then_inc(M["start0_done"], 1)
                            act.activation(beta4[:, kg], ab[:, 1], ACT.Copy).then_inc(M["beta_copied"], 1)
                        if act_on(n):
                            wait(act, "mean_done", n)
                            wait(act, "xn_done", n - 1)
                            act.activation(rstd[:, 1:2], mv[:, 1:2], ACT.Ln, bias=eps_ln[:]).then_inc(M["ln_rstd"], 1)
                            wait(act, "ln_rstd", n)
                            act.activation(rstd[:, 0:1], rstd[:, 1:2], ACT.Exp, scale=-0.5, bias=zero[:]) \
                                .then_inc(M["rstd_done"], 1)
                        c, kc_ = n - LAG_PROJ, slot(k, LAG_PROJ)
                        if act_on(c):
                            wait(act, "xt_done", c)
                            wait(act, "proj_done", c - 2)
                            act.activation(hT2[:, kc_ % 2].rearrange("p k t -> p (k t)"), tbank[:, 0:E], ACT.Copy) \
                                .then_inc(M["hT_done"], 1)
                        if act_on(o):
                            wait(act, "ms_done", o)
                            wait(act, "og_done", o - 1)
                            act.activation(o_sq[:], zbank[:, 128:128 + E], ACT.Ln, scale=1.0 / D ** 2, bias=eps_rms[:]) \
                                .then_inc(M["lnms_done"], 1)
                            wait(act, "lnms_done", o)
                            act.activation(o_r[:, 0, :], o_sq[:], ACT.Exp, scale=-0.5, bias=zero[:]) \
                                .then_inc(M["rms_done"], 1)
                        if act_on(e):
                            wait(act, "h2t_mm", e)
                            wait(act, "rl_done", e - 1)
                            act.activation(h2T[:].rearrange("p k t -> p (k t)"), tbank[:, 0:E], ACT.Copy) \
                                .then_inc(M["h2T_done"], 1)
                        if act_on(c):
                            wait(act, "proj_done", c)
                            wait(act, "inv_done", c - 1)
                            act.activation(sqk[:].rearrange("p m t -> p (m t)"), qkbank[:, :], ACT.Square,
                                           bias=zero[:]).then_inc(M["sq_done"], 1)
                            wait(act, "rhsf_done", c - 4, 2)
                            act.activation(v4[:, kc_].rearrange("p u t -> p (u t)"), vgbank[:, 0:E], ACT.Copy) \
                                .then_inc(M["vcopy_done"], 1)
                            wait(act, "decay_steps", c, DECAY, 3)
                            act.activation(u32[:], w32[:], ACT.Exp, bias=zero[:]).then_inc(M["expz_done"], 1)
                            wait(act, "gate_done", c - 1)
                            act.activation(sig[:, 0, :], vgbank[:, E:2 * E], ACT.Exp, scale=-1.0, bias=zero[:]) \
                                .then_inc(M["gate_e"], 1)
                            wait(act, "gate_e", c)
                            act.activation(sig[:, 1, :], sig[:, 0, :], ACT.Ln, bias=one[:]).then_inc(M["gate_l"], 1)
                            wait(act, "gate_l", c)
                            act.activation(sig[:, 2, :], sig[:, 1, :], ACT.Exp, scale=-1.0, bias=zero[:]) \
                                .then_inc(M["gate_s"], 1)
                        r = n - LAG_REC
                        if act_on(r):
                            for h_ in range(2):
                                wait(act, "sum_done", *half(r, h_))
                                wait(act, "sturn_done", *half(r - 1, h_))
                                pair(s_pair[:, units(h_)], os[:, units(h_), 1, :]).then_inc(M["spair_done"], 1)
                        if act_on(c):
                            wait(act, "ss_done", c)
                            act.activation(sqk[:].rearrange("p m t -> p (m t)"), tbank[:, :], ACT.Ln,
                                           bias=zero[:]).then_inc(M["lnss_done"], 1)
                            wait(act, "lnss_done", c)
                            wait(act, "q_done", c - 1)
                            act.activation(inv_norm[:], sqk[:], ACT.Exp, scale=-0.5, bias=zero[:]) \
                                .then_inc(M["inv_done"], 1)
                        if act_on(o):
                            wait(act, "mean2_done", o)
                            wait(act, "xn2_done", o - 1)
                            act.activation(rstd2[:, 1:2], mv2[:, 1:2], ACT.Ln, bias=eps_ln[:]) \
                                .then_inc(M["ln_rstd2"], 1)
                            wait(act, "ln_rstd2", o)
                            act.activation(rstd2[:, 0:1], rstd2[:, 1:2], ACT.Exp, scale=-0.5, bias=zero[:]) \
                                .then_inc(M["rstd2_done"], 1)
                        if act_on(e):
                            wait(act, "max_done", e)
                            wait(act, "sc_done", e - 1)
                            act.activation(expl[:], logit[:], ACT.Exp, bias=nmax[:], accum_out=esum[:, 0:1]) \
                                .then_inc(M["expl_done"], 1)
                        if act_on(c):
                            wait(act, "k_done", c)
                            wait(act, "kturn_done", c - 1)
                            pair(k_pair[:], mk4[:, kc_, :, KF, :]).then_inc(M["kpair_done"], 1)
                        if act_on(c):
                            wait(act, "decay_steps", c, DECAY, DECAY)
                            wait(act, "ab_done", c - 1)
                            act.activation(decay_rep[:, 0], bcast(ser[:, 5, :].unsqueeze(2), [P, H, C]), ACT.Exp,
                                           bias=zero[:]).then_inc(M["alpha_done"], 1)
                            act.activation(decay_rep[:, 1], bcast(rec[:, H:].unsqueeze(2), [P, H, C]), ACT.Copy) \
                                .then_inc(M["beta_done"], 1)
                    run(act, step)

                @block.vector
                def _(v):
                    count = [0]

                    def link(ins):
                        count[0] += 1
                        ins.then_inc(K["c_vec"], 1)
                        v.wait_ge(K["c_vec"], count[0])

                    v.wait_ge(K["c_pool"], SETUP_POOL)
                    v.wait_ge(K["c_in"], LOADS * 16)
                    link(v.tensor_reduce(ident_rep[:, 0, :], ident[:].rearrange("p (h r) -> p r h", r=D), AX.X, ALU.add))
                    link(v.tensor_copy(ident_rep[:, 1:, :], bcast(ident_rep[:, 0:1, :], [P, U - 1, C])))
                    link(v.tensor_reduce(head_side[:], head_mask[:].rearrange("p (a b) -> p b a", b=2), AX.X, ALU.add))
                    link(v.tensor_reduce(pair_mask[:], head_mask[:].rearrange("p (a b) -> p a b", b=2), AX.X, ALU.add))
                    link(v.memset(solved[:], 0.0))
                    for i in range(C):
                        link(v.memset(solved[:, i, :, i:i + 1], 1.0))
                    for g in range(HG):
                        link(v.tensor_scalar(w_out[:, g, :], w_out[:, g, :], rms_col[:, 0:1], D ** -0.5, ALU.mult, ALU.mult))
                    v.wait_ge(K["c_act"], 1)
                    link(v.tensor_scalar(x4[0:B, 1, :], x4[0:B, 0, :], 1.0, None, ALU.add))
                    link(v.reciprocal(x4[0:B, 2, :], x4[0:B, 1, :]))
                    link(v.tensor_tensor(out=x4[0:B, 3, :], in0=x4[0:B, 2, :], in1=h[0:B, :], op=ALU.mult))
                    v.wait_ge(K["c_pe"], 1)
                    for kc in range(KC):
                        link(v.tensor_copy(cT[:, kc, :].rearrange("p (b i) -> p b i", i=C),
                                           bcast(tbank[:, kc * P:kc * P + B].unsqueeze(2), [P, B, C])))
                        link(v.tensor_copy(router_t[:, kc, :], tbank[:, (2 + kc) * P:(2 + kc) * P + NE]))
                    v.wait_ge(K["c_act"], SETUP_ACT)
                    link(v.tensor_scalar(neg_rate[:], neg_rate[:], -1.0, None, ALU.mult))
                    for m in (CA, CB):
                        link(v.tensor_scalar(mod[:, m, :], mod[:, m, :], 1.0, None, ALU.add))
                    for m in (GA, GB):
                        link(v.tensor_scalar(xr2[:, 0, :], mod[:, m, :], 0.0, 2.0, ALU.is_ge, ALU.mult))
                        link(v.scalar_tensor_tensor(out=xr2[:, 1, :], in0=mod[:, m, :], scalar=-1.0,
                                                    in1=mod[:, m, :], op0=ALU.mult, op1=ALU.max))
                        link(v.tensor_scalar(xr2[:, 1, :], xr2[:, 1, :], 0.25, None, ALU.max))
                        link(v.scalar_tensor_tensor(out=mod[:, m, :], in0=xr2[:, 0, :], scalar=-1.0,
                                                    in1=xr2[:, 1, :], op0=ALU.add, op1=ALU.mult))
                    v.wait_ge(K["c_pe"], 4)
                    link(v.tensor_copy(gb_col[:], tbank[:, 0:2 * P].rearrange("p (k b i) -> p k b i", k=KC, i=C)[:, :, :, 0]))
                    assert count[0] == SETUP_VEC, count[0]

                    def solve_row(even, i, reduce=None):
                        if reduce is None:
                            solve_row(even, i, False)
                            solve_row(even, i, True)
                            return
                        base = LANES // 2 * even
                        a = low[:, 0, :].rearrange("p (i h l) -> p i h l", h=2, l=C)[:, i, :, 0:i]
                        t = solved[:, 0:i, :, 0:i].rearrange("p l h j -> p h j l")
                        pr = prod[:, 0:2 * i * i].rearrange("p (h j l) -> p h j l", h=2, l=i)
                        if not reduce:
                            v.wait_ge(M["lanes_steps"], base + 3 + 2 * (i - 1))
                            v.tensor_tensor(out=pr, in0=bcast(a.unsqueeze(2), [P, 2, i, i]), in1=t, op=ALU.mult) \
                                .then_inc(M["lanes_steps"], 1)
                            return
                        v.wait_ge(M["lanes_steps"], base + 4 + 2 * (i - 1))
                        v.tensor_reduce(solved[:, i, :, 0:i], pr, AX.X, ALU.add, negate=True) \
                            .then_inc(M["lanes_steps"], 1)

                    def lanes_in(even, s):
                        lane = low[:].rearrange("p a (i c) -> p a i c", c=32)
                        v.transpose(lane[:, 0].rearrange("p i (c u) -> p i c u", c=2),
                                    ap4[:, s:s + 2, 0:U, 0, :].rearrange("p c u i -> p i c u")) \
                            .then_inc(M["lanes_steps"], 1)
                        v.transpose(lane[:, 1], beta4[:, s:s + 2].rearrange("p c u i -> p i (c u)")) \
                            .then_inc(M["lanes_steps"], 1)
                        v.wait_ge(M["lanes_steps"], LANES // 2 * even + 2)
                        v.tensor_tensor(out=low[:, 0, :], in0=low[:, 0, :], in1=low[:, 1, :], op=ALU.mult) \
                            .then_inc(M["lanes_steps"], 1)

                    def lanes_out(even, s):
                        v.wait_ge(M["lanes_steps"], LANES // 2 * even + 3 + 2 * (C - 1))
                        beta = low[:, 1, :].rearrange("p (j h r) -> p j h r", h=2, r=C)[:, :, :, 0] \
                            .rearrange("p j h -> p h j")
                        v.tensor_tensor(out=solved_b[:], in0=solved[:],
                                        in1=bcast(beta.unsqueeze(1), [P, C, 2, C]), op=ALU.mult) \
                            .then_inc(M["lanes_steps"], 1)
                        v.wait_ge(M["lanes_steps"], LANES // 2 * even + 4 + 2 * (C - 1))
                        wait(v, "tdiag_done", even + 1 - 4)
                        v.transpose(t2[:, s].rearrange("p c u i -> p i (c u)"),
                                    solved_b[:].rearrange("p i h j -> p i (h j)")).then_inc(M["t_done"], 2)

                    def decay_step(base, j):
                        last = 4 + len(LOG1P)
                        v.wait_ge(M["decay_steps"], base + (3 + j))
                        if j == 0:
                            ins = v.tensor_scalar(den[:, 0:H], u32[:, 0:H], 2.0, None, ALU.add)
                        elif j == 1:
                            ins = v.tensor_scalar(den[:, H:], u32[:, H:], 1.0, None, ALU.add)
                        elif j == 2:
                            ins = v.reciprocal(rec[:], den[:])
                        elif j == 3:
                            ins = v.tensor_tensor(out=ser[:, 0, :], in0=u32[:, 0:H], in1=rec[:, 0:H], op=ALU.mult)
                        elif j == 4:
                            ins = v.tensor_tensor(out=ser[:, 1, :], in0=ser[:, 0, :], in1=ser[:, 0, :], op=ALU.mult)
                        elif j == 5:
                            ins = v.tensor_scalar(ser[:, 2, :], ser[:, 1, :], LOG1P[0], None, ALU.mult)
                        elif j <= last:
                            m = j - 6
                            ins = v.scalar_tensor_tensor(out=ser[:, 3 - m % 2, :], in0=ser[:, 2 + m % 2, :],
                                                         scalar=LOG1P[m + 1], in1=ser[:, 1, :], op0=ALU.add, op1=ALU.mult)
                        elif j == last + 1:
                            ins = v.scalar_tensor_tensor(out=ser[:, 4, :], in0=ser[:, 3, :], scalar=1.0,
                                                         in1=ser[:, 0, :], op0=ALU.add, op1=ALU.mult)
                        elif j == last + 2:
                            ins = v.tensor_scalar(ser[:, 2, :], z32[:, 0:H], 0.0, None, ALU.max)
                        elif j == last + 3:
                            ins = v.scalar_tensor_tensor(out=ser[:, 3, :], in0=ser[:, 4, :], scalar=2.0,
                                                         in1=ser[:, 2, :], op0=ALU.mult, op1=ALU.add)
                        else:
                            ins = v.tensor_tensor(out=ser[:, 5, :], in0=ser[:, 3, :], in1=neg_rate[:], op=ALU.mult)
                        ins.then_inc(M["decay_steps"], 1)

                    def step(n, k):
                        r, kr = n - LAG_REC, slot(k, LAG_REC)
                        o, ko = n - LAG_OUT, slot(k, LAG_OUT)
                        g, kg = n - LAG_GRAM, slot(k, LAG_GRAM)
                        c, kc_ = n - LAG_PROJ, slot(k, LAG_PROJ)
                        e = n - LAG_ROUTE
                        w, kw = n - LAG_SCORE, slot(k, LAG_SCORE)
                        first = k % 2 == 1
                        lag = LAG_GRAM + 1 if first else LAG_GRAM + 2
                        even, ps = n - lag, slot(k, lag)
                        solving = act_on(even)

                        if act_on(r):
                            for h_ in range(2):
                                wait(v, "read_mm", *half(r, h_))
                                wait(v, "rhsf_done", *half(r - 1, h_))
                                v.tensor_tensor(out=rhs_g[:, units(h_)], in0=banked(h_, KST), in1=gam4[:, kr, units(h_)],
                                                op=ALU.mult).then_inc(M["gks_done"], 1)
                            for h_ in range(2):
                                wait(v, "gks_done", *half(r, h_))
                                wait(v, "vcopy_done", r)
                                wait(v, "rpair_done", *half(r - 1, h_))
                                v.tensor_tensor(out=rhs_f[:, units(h_)], in0=v4[:, kr, units(h_)], in1=rhs_g[:, units(h_)],
                                                op=ALU.subtract).then_inc(M["rhsf_done"], 1)
                            for h_ in range(2):
                                wait(v, "rhsf_done", *half(r, h_))
                                wait(v, "rturn_done", *half(r - 1, h_))
                                v.tensor_tensor(out=r_pair[:, units(h_)],
                                                in0=bcast(rhs_f[:, units(h_)].unsqueeze(2), [P, HU, 2, C]),
                                                in1=bcast(head_side[:].unsqueeze(1).unsqueeze(3), [P, HU, 2, C]),
                                                op=ALU.mult).then_inc(M["rpair_done"], 1)
                            for h_ in range(2):
                                wait(v, "rpair_done", *half(r, h_))
                                wait(v, "rhs_done", *half(r - 1, h_))
                                v.transpose(r_turn[:, units(h_)].rearrange("p u s c -> p (u s c)"),
                                            r_pair[:, units(h_)].rearrange("p u s c -> p (u s c)")) \
                                    .then_inc(M["rturn_done"], 1)
                            for h_ in range(2):
                                wait(v, "rturn_done", *half(r, h_))
                                wait(v, "delta_mm", r - 1)
                                v.tensor_tensor(out=rhs[:, units(h_)], in0=r_turn[:, units(h_), 0, :],
                                                in1=r_turn[:, units(h_), 1, :], op=ALU.add) \
                                    .then_inc(M["rhs_done"], 1)
                        if act_on(n):
                            wait_ring(v, XS, n, k)
                            wait(v, "mean_done", n - 1)
                            v.bn_stats(stats[:], x4[:, k, :]).then_inc(M["stats_done"], 1)
                            wait(v, "rstd_done", n - 1)
                            wait(v, "xn_done", n - 1)
                            wait(v, "stats_done", n)
                            v.tensor_copy(tick[:, 0:1], zero[:])
                            v.bn_aggr(mv[:], stats[:]).then_inc(M["mean_done"], 1)
                        if act_on(g):
                            wait(v, "beta_copied", g)
                            for name in ("ap_done", "dk_done", "gi_done"):
                                wait(v, name, g - 4)
                            wait(v, "gks_done", g - 4, 2)
                            v.tensor_tensor_scan(dec4[:, kg].rearrange("p u i -> p (u i)"),
                                                 alpha0[:].rearrange("p u i -> p (u i)"),
                                                 ident_rep[:].rearrange("p u i -> p (u i)"), 0.0, ALU.mult, ALU.add) \
                                .then_inc(M["dec_done"], 1)
                            v.tensor_tensor_scan(gam4[:, kg].rearrange("p u i -> p (u i)"),
                                                 alpha0[:].rearrange("p u i -> p (u i)"),
                                                 start0[:].rearrange("p u i -> p (u i)"), 0.0, ALU.mult, ALU.add) \
                                .then_inc(M["gam_done"], 1)
                        if act_on(g):
                            wait(v, "gram_done", g)
                            wait(v, "dec_done", g)
                            wait(v, "add_mm", g - 4, 2)
                            v.tensor_tensor(out=ap4[:, kg, 0:U, 0:2, :], in0=gram[:].rearrange("p u (a i) -> p u a i", a=2),
                                            in1=bcast(dec4[:, kg].unsqueeze(2), [P, U, 2, C]), op=ALU.mult) \
                                .then_inc(M["ap_done"], 1)
                            wait(v, "kpair_done", g)
                            wait(v, "ktok_done", g - 1)
                            v.transpose(k_turn[:].rearrange("p u s c -> p (u s c)"),
                                        k_pair[:].rearrange("p u s c -> p (u s c)")).then_inc(M["kturn_done"], 1)
                        if solving and first:
                            wait(v, "ap_done", even + 1)
                            wait(v, "beta_copied", even + 1)
                            wait(v, "t_done", even - 1)
                            lanes_in(even, ps)
                        if solving and not first:
                            for i in range(11, 13):
                                solve_row(even, i)
                        if act_on(r):
                            wait(v, "delta_mm", r)
                            for h_ in range(2):
                                wait(v, "add_mm", *half(r - 1, h_))
                                d_unit = obank[:, 0, :].rearrange("p (u c) -> p u c", c=C)[:, units(h_)]
                                v.tensor_tensor(out=d_diag[:, units(h_)], in0=bcast(d_unit.unsqueeze(2), [P, HU, HP, C]),
                                                in1=bcast(head_mask[:].unsqueeze(1).unsqueeze(3), [P, HU, HP, C]),
                                                op=ALU.mult).then_inc(M["ddiag_done"], 1)
                        if act_on(n):
                            wait(v, "rstd_done", n)
                            wait(v, "h_done", n - 1)
                            v.tensor_scalar(xn[:], x4[:, k, :], mv[:, 0:1], rstd[:, 0:1], ALU.subtract, ALU.mult) \
                                .then_inc(M["xn_done"], 1)
                        if solving:
                            for i in (range(1, 4) if first else range(13, 14)):
                                solve_row(even, i)
                        base = c * DECAY if act_on(c) else None
                        if act_on(c):
                            wait(v, "z_done", c)
                            wait(v, "expz_done", c - 1)
                            v.tensor_tensor(out=z32[:], in0=small_z, in1=dtb[:], op=ALU.add) \
                                .then_inc(M["decay_steps"], 1)
                            v.wait_ge(M["decay_steps"], base + 1)
                            v.scalar_tensor_tensor(out=w32[:, 0:H], in0=z32[:, 0:H], scalar=-1.0, in1=z32[:, 0:H],
                                                   op0=ALU.mult, op1=ALU.min) \
                                .then_inc(M["decay_steps"], 1)
                            v.tensor_scalar(w32[:, H:], z32[:, H:], -1.0, None, ALU.mult) \
                                .then_inc(M["decay_steps"], 1)
                        if act_on(w):
                            wait(v, "st_done", w)
                            wait(v, "rl_done", e if act_on(e) else -1)
                            wait(v, "z_done", c if act_on(c) else -1)
                            wait_ring(v, SO, w - 4, kw)
                            v.tensor_copy(scT4[:, kw, :], small_st).then_inc(M["scT_done"], 1)
                        if act_on(e):
                            wait(v, "rl_done", e)
                            wait(v, "z_done", c if act_on(c) else -1)
                            wait(v, "expl_done", e - 1)
                            v.tensor_copy(logit[:], small_rl).then_inc(M["logit_done"], 1)
                            wait(v, "logit_done", e)
                            v.tensor_reduce(nmax[:], logit[:], AX.X, ALU.max, negate=True).then_inc(M["max_done"], 1)
                        if act_on(c):
                            wait(v, "expz_done", c)
                            wait(v, "beta_done", c - 1)
                        row, rows_end = ((4, 8) if first else (14, C)) if solving else (0, 0)
                        for j in range(EARLY_DECAY):
                            if act_on(c):
                                decay_step(base, j)
                            if row + j // 2 < rows_end:
                                solve_row(even, row + j // 2, j % 2 == 1)
                        if act_on(o):
                            wait(v, "y_done", o)
                            wait(v, "h2mul_done", o - 1)
                            v.tensor_tensor(out=xn2[:], in0=zbank[:, 128:128 + E], in1=mod[:, GA, :], op=ALU.mult) \
                                .then_inc(M["yga_done"], 1)
                            wait(v, "yga_done", o)
                            wait_ring(v, XR, o, ko)
                            wait_ring(v, XO, o - 2, (ko + 2) % 4)
                            v.tensor_tensor(out=x2_2[:, ko % 2, :], in0=xn2[:], in1=xr2[:, ko % 2, :], op=ALU.add) \
                                .then_inc(M["x2_done"], 1)
                            wait(v, "x2_done", o)
                            v.bn_stats(stats2[:], x2_2[:, ko % 2, :]).then_inc(M["stats2_done"], 1)
                            wait(v, "stats2_done", o)
                            wait(v, "xn2_done", o - 1)
                            v.tensor_copy(tick[:, 1:2], zero[:])
                            v.bn_aggr(mv2[:], stats2[:]).then_inc(M["mean2_done"], 1)
                        if act_on(r):
                            wait(v, "osq_done", r - 1)
                            wait(v, "og1_done", r - 1)
                            for h_ in range(2):
                                wait(v, "add_mm", *half(r, h_))
                                wait(v, "spair_done", *half(r - 1, h_))
                                v.tensor_tensor(out=os[:, units(h_)].rearrange("p u a c -> p u (a c)"),
                                                in0=held[:, units(h_)].rearrange("p u a c -> p u (a c)"),
                                                in1=banked(h_, OT, ST + 1), op=ALU.add).then_inc(M["sum_done"], 1)
                            for h_ in range(2):
                                wait(v, "spair_done", *half(r, h_))
                                wait(v, "sdiag_done", *half(r - 1, h_))
                                v.transpose(s_turn[:, units(h_)].rearrange("p u s c -> p (u s c)"),
                                            s_pair[:, units(h_)].rearrange("p u s c -> p (u s c)")) \
                                    .then_inc(M["sturn_done"], 1)
                            for h_ in range(2):
                                wait(v, "sturn_done", *half(r, h_))
                                wait(v, "read_mm", *half(r, h_))
                                src = s_turn[:, units(h_)].rearrange("p u s c -> p u (s c)").unsqueeze(2)
                                v.tensor_tensor(out=s_diag[:, units(h_)].rearrange("p u (a s) c -> p u a (s c)", s=2),
                                                in0=bcast(src, [P, HU, HP // 2, 2 * C]),
                                                in1=bcast(pair_mask[:].unsqueeze(1).unsqueeze(3), [P, HU, HP // 2, 2 * C]),
                                                op=ALU.mult).then_inc(M["sdiag_done"], 1)
                        if act_on(c):
                            wait(v, "gate_s", c)
                            wait(v, "og1_done", c - 8)
                            v.tensor_tensor(out=gate8[:, c % 8].rearrange("p g t -> p (g t)"), in0=vgbank[:, E:],
                                            in1=sig[:, 2, :], op=ALU.mult).then_inc(M["gate_done"], 1)
                            wait(v, "inv_done", c)
                            wait(v, "read_mm", c - 4, 2)
                            for m, name in ((1, "k_done"), (0, "q_done")):
                                v.scalar_tensor_tensor(
                                    out=mk4[:, kc_, :, (QF, KF)[m], :],
                                    in0=inv_norm[:, 2 * m:2 * m + 2, :].rearrange("p g (b i) -> p (g b) i", i=C),
                                    scalar=1e12,
                                    in1=qkbank[:, m * E:(m + 1) * E].rearrange("p (u i) -> p u i", i=C),
                                    op0=ALU.min, op1=ALU.mult).then_inc(M[name], 1)
                        row, rows_end = (8, 11) if solving and first else (0, 0)
                        for j in range(EARLY_DECAY, DECAY - 3):
                            if act_on(c):
                                decay_step(base, j)
                            i = j - EARLY_DECAY
                            if row + i // 2 < rows_end:
                                solve_row(even, row + i // 2, i % 2 == 1)
                        if solving and not first:
                            lanes_out(even, ps // 2)
                        if act_on(o):
                            wait(v, "rstd2_done", o)
                            wait(v, "h2mul_done", o - 1)
                            v.tensor_scalar(xn2[:], x2_2[:, ko % 2, :], mv2[:, 0:1], rstd2[:, 0:1], ALU.subtract, ALU.mult) \
                                .then_inc(M["xn2_done"], 1)
                        if act_on(e):
                            wait(v, "expl_done", e)
                            v.reciprocal(esum[:, 1:2], esum[:, 0:1]).then_inc(M["esum_done"], 1)
                            wait(v, "esum_done", e)
                            wait(v, "st_done", e - 1)
                            v.tensor_scalar(sc[:], expl[:], esum[:, 1:2], None, ALU.mult).then_inc(M["sc_done"], 1)
                    run(v, step)

                @block.tensor
                def _(pe):
                    pe.wait_ge(K["c_pool"], SETUP_POOL)
                    pe.wait_ge(K["c_in"], LOADS * 16)
                    pe.wait_ge(K["c_vec"], SILU_VEC)
                    for kc in range(KC):
                        pe.transpose(tbank[:, kc * P:kc * P + B], x4[0:B, 3, kc * P:(kc + 1) * P], ident[0:B, 0:B])
                    for kc in range(KC):
                        ins = pe.transpose(tbank[:, (2 + kc) * P:(2 + kc) * P + NE], xn[0:NE, kc * P:(kc + 1) * P],
                                           ident[0:NE, 0:NE])
                    ins.then_inc(K["c_pe"], 1)
                    pe.wait_ge(K["c_vec"], COND_VEC)
                    for m in range(3):
                        for kc in range(KC):
                            ins = pe.matmul([zbank, qkbank, vgbank][m][:, :], cT[:, kc, :],
                                            wm[:, kc, m * 512:(m + 1) * 512], start=(kc == 0), stop=(kc == KC - 1))
                    ins.then_inc(K["c_pe"], 2)
                    pe.wait_ge(K["c_vec"], SETUP_VEC - 1)
                    for kc in range(KC):
                        ins = pe.transpose(tbank[:, kc * P:(kc + 1) * P], mod[:, GB, kc * P:(kc + 1) * P], ident[:])
                    ins.then_inc(K["c_pe"], 1)
                    pe.wait_ge(K["c_vec"], SETUP_VEC)

                    o_units = obank[:].rearrange("p a (u c) -> p (a u) c", c=C)

                    def twice(h_, j):
                        return rec_block[h_][:, j:HU + 1:HU - j, :]

                    def repeated(ap):
                        return bcast(ap.unsqueeze(1), [P, WIDE // (3 * C), 3 * C])

                    def window(ap, u, end=None):
                        per = ap.shape[-1]
                        stop = u + WIDE // per
                        return ap[:, u:stop if end is None else min(stop, end)]

                    def step(n, k):
                        r, kr = n - LAG_REC, slot(k, LAG_REC)
                        o, ko = n - LAG_OUT, slot(k, LAG_OUT)
                        g, kg = n - LAG_GRAM, slot(k, LAG_GRAM)
                        c, kc_ = n - LAG_PROJ, slot(k, LAG_PROJ)
                        e, ke = n - LAG_ROUTE, slot(k, LAG_ROUTE)
                        w = n - LAG_SCORE
                        if act_on(r):
                            wait(pe, "gq_done", r)
                            wait(pe, "gi_done", r)
                            for h_ in range(2):
                                wait(pe, "sum_done", *half(r - 1, h_))
                                wait(pe, "sdiag_done", *half(r - 1, h_))
                                for j in range(HU):
                                    u = h_ * HU + j
                                    ins = pe.matmul(twice(h_, j), s_diag[:, u].rearrange("p g i -> p (g i)"),
                                                    repeated(mk4[:, kr, u, 0:3, :].rearrange("p a i -> p (a i)")),
                                                    start=True, stop=True)
                                ins.then_inc(M["read_mm"], 1)
                        if act_on(g):
                            wait(pe, "alpha_done", g)
                            wait(pe, "beta_done", g)
                            wait(pe, "lnss_done", g)
                            for a in range(2):
                                for hg in range(HG):
                                    src = decay_rep[:, a, hg * HP:(hg + 1) * HP, :].rearrange("p h r -> p (h r)")
                                    ins = pe.transpose(tbank[:, (2 * a + hg) * P:(2 * a + hg + 1) * P], src, ident[:])
                            ins.then_inc(M["ab_done"], 1)
                        if act_on(g):
                            wait(pe, "kdiag_done", g)
                            wait(pe, "q_done", g)
                            wait(pe, "ap_done", g - 1)
                            keys = mk4[:, kg, :, KF:QF + 1, :].rearrange("p u a i -> p u (a i)")
                            for u in range(U):
                                ins = pe.matmul(window(gram, u, U), k_diag2[:, kg % 2, u].rearrange("p g i -> p (g i)"),
                                                window(keys, u, U), start=True, stop=True)
                            ins.then_inc(M["gram_done"], 1)
                        if act_on(c):
                            wait(pe, "h_done", c)
                            wait(pe, "beta_copied", c - 1)
                            for kc in range(KC):
                                ins = pe.transpose(tbank[:, kc * P:(kc + 1) * P], h[:, kc * P:(kc + 1) * P], ident[:])
                            ins.then_inc(M["xt_done"], 1)
                        if act_on(r):
                            wait(pe, "tdiag_done", r)
                            wait(pe, "ddiag_done", r - 1, 2)
                            wait(pe, "rhs_done", r, 2)
                            for u in range(U):
                                ins = pe.matmul(window(o_units, u), t_diag2[:, kr % 2, u].rearrange("p g i -> p (g i)"),
                                                window(rhs, u), start=True, stop=True)
                            ins.then_inc(M["delta_mm"], 1)
                        if act_on(o):
                            wait(pe, "osq_done", o)
                            wait(pe, "yga_done", o - 1)
                            pe.matmul(zbank[:, 128:128 + E], head_ones[:], o_sq[:], start=True, stop=True) \
                                .then_inc(M["ms_done"], 1)
                        if act_on(e):
                            wait(pe, "h2_done", e)
                            if act_on(c):
                                wait(pe, "hT_done", c)
                            elif act_on(g):
                                wait(pe, "beta_copied", g)
                            for kc in range(KC):
                                ins = pe.transpose(tbank[:, kc * P:(kc + 1) * P], h2_2[:, ke % 2, kc * P:(kc + 1) * P],
                                                   ident[:])
                            ins.then_inc(M["h2t_mm"], 1)
                        if act_on(c):
                            wait(pe, "hT_done", c)
                            wait(pe, "q_done", c - 1)
                            wait(pe, "gate_done", c - 1)
                            for m, name in enumerate("qkvg"):
                                bank = qkbank if m < 2 else vgbank
                                for hg in range(HG):
                                    for kc in range(KC):
                                        col = (m % 2) * E + hg * P
                                        ins = pe.matmul(bank[:, col:col + P], w_in[name][:, kc, hg * P:(hg + 1) * P],
                                                        hT2[:, kc_ % 2, kc, :], start=(kc == 0), stop=(kc == KC - 1))
                            ins.then_inc(M["proj_done"], 1)
                        wait(pe, "ddiag_done", r if act_on(r) else -1, 2)
                        if act_on(w):
                            wait(pe, "sc_done", w)
                            pe.transpose(small_st, sc[:], ident[:]).then_inc(M["st_done"], 1)
                        if act_on(e):
                            wait(pe, "h2T_done", e)
                            wait(pe, "expl_done", e - 1)
                            for kc in range(KC):
                                ins = pe.matmul(small_rl, h2T[:, kc, :], router_t[:, kc, :],
                                                start=(kc == 0), stop=(kc == KC - 1))
                            ins.then_inc(M["rl_done"], 1)
                        if act_on(c):
                            for kc in range(KC):
                                ins = pe.matmul(small_z, hT2[:, kc_ % 2, kc, :], w_ab[:, kc, :],
                                                start=(kc == 0), stop=(kc == KC - 1))
                            ins.then_inc(M["z_done"], 1)
                        if act_on(o):
                            wait(pe, "og_done", o)
                            wait(pe, "lnms_done", o)
                            for hg in range(HG):
                                ins = pe.matmul(zbank[:, 128:128 + E], og[:, ko % 2, hg, :], w_out[:, hg, :],
                                                start=(hg == 0), stop=(hg == HG - 1))
                            ins.then_inc(M["y_done"], 1)
                        if act_on(r):
                            wait(pe, "dk_done", r)
                            wait(pe, "ap_done", r)
                            wait(pe, "gks_done", r, 2)
                            for h_ in range(2):
                                wait(pe, "held_done", *half(r, h_))
                                wait(pe, "ddiag_done", *half(r, h_))
                                for j in range(HU):
                                    u = h_ * HU + j
                                    moving = ap4[:, kr].rearrange("p u a i -> p (u a i)")[:, (3 * u + 1) * C:(3 * u + 4) * C]
                                    ins = pe.matmul(twice(h_, j), d_diag[:, u].rearrange("p g i -> p (g i)"),
                                                    repeated(moving), start=True, stop=True)
                                ins.then_inc(M["add_mm"], 1)
                        if act_on(c):
                            wait(pe, "sq_done", c)
                            pe.matmul(tbank[:, :], head_ones[:], sqk[:].rearrange("p m t -> p (m t)"),
                                      start=True, stop=True).then_inc(M["ss_done"], 1)
                    run(pe, step)


        PAIRS = NE * B
        NT = 3
        TR = -(-CAP // NT)
        width = [min(TR, CAP - t * TR) for t in range(NT)]

        experts = ctx.enter_context(ExitStack())

        def eb(name, shape, dt=F32):
            return experts.enter_context(nc.sbuf_tensor(name, shape, dt))

        score = eb("score", [PAIRS, T])
        best = eb("best", [PAIRS, ROUNDS * 8])
        place = eb("place", [PAIRS, ROUNDS * 8])
        best8 = eb("best8", [PAIRS, 8])
        place8 = eb("place8", [PAIRS, 8], U32)
        batch_hot = eb("batch_hot", [PAIRS, B])
        batch_row = eb("batch_row", [P, B])
        batch_int = eb("batch_int", [P, B], U32)
        batch_base = eb("batch_base", [PAIRS, 1])
        gate_col = eb("gate_col", [TR, NT, PAIRS])
        row_col = eb("row_col", [TR, NT, PAIRS + 2], U32)
        b1_rows = eb("b1_rows", [NE * HID // P, P])
        b2_rows = eb("b2_rows", [NE * KC, P])
        b1_col = eb("b1_col", [P, NE * HID // P])
        b2_col = eb("b2_col", [P, NE * KC])
        w1_2 = eb("w1_2", [P, 2, KC, HID])
        w2_2 = eb("w2_2", [P, 2, HID // P, E])
        b1_now = eb("b1_now", [P, 2, HID // P])
        carry = eb("carry", [P, 128])
        from_row = eb("from_row", [TR, 2, NT], U32)
        to_row = eb("to_row", [TR, 2, NT], U32)
        tok2 = eb("tok2", [TR, 2, NT, E])
        tokT2 = eb("tokT2", [P, 2, KC, CAP])
        act2 = eb("act2", [P, 2, HID // P, CAP])
        yT2 = eb("yT2", [P, 2, KC, CAP])
        ys2 = eb("ys2", [TR, 2, NT, E])

        N = sems("scores_in biases_in round_max round_place round_next round_kept best_ready place_ready hot_steps "
                 "lists_turned lists_ready rows_zeroed biases_turned biases_ready b1_picked from_picked to_picked tokT_mm "
                 "tokT_ready up_mm gelu_done down_mm yT_ready back_mm ys_ready")
        W1 = [sem(f"w1_loaded{i}") for i in range(2)]
        W2 = [sem(f"w2_loaded{i}") for i in range(2)]
        GATHERED = [sem(f"gathered{i}") for i in range(2)]
        ADDED = [sem(f"added{i}") for i in range(2)]
        HC = HID // P

        with nc.Block() as block:
            place_of = [-1]

            def settle(eng):
                place_of[0] += 1
                col = slice(place_of[0], place_of[0] + 1)
                if eng is nc.gpsimd:
                    eng.tensor_tensor(out=carry[:, col], in0=zero[:], in1=zero[:], op=ALU.add)
                elif eng is nc.scalar:
                    eng.activation(carry[:, col], zero[:], ACT.Copy)
                else:
                    eng.tensor_copy(carry[:, col], zero[:])

            def wait_added(eng, q, j):
                if isinstance(q, int) and q < 2:
                    return
                eng.wait_ge(ADDED[j], (q - j) * (8 * NT))

            def back(t):
                return [vgbank[0:width[0], 0:E], vgbank[0:width[1], E:2 * E], tbank[0:width[2], 0:E]][t]

            def chain_bank(kc):
                return [rec_banks[:, 0, :], obank[:].rearrange("p a c -> p (a c)")][kc][:, 0:CAP]

            def side_bank(j):
                return [gram[:].rearrange("p u c -> p (u c)"), rec_banks[:, 1, :]][j]

            def up_bank(m):
                return side_bank(m % 2)[:, 0:CAP]

            def each_unit(eng, unit):
                unit(0, 0, 0, 0, 0, finish=False)
                unit(1, 1, 0, 0, 1)
                with eng.Fori(1, B // 2) as b2_:
                    for j in range(2):
                        unit(b2_ * 2 + j, b2_ * 2 + j, 0, 0, j)
                with eng.Fori(0, B // 2) as b2_:
                    for j in range(2):
                        unit(b2_ * 2 + (B + j), b2_ * 2 + j, 1, 1, j)
                with eng.Fori(1, NE // 2) as e2:
                    for par in range(2):
                        with eng.Fori(0, B // 2) as b2_:
                            for j in range(2):
                                unit(e2 * (2 * B) + b2_ * 2 + (par * B + j), b2_ * 2 + j, e2 * 2 + par, par, j)

            def load_weights(sp, e, par):
                sp.dma_start(w1_2[:, par], w1[e].rearrange("(k p) n -> p k n", p=P)).then_inc(W1[par], 16)
                sp.dma_start(w2_2[:, par], w2[e].rearrange("(j p) n -> p j n", p=P)).then_inc(W2[par], 16)

            @block.sync
            def _(sp):
                sp.dma_start(score[:], score_dram.rearrange("e b t -> (e b) t")).then_inc(N["scores_in"], 16)
                sp.dma_start(b1_rows[:], b1.rearrange("e (j p) -> (e j) p", p=P)).then_inc(N["biases_in"], 16)
                sp.dma_start(b2_rows[:], b2.rearrange("e (k p) -> (e k) p", p=P)).then_inc(N["biases_in"], 16)
                for par in range(2):
                    load_weights(sp, par, par)
                with sp.Fori(1, NE // 2) as e2:
                    for par in range(2):
                        sp.wait_ge(N["down_mm"], (e2 * 2 + par - 1) * B)
                        load_weights(sp, e2 * 2 + par, par)

            @block.vector
            def _(v):
                steps = [0]

                def link(ins):
                    steps[0] += 1
                    ins.then_inc(N["hot_steps"], 1)
                    v.wait_ge(N["hot_steps"], steps[0])

                link(v.memset(row_col[:], 0))
                link(v.tensor_reduce(batch_hot[:], ident[0:PAIRS, 0:PAIRS].rearrange("p (e b) -> p b e", b=B),
                                     AX.X, ALU.add))
                v.wait_ge(N["rows_zeroed"], 1)
                link(v.tensor_copy(batch_row[:], batch_int[:]))
                link(v.tensor_tensor(out=batch_hot[:], in0=batch_hot[:], in1=batch_row[0:PAIRS, :], op=ALU.mult))
                link(v.tensor_reduce(batch_base[:], batch_hot[:], AX.X, ALU.add))
                v.wait_ge(N["scores_in"], 16)
                def best_eight(r):
                    if not isinstance(r, int):
                        v.wait_ge(N["round_next"], r)
                        v.wait_ge(N["round_kept"], r * 2)
                        settle(v)
                    v.max(best8[:], score[:]).then_inc(N["round_max"], 1)
                    v.wait_ge(N["round_max"], r + 1)
                    v.tensor_scalar(best[:, bass.ds(r * 8, 8)], best8[:], 1.0, None, ALU.mult) \
                        .then_inc(N["round_kept"], 1)
                    v.max_index(place8[:], best8[:], score[:]).then_inc(N["round_place"], 1)
                    v.wait_ge(N["round_place"], r + 1)
                    v.tensor_scalar(place[:, bass.ds(r * 8, 8)], place8[:], batch_base[:, 0:1], None, ALU.add) \
                        .then_inc(N["round_kept"], 1)
                    v.match_replace(score[:], best8[:], score[:], -1.0).then_inc(N["round_next"], 1)

                best_eight(0)
                with v.Fori(1, ROUNDS) as r:
                    best_eight(r)
                v.wait_ge(N["lists_turned"], 1)
                for src, dst in ((0, gate_col), (1, row_col)):
                    for t in range(NT):
                        w = width[t]
                        v.tensor_copy(dst[0:w, t, 0:PAIRS], side_bank(src)[0:w, t * PAIRS:(t + 1) * PAIRS]) \
                            .then_inc(N["lists_ready"], 1)
                v.wait_ge(N["biases_turned"], 1)
                v.tensor_copy(b1_col[:], rec_banks[:, 0, :][:, 0:NE * HC]) \
                    .then_inc(N["biases_ready"], 1)
                v.tensor_copy(b2_col[:], rec_banks[:, 0, :][:, P:P + NE * KC]) \
                    .then_inc(N["biases_ready"], 1)

                def unit(q, b, e, par, j, turn_next=True, finish=True, start=True):
                    if turn_next:
                        v.wait_ge(N["tokT_mm"], q + 2)
                        for kc in range(KC):
                            v.tensor_copy(tokT2[:, (j + 1) % 2, kc, :], [zbank, qkbank][kc][:, 0:CAP]) \
                                .then_inc(N["tokT_ready"], 1)
                    if finish:
                        v.wait_ge(N["back_mm"], q)
                        wait_added(v, q - 1, (j + 1) % 2)
                        for t in range(NT):
                            col = gate_col[0:width[t], t, bass.ds(q - 1, 1)]
                            v.tensor_scalar(ys2[0:width[t], (j + 1) % 2, t, :], back(t), col, None, ALU.mult) \
                                .then_inc(N["ys_ready"], 1)
                    if start:
                        v.wait_ge(N["down_mm"], q + 1)
                        for kc in range(KC):
                            v.tensor_scalar(yT2[:, j, kc, :], chain_bank(kc), b2_col[:, bass.ds(e * KC + kc, 1)],
                                            gb_col[:, kc, bass.ds(b, 1)], ALU.add, ALU.mult) \
                                .then_inc(N["yT_ready"], 1)

                v.wait_ge(N["tokT_mm"], 1)
                for kc in range(KC):
                    v.tensor_copy(tokT2[:, 0, kc, :], [zbank, qkbank][kc][:, 0:CAP]).then_inc(N["tokT_ready"], 1)
                each_unit(v, unit)
                unit(PAIRS, 0, 0, 0, 0, turn_next=False, start=False)

            @block.scalar
            def _(act):
                act.wait_ge(N["biases_ready"], 2)

                def unit(q, b, e, par, j, finish=True):
                    act_free = q - 1
                    if not isinstance(q, int) or q >= 2:
                        act.wait_ge(N["down_mm"], act_free)
                        settle(act)
                    act.activation(b1_now[:, j, :], b1_col[:, bass.ds(e * HC, HC)], ACT.Copy) \
                        .then_inc(N["b1_picked"], 1)
                    act.wait_ge(N["b1_picked"], q + 1)
                    for m in range(HC):
                        act.wait_ge(N["up_mm"], q * HC + (m + 1))
                        act.activation(act2[:, j, m, :], up_bank(m), ACT.Gelu,
                                       bias=b1_now[:, j, m:m + 1]).then_inc(N["gelu_done"], 1)
                each_unit(act, unit)

            @block.tensor
            def _(pe):
                pe.wait_ge(N["biases_in"], 32)
                flat = rec_banks[:, 0, :]
                pe.transpose(flat[:, 0:NE * HC], b1_rows[:], ident[0:NE * HC, 0:NE * HC])
                pe.transpose(flat[:, P:P + NE * KC], b2_rows[:], ident[0:NE * KC, 0:NE * KC]) \
                    .then_inc(N["biases_turned"], 1)
                pe.wait_ge(N["round_kept"], ROUNDS * 2)
                for src, rows_ in ((0, best), (1, place)):
                    for t in range(NT):
                        ins = pe.transpose(side_bank(src)[0:width[t], t * PAIRS:(t + 1) * PAIRS],
                                           rows_[:, t * TR:t * TR + width[t]], ident[0:PAIRS, 0:PAIRS])
                ins.then_inc(N["lists_turned"], 1)

                def turn(q, j):
                    pe.wait_ge(GATHERED[j % 2], (q - j % 2) * (8 * NT) + 16 * NT)
                    if not isinstance(q, int) or q > 0:
                        pe.wait_ge(N["tokT_ready"], q * KC)
                    for kc in range(KC):
                        for t in range(NT):
                            ins = pe.transpose([zbank, qkbank][kc][:, t * TR:t * TR + width[t]],
                                               tok2[0:width[t], j, t, kc * P:(kc + 1) * P],
                                               ident[0:width[t], 0:width[t]])
                    ins.then_inc(N["tokT_mm"], 1)

                def back_rows(q, j):
                    pe.wait_ge(N["yT_ready"], q * KC + KC)
                    if not isinstance(q, int) or q > 0:
                        pe.wait_ge(N["ys_ready"], q * NT)
                    for t in range(NT):
                        for kc in range(KC):
                            ins = pe.transpose(back(t)[:, kc * P:(kc + 1) * P],
                                               yT2[:, j, kc, t * TR:t * TR + width[t]], ident[:])
                    ins.then_inc(N["back_mm"], 1)

                def unit(q, b, e, par, j, finish=True):
                    if j == 0:
                        pe.wait_ge(W1[par], (e - par) * 8 + 16)
                        pe.wait_ge(W2[par], (e - par) * 8 + 16)
                    pe.wait_ge(N["tokT_ready"], q * KC + KC)
                    for m in range(HC):
                        if m < 2 and isinstance(q, int) and q == 0:
                            pe.wait_ge(N["lists_ready"], 2 * NT)
                        else:
                            pe.wait_ge(N["gelu_done"], q * HC + (m - 1))
                        for kc in range(KC):
                            ins = pe.matmul(up_bank(m), w1_2[:, par, kc, m * P:(m + 1) * P], tokT2[:, j, kc, :],
                                            start=(kc == 0), stop=(kc == KC - 1))
                        ins.then_inc(N["up_mm"], 1)
                    turn(q + 1, (j + 1) % 2)
                    if finish:
                        back_rows(q - 1, (j + 1) % 2)
                    if not isinstance(q, int) or q > 0:
                        pe.wait_ge(N["yT_ready"], q * KC)
                    else:
                        pe.wait_ge(N["biases_ready"], 2)
                    for kc in range(KC):
                        for m in range(HC):
                            if kc == 0:
                                pe.wait_ge(N["gelu_done"], q * HC + (m + 1))
                            ins = pe.matmul(chain_bank(kc), w2_2[:, par, m, kc * P:(kc + 1) * P], act2[:, j, m, :],
                                            start=(m == 0), stop=(m == HC - 1))
                    ins.then_inc(N["down_mm"], 1)

                turn(0, 0)
                each_unit(pe, unit)
                back_rows(PAIRS - 1, 1)

            @block.gpsimd
            def _(pool):
                pool.iota(batch_int[:], pattern=[[T, B]], base=0, channel_multiplier=0).then_inc(N["rows_zeroed"], 1)
                pool.wait_ge(N["lists_ready"], 2 * NT)

                def gather(q, j):
                    if not isinstance(q, int) or q >= 2:
                        pool.wait_ge(N["tokT_mm"], q - 1)
                    settle(pool)
                    pool.tensor_copy(from_row[:, j, :], row_col[:, :, bass.ds(q, 1)].rearrange("p t o -> p (t o)")) \
                        .then_inc(N["from_picked"], 1)
                    pool.wait_ge(N["from_picked"], q + 1)
                    settle(pool)
                    for t in range(NT):
                        pool.indirect_dma_start(tok2[0:width[t], j, t, :], None, h2_dram,
                                                bass.IndirectOffsetOnAxis(ap=from_row[0:width[t], j, t:t + 1], axis=0)) \
                            .then_inc(GATHERED[j], 16)

                def scatter(q, j):
                    wait_added(pool, q, j)
                    settle(pool)
                    pool.tensor_copy(to_row[:, j, :], row_col[:, :, bass.ds(q, 1)].rearrange("p t o -> p (t o)")) \
                        .then_inc(N["to_picked"], 1)
                    pool.wait_ge(N["to_picked"], q + 1)
                    pool.wait_ge(N["ys_ready"], q * NT + NT)
                    if not isinstance(q, int) or q > 0:
                        other = (j + 1) % 2
                        pool.wait_ge(ADDED[other], (q - 1 - other) * (8 * NT) + 16 * NT)
                    settle(pool)
                    for t in range(NT):
                        pool.indirect_dma_start(out_rows, bass.IndirectOffsetOnAxis(ap=to_row[0:width[t], j, t:t + 1], axis=0),
                                                ys2[0:width[t], j, t, :], None, compute_op=ALU.add) \
                            .then_inc(ADDED[j], 16)

                out_rows = out.rearrange("b t e -> (b t) e")

                gather(0, 0)
                gather(1, 1)

                def unit(q, b, e, par, j, finish=True):
                    gather(q + 2, j)
                    scatter(q, j)
                each_unit(pool, unit)
                for j in range(2):
                    pool.wait_ge(ADDED[j], PAIRS * 8 * NT)
                    pool.wait_ge(GATHERED[j], (PAIRS + 2) * 8 * NT)


_INS = ["L0_attn_x", "L0_attn_Wq", "L0_attn_Wk", "L0_attn_Wv", "L0_attn_Walpha", "L0_attn_Wbeta", "L0_attn_A_log",
        "L0_attn_dt_bias", "L0_attn_Wgate", "L0_attn_Wout", "L0_attn_rms_w", "L0_ffn_router_w", "L0_ffn_w1",
        "L0_ffn_b1", "L0_ffn_w2", "L0_ffn_b2", "L0_c", "L0_wmod"]
_OUTS = [((B, T, E), "float32")]


def kernel(**inputs):
    import numpy as _np
    import concourse.bacc as _bacc
    from concourse import mybir as _mybir
    from concourse.bass_utils import run_bass_kernel_spmd as _run

    nc = _bacc.Bacc("TRN2", target_bir_lowering=False, num_devices=1)
    arrays, args = {}, []
    for name in _INS:
        a = _np.ascontiguousarray(inputs[name])
        arrays[f"in_{name}_dram"] = a
        args.append(nc.dram_tensor(f"in_{name}_dram", a.shape, _mybir.dt.from_np(a.dtype), kind="ExternalInput").ap())
    for i, (shape, dtype) in enumerate(_OUTS):
        dt = _mybir.dt.from_np(_np.dtype(dtype))
        args.append(nc.dram_tensor(f"out_{i}_dram", shape, dt, kind="ExternalOutput").ap())
    program(nc, *args)
    r = _run(nc, [arrays], core_ids=[0])
    got = tuple(r.results[0][f"out_{i}_dram"] for i in range(len(_OUTS)))
    return got[0]
```

```python
from contextlib import ExitStack

import concourse.bass as bass
from concourse import mybir

F32 = mybir.dt.float32
U32 = mybir.dt.uint32
F32R = mybir.dt.float32r
ALU = mybir.AluOpType
ACT = mybir.ActivationFunctionType
AX = mybir.AxisListType

P = 128
B, T, E, H, D = 8, 1024, 256, 16, 16
C = 16
NCH = T // C
HG = H * D // P
HP = H // HG
U = HG * B
KC = E // P
NE = 8
HID = 1024
CAP = T * 2 // NE + 1
COLS = CAP + CAP % 2
ROUNDS = -(-CAP // 8)
UNROLL = 4
WIDE = 96
PAD = WIDE // C - 1
HU = U // 2

LAG_PROJ, LAG_GRAM, LAG_REC, LAG_OUT, LAG_ROUTE, LAG_SCORE = 1, 2, 5, 6, 7, 8
STEPS = NCH + LAG_SCORE
HEAD = 12

LOG1P = [1.0 / k for k in range(13, 1, -2)]


def bcast(ap, shape):
    return ap.to_broadcast(shape)


def program(nc, x, wq, wk, wv, walpha, wbeta, a_log, dt_bias, wgate, wout, rms_w,
            router_w, w1, b1, w2, b2, cond, wmod, out, debug=None):
    with ExitStack() as ctx:
        def sb(name, shape, dt=F32):
            return ctx.enter_context(nc.sbuf_tensor(name, shape, dt))

        def sem(name):
            return ctx.enter_context(nc.semaphore(name))

        def sems(names):
            return {n: sem(n) for n in names.split()}

        h2_dram = nc.dram_tensor("h2_rows", (B * T, E), F32).ap()
        score_dram = nc.dram_tensor("scores", (NE, B, T), F32).ap()

        ident = sb("ident", [P, P])
        head_mask = sb("head_mask", [P, HP])
        ident_rep = sb("ident_rep", [P, U, C])
        head_ones = sb("head_ones", [P, P])
        eps_ln = sb("eps_ln", [P, 1])
        eps_rms = sb("eps_rms", [P, 1])
        one = sb("one", [P, 1])
        zero = sb("zero", [P, 1])
        mod = sb("mod", [P, 6, E])
        SA, CA, GA, SB_, CB, GB = range(6)
        gb_col = sb("gb_col", [P, KC, B])
        neg_rate = sb("neg_rate", [P, H])
        dtb = sb("dtb", [P, 2 * H])
        w_in = {n: sb(f"w_{n}", [P, KC, E]) for n in ("q", "k", "v", "g")}
        w_ab = sb("w_ab", [P, KC, 2 * H])
        w_out = sb("w_out", [P, HG, E])
        rms_col = sb("rms_col", [P, 1])
        router_t = sb("router_t", [P, KC, NE])

        banks = [ctx.enter_context(nc.psum_tensor(f"bank{i}", [P, 512], F32)) for i in range(4)]
        gram = ctx.enter_context(nc.psum_tensor("gram", [P, U, 2 * C], F32))
        rec_banks = ctx.enter_context(nc.psum_tensor("rec_banks", [P, 2, 512], F32))
        obank = ctx.enter_context(nc.psum_tensor("obank", [P, 2, E], F32))
        zbank, qkbank, vgbank, tbank = banks

        K = sems("c_pool c_vec c_act c_pe c_in")

        x_v = x.rearrange("b (n i) e -> n b i e", i=C)
        out_v = out.rearrange("b (n i) e -> n b i e", i=C)
        h2_v = h2_dram.rearrange("(b n i) e -> n b i e", b=B, i=C)
        score_v = score_dram.rearrange("e b (n i) -> n e b i", i=C)

        def rows(ap):
            return ap

        with ExitStack() as mixer:
            def mb(name, shape, dt=F32):
                return mixer.enter_context(nc.sbuf_tensor(name, shape, dt))

            x4 = mb("x4", [P, 4, E])
            stats = mb("stats", [P, 6])
            mv = mb("mv", [P, 2])
            rstd = mb("rstd", [P, 4])
            xn = mb("xn", [P, E])
            h = mb("h", [P, E])
            hT2 = mb("hT2", [P, 2, KC, P])
            sqk = mb("sqk", [P, 4, P])
            inv_norm = mb("inv_norm", [P, 4, P])
            mk4 = mb("mk4", [P, 4, U, 5, C])
            GK, GI, GQ, KF, QF = range(5)
            head_side = mb("head_side", [P, 2])
            pair_mask = mb("pair_mask", [P, HP // 2])
            k_pair = mb("k_pair", [P, U, 2, C])
            k_turn = mb("k_turn", [P, U, 2, C])
            k_tok = mb("k_tok", [P, U, C])
            k_diag2 = mb("k_diag2", [P, 2, U, HP, C])
            v4 = mb("v4", [P, 4, U, C])
            gate8 = mb("gate8", [P, 8, HG, P])
            sig = mb("sig", [P, 3, E])
            z32 = mb("z32", [P, 2 * H])
            w32 = mb("w32", [P, 2 * H])
            u32 = mb("u32", [P, 2 * H])
            den = mb("den", [P, 2 * H])
            rec = mb("rec", [P, 2 * H])
            ser = mb("ser", [P, 6, H])
            decay_rep = mb("decay_rep", [P, 2, H, C])
            alpha0 = mb("alpha0", [P, U, C])
            start0 = mb("start0", [P, U, C])
            beta4 = mb("beta4", [P, 4, U, C])
            dec4 = mb("dec4", [P, 4, U, C])
            gam4 = mb("gam4", [P, 4, U, C])
            ap4 = mb("ap4", [P, 4, U, 3, C])
            low = mb("low", [P, 2, 2 * P * 2])
            solved = mb("solved", [P, C, 2, C])
            solved_b = mb("solved_b", [P, C, 2, C])
            prod = mb("prod", [P, 2 * C * C])
            t2 = mb("t2", [P, 2, 2, U, C])
            t_diag2 = mb("t_diag2", [P, 2, U, HP, C])
            s_pair = mb("s_pair", [P, U, 2, C])
            s_turn = mb("s_turn", [P, U, 2, C])
            s_diag = mb("s_diag", [P, U, HP, C])
            held = mb("held", [P, U, 2, C])
            os = mb("os", [P, U, 2, C])
            rhs_f = mb("rhs_f", [P, U, C])
            r_pair = mb("r_pair", [P, U, 2, C])
            r_turn = mb("r_turn", [P, U, 2, C])
            rhs = mb("rhs", [P, U + PAD, C])
            d_diag = mb("d_diag", [P, U, HP, C])
            o_sq = mb("o_sq", [P, E])
            o_r = mb("o_r", [P, 2, E])
            og = mb("og", [P, 2, HG, P])
            xr2 = mb("xr2", [P, 2, E])
            x2_2 = mb("x2_2", [P, 2, E])
            xn2 = mb("xn2", [P, E])
            h2_2 = mb("h2_2", [P, 2, E])
            stats2 = mb("stats2", [P, 6])
            mv2 = mb("mv2", [P, 2])
            rstd2 = mb("rstd2", [P, 4])
            tick = mb("tick", [P, 2])
            h2T = mb("h2T", [P, KC, P])
            logit = mb("logit", [P, NE])
            nmax = mb("nmax", [P, 1])
            esum = mb("esum", [P, 2])
            expl = mb("expl", [P, NE])
            sc = mb("sc", [P, NE])
            scT4 = mb("scT4", [NE, 4, P])

            wm = k_diag2[:, 0:2].rearrange("p r u g c -> p (r u g c)")[:, 0:KC * 6 * E] \
                .rearrange("p (k n) -> p k n", k=KC)
            cT = sqk[:, 0:KC, :]

            XS = [sem(f"x_loaded{i}") for i in range(4)]
            XR = [sem(f"residual_loaded{i}") for i in range(4)]
            XO = [sem(f"x2_stored{i}") for i in range(4)]
            HO = [sem(f"h2_stored{i}") for i in range(4)]
            SO = [sem(f"scores_stored{i}") for i in range(4)]
            M = sems("shift neg_shift shift2 neg_shift2 stats_done mean_done ln_rstd rstd_done xn_done hmul_done h_done xt_done hT_done "
                     "proj_done z_done sq_done vcopy_done gate_e gate_l gate_s gate_done ss_done lnss_done "
                     "inv_done k_done q_done decay_steps expz_done alpha_done beta_done ab_done "
                     "alpha0_done start0_done beta_copied dec_done gam_done gq_done gi_done kdiag_done "
                     "kpair_done kturn_done ktok_done dk_done gram_done ap_done lanes_steps t_done tdiag_done "
                     "read_mm rhsf_done rpair_done rturn_done rhs_done delta_mm ddiag_done "
                     "add_mm held_done sum_done spair_done sturn_done sdiag_done sdiag2_done osq_done ms_done lnms_done rms_done "
                     "og1_done og_done y_done yga_done x2_done stats2_done mean2_done ln_rstd2 "
                     "rstd2_done xn2_done h2mul_done h2_done h2t_mm h2T_done rl_done logit_done "
                     "max_done expl_done esum_done sc_done st_done scT_done")

            def act_on(c):
                return not isinstance(c, int) or 0 <= c < NCH

            def wait(eng, name, c, per=1, plus=None):
                if isinstance(c, int) and c < 0:
                    return
                eng.wait_ge(M[name], c * per + (per if plus is None else plus))

            def wait_ring(eng, ring, c, slot):
                if isinstance(c, int) and c < 0:
                    return
                eng.wait_ge(ring[slot], (c - slot) * 4 + 16)

            def run(eng, step):
                for n in range(HEAD):
                    step(n, n % UNROLL)
                with eng.Fori(HEAD // UNROLL, NCH // UNROLL) as m:
                    for k in range(UNROLL):
                        step(m * UNROLL + k, k)
                for n in range(NCH, STEPS):
                    step(n, n % UNROLL)

            def half(c, h):
                return c, 2, h + 1

            def units(h):
                return slice(h * HU, (h + 1) * HU)

            KST, ST, OT = range(3)
            rec_block = [rec_banks[:, h, 0:(HU + 1) * 3 * C].rearrange("p (u n) -> p u n", n=3 * C) for h in range(2)]

            def banked(h, part, end=None):
                return rec_block[h][:, 0:HU, part * C:(part + 1 if end is None else end) * C]

            def state_diag(eng, h):
                src = s_turn[:, units(h)].rearrange("p u s c -> p u (s c)").unsqueeze(2)
                return eng.tensor_tensor(out=s_diag[:, units(h)].rearrange("p u (a s) c -> p u a (s c)", s=2),
                                         in0=bcast(src, [P, HU, HP // 2, 2 * C]),
                                         in1=bcast(pair_mask[:].unsqueeze(1).unsqueeze(3), [P, HU, HP // 2, 2 * C]),
                                         op=ALU.mult)

            small_z, small_rl, small_st = zbank[:, 0:2 * H], obank[:, 1, 2 * H:2 * H + NE], obank[0:NE, 1, P:2 * P]

            def slot(k, lag, size=4):
                return (k - lag) % size

            DECAY = 12 + len(LOG1P)
            ROWS = (((12, 13), (1, 4)), ((13, 14), (4, 5)), ((14, C), (5, 12)))
            EARLY_DECAY = 9
            LANES = 4 + 2 * (C - 1)
            LOADS = 12 + HP
            SETUP_POOL = 16
            SETUP_ACT = 5
            SILU_VEC = 5 + C + HG + 3
            COND_VEC = SILU_VEC + 2 * KC
            SETUP_VEC = COND_VEC + 12

            with nc.Block() as block:
                @block.sync
                def _(sp):
                    loads = [(w_in["q"], wq), (w_in["k"], wk), (w_in["v"], wv), (w_in["g"], wgate)]
                    sp.dma_start(wm, wmod.rearrange("(k p) n -> p k n", p=P)).then_inc(K["c_in"], 16)
                    for dst, src in loads:
                        sp.dma_start(dst[:], src.rearrange("(k p) n -> p k n", p=P)).then_inc(K["c_in"], 16)
                    sp.dma_start(w_ab[:, :, 0:H], walpha.rearrange("(k p) n -> p k n", p=P)).then_inc(K["c_in"], 16)
                    sp.dma_start(w_ab[:, :, H:2 * H], wbeta.rearrange("(k p) n -> p k n", p=P)).then_inc(K["c_in"], 16)
                    sp.dma_start(w_out[:], wout.rearrange("(g p) n -> p g n", p=P)).then_inc(K["c_in"], 16)
                    sp.dma_start(z32[:, 0:H], a_log.partition_broadcast(P)).then_inc(K["c_in"], 16)
                    sp.dma_start(dtb[:, 0:H], dt_bias.partition_broadcast(P)).then_inc(K["c_in"], 16)
                    for g in range(HP):
                        sp.dma_start(rms_col[g * D:(g + 1) * D, :], rms_w.unsqueeze(1)).then_inc(K["c_in"], 16)
                    sp.dma_start(xn[0:NE, :], router_w).then_inc(K["c_in"], 16)
                    sp.dma_start(h[0:B, :], cond).then_inc(K["c_in"], 16)

                    sp.wait_ge(K["c_vec"], SETUP_VEC)

                    def step(n, k):
                        if act_on(n):
                            wait(sp, "xn_done", n - 4)
                            sp.dma_start(rows(x4[:, k, :]), x_v[n]).then_inc(XS[k], 16)
                        o, ko = n - LAG_OUT + 1, slot(k, LAG_OUT - 1)
                        if act_on(o):
                            wait(sp, "x2_done", o - 2)
                            sp.dma_start(rows(xr2[:, ko % 2, :]), x_v[o]).then_inc(XR[ko], 16)
                        o, ko = n - LAG_ROUTE, slot(k, LAG_ROUTE)
                        if act_on(o):
                            wait(sp, "x2_done", o)
                            sp.dma_start(out_v[o], rows(x2_2[:, ko % 2, :])).then_inc(XO[ko], 16)
                            wait(sp, "h2_done", o)
                            sp.dma_start(h2_v[o], rows(h2_2[:, ko % 2, :])).then_inc(HO[ko], 16)
                        o, ko = n - LAG_SCORE, slot(k, LAG_SCORE)
                        if act_on(o):
                            wait(sp, "scT_done", o)
                            sp.dma_start(score_v[o], scT4[:, ko, :].rearrange("e (b i) -> e b i", i=C)) \
                                .then_inc(SO[ko], 16)
                    run(sp, step)
                    for ring in (XO, HO, SO):
                        for s in ring:
                            sp.wait_ge(s, 16 * (NCH // 4))

                @block.gpsimd
                def _(pool):
                    count = [0]

                    def link(ins):
                        count[0] += 1
                        ins.then_inc(K["c_pool"], 1)
                        pool.wait_ge(K["c_pool"], count[0])

                    link(pool.memset(ident[:], 0.0))
                    link(pool.memset(head_mask[:], 1.0))
                    link(pool.affine_select(out=ident[:], in_=ident[:], compare_op=ALU.not_equal, fill=1.0,
                                            base=0, pattern=[[-1, P]], channel_multiplier=1))
                    link(pool.affine_select(out=head_mask[:], in_=head_mask[:], compare_op=ALU.is_ge, fill=0.0,
                                            base=0, pattern=[[-D, HP]], channel_multiplier=1))
                    link(pool.affine_select(out=head_mask[:], in_=head_mask[:], compare_op=ALU.is_ge, fill=0.0,
                                            base=D - 1, pattern=[[D, HP]], channel_multiplier=-1))
                    link(pool.tensor_copy(head_ones[:].rearrange("p (h r) -> p h r", r=D),
                                          bcast(head_mask[:].unsqueeze(2), [P, HP, D])))
                    for tile, value in ((eps_ln, 1e-5), (eps_rms, 1e-6), (one, 1.0), (zero, 0.0)):
                        link(pool.memset(tile[:], value))
                    link(pool.memset(dtb[:, H:], 0.0))
                    for tile in (alpha0, start0, s_diag, ap4, rhs):
                        link(pool.memset(tile[:], 0.0))

                    def diag(dst, src):
                        return pool.tensor_tensor(
                            out=dst, in0=bcast(src.unsqueeze(2), [P, U, HP, C]),
                            in1=bcast(head_mask[:].unsqueeze(1).unsqueeze(3), [P, U, HP, C]), op=ALU.mult)

                    def step(n, k):
                        r, kr = n - LAG_REC, slot(k, LAG_REC)
                        e, ke = n - LAG_ROUTE, slot(k, LAG_ROUTE)
                        g, kg = n - LAG_GRAM, slot(k, LAG_GRAM)
                        o, ko = n - LAG_OUT, slot(k, LAG_OUT)
                        c, kc_ = n - LAG_PROJ, slot(k, LAG_PROJ)
                        if act_on(r):
                            pool.wait_ge(M["t_done"], r - kr % 2 + 2)
                            wait(pool, "delta_mm", r - 2)
                            diag(t_diag2[:, kr % 2], t2[:, kr // 2, kr % 2]).then_inc(M["tdiag_done"], 1)
                        if act_on(e):
                            wait(pool, "xn2_done", e)
                            wait_ring(pool, HO, e - 2, (ke + 2) % 4)
                            wait(pool, "h2t_mm", e - 2)
                            pool.tensor_tensor(out=h2_2[:, ke % 2, :], in0=xn2[:], in1=mod[:, CB, :], op=ALU.mult) \
                                .then_inc(M["h2mul_done"], 1)
                            wait(pool, "h2mul_done", e)
                            pool.tensor_tensor(out=h2_2[:, ke % 2, :], in0=h2_2[:, ke % 2, :], in1=mod[:, SB_, :], op=ALU.add) \
                                .then_inc(M["h2_done"], 1)
                        if act_on(g):
                            wait(pool, "gam_done", g)
                            wait(pool, "q_done", g)
                            wait(pool, "read_mm", g - 4, 2)
                            pool.tensor_tensor(out=mk4[:, kg, :, GK:GQ + 1:2, :],
                                               in0=bcast(gam4[:, kg].unsqueeze(2), [P, U, 2, C]), in1=mk4[:, kg, :, KF:, :],
                                               op=ALU.mult).then_inc(M["gq_done"], 1)
                            pool.tensor_tensor(out=mk4[:, kg, :, GI, :], in0=ident_rep[:],
                                               in1=bcast(gam4[:, kg, :, C - 1:C], [P, U, C]), op=ALU.mult) \
                                .then_inc(M["gi_done"], 1)
                        if act_on(o):
                            wait(pool, "sum_done", o, 2)
                            wait(pool, "gate_done", o)
                            wait(pool, "og_done", o - 1)
                            g8 = gate8[:, o % 8].rearrange("p g (b i) -> p (g b) i", i=C)
                            pool.tensor_tensor(out=o_r[:, 1, :].rearrange("p (u i) -> p u i", i=C), in0=os[:, :, 1, :],
                                               in1=g8, op=ALU.mult) \
                                .then_inc(M["og1_done"], 1)
                        if act_on(n):
                            wait(pool, "xn_done", n)
                            wait(pool, "xt_done", n - 1)
                            pool.tensor_tensor(out=h[:], in0=xn[:], in1=mod[:, CA, :], op=ALU.mult) \
                                .then_inc(M["hmul_done"], 1)
                            wait(pool, "hmul_done", n)
                            pool.tensor_tensor(out=h[:], in0=h[:], in1=mod[:, SA, :], op=ALU.add) \
                                .then_inc(M["h_done"], 1)
                        if act_on(o):
                            wait(pool, "rms_done", o)
                            wait(pool, "og1_done", o)
                            wait(pool, "y_done", o - 2)
                            pool.tensor_tensor(out=og[:, ko % 2].rearrange("p g t -> p (g t)"), in0=o_r[:, 1, :],
                                               in1=o_r[:, 0, :], op=ALU.mult).then_inc(M["og_done"], 1)
                        if act_on(c):
                            wait(pool, "k_done", c)
                            wait(pool, "gram_done", c - 2)
                            diag(k_diag2[:, kc_ % 2], mk4[:, kc_, :, KF, :]).then_inc(M["kdiag_done"], 1)

                        if act_on(r):
                            wait(pool, "sturn_done", *half(r, 1))
                            wait(pool, "read_mm", *half(r, 1))
                            state_diag(pool, 1).then_inc(M["sdiag2_done"], 1)
                        if act_on(o):
                            wait(pool, "yga_done", o)
                            wait_ring(pool, XR, o, ko)
                            wait_ring(pool, XO, o - 2, (ko + 2) % 4)
                            pool.tensor_tensor(out=x2_2[:, ko % 2, :], in0=xn2[:], in1=xr2[:, ko % 2, :], op=ALU.add) \
                                .then_inc(M["x2_done"], 1)

                        if act_on(g):
                            wait(pool, "kturn_done", g)
                            wait(pool, "dk_done", g - 1)
                            pool.tensor_tensor(out=k_tok[:], in0=k_turn[:, :, 0, :], in1=k_turn[:, :, 1, :],
                                               op=ALU.add).then_inc(M["ktok_done"], 1)
                            wait(pool, "ktok_done", g)
                            wait(pool, "add_mm", g - 4, 2)
                            pool.tensor_tensor(out=ap4[:, kg, :, 1, :], in0=k_tok[:],
                                               in1=bcast(dec4[:, kg, :, C - 1:C], [P, U, C]), op=ALU.mult) \
                                .then_inc(M["dk_done"], 1)

                    pool.wait_ge(K["c_vec"], SETUP_VEC)
                    run(pool, step)

                @block.scalar
                def _(act):
                    count = [0]

                    def link(ins):
                        count[0] += 1
                        ins.then_inc(K["c_act"], 1)
                        act.wait_ge(K["c_act"], count[0])

                    act.preload_act_table_set("natural_log_exp_and_others")
                    act.wait_ge(K["c_pool"], SETUP_POOL)
                    act.wait_ge(K["c_in"], LOADS * 16)
                    link(act.activation(x4[0:B, 0, :], h[0:B, :], ACT.Exp, scale=-1.0, bias=zero[0:B, :]))
                    link(act.activation(neg_rate[:], z32[:, 0:H], ACT.Exp, bias=zero[:]))
                    act.wait_ge(K["c_pe"], 3)
                    for m in range(3):
                        link(act.activation(mod[:, 2 * m:2 * m + 2, :].rearrange("p m e -> p (m e)"),
                                            [zbank, qkbank, vgbank][m][:, :], ACT.Copy))

                    def pair(dst, src):
                        for s in range(2):
                            ins = act.activation(dst[:, :, s, :], src, ACT.Copy, scale=head_side[:, s:s + 1])
                        return ins

                    def step(n, k):
                        o, ko = n - LAG_OUT, slot(k, LAG_OUT)
                        e = n - LAG_ROUTE
                        r = n - LAG_REC
                        c, kc_ = n - LAG_PROJ, slot(k, LAG_PROJ)
                        w, kw = n - LAG_SCORE, slot(k, LAG_SCORE)
                        if act_on(o):
                            wait(act, "sum_done", o, 2)
                            wait(act, "rms_done", o - 1)
                            act.activation(o_sq[:].rearrange("p (u c) -> p u c", c=C), os[:, :, 1, :], ACT.Square,
                                           bias=zero[:]).then_inc(M["osq_done"], 1)
                        if act_on(r):
                            for h_ in range(2):
                                wait(act, "read_mm", *half(r, h_))
                                wait(act, "rhsf_done", *half(r, h_))
                                wait(act, "sum_done", *half(r - 1, h_))
                                act.activation(held[:, units(h_)].rearrange("p u a c -> p u (a c)"), banked(h_, ST, OT + 1),
                                               ACT.Copy).then_inc(M["held_done"], 1)
                        if act_on(c):
                            wait(act, "proj_done", c)
                            wait(act, "inv_done", c - 1)
                            act.activation(sqk[:].rearrange("p m t -> p (m t)"), qkbank[:, :], ACT.Square,
                                           bias=zero[:]).then_inc(M["sq_done"], 1)
                        if act_on(c):
                            wait(act, "decay_steps", c, DECAY, 3)
                            act.activation(u32[:], w32[:], ACT.Exp, bias=zero[:]).then_inc(M["expz_done"], 1)
                        if act_on(c):
                            wait(act, "gate_done", c - 1)
                            act.activation(sig[:, 0, :], vgbank[:, E:2 * E], ACT.Exp, scale=-1.0, bias=zero[:]) \
                                .then_inc(M["gate_e"], 1)
                            wait(act, "gate_e", c)
                            act.activation(sig[:, 1, :], sig[:, 0, :], ACT.Ln, bias=one[:]).then_inc(M["gate_l"], 1)
                            wait(act, "gate_l", c)
                            act.activation(sig[:, 2, :], sig[:, 1, :], ACT.Exp, scale=-1.0, bias=zero[:]) \
                                .then_inc(M["gate_s"], 1)
                        if act_on(c):
                            wait(act, "rhsf_done", c - 4, 2)
                            act.activation(v4[:, kc_].rearrange("p u t -> p (u t)"), vgbank[:, 0:E], ACT.Copy) \
                                .then_inc(M["vcopy_done"], 1)
                        if act_on(n):
                            wait(act, "mean_done", n)
                            wait(act, "xn_done", n - 1)
                            act.activation(rstd[:, 1:2], mv[:, 1:2], ACT.Ln, bias=eps_ln[:]).then_inc(M["ln_rstd"], 1)
                            wait(act, "ln_rstd", n)
                            act.activation(rstd[:, 0:1], rstd[:, 1:2], ACT.Exp, scale=-0.5, bias=zero[:]) \
                                .then_inc(M["rstd_done"], 1)
                            wait(act, "rstd_done", n)
                            act.activation(rstd[:, 2:3], mv[:, 0:1], ACT.Copy, scale=rstd[:, 0:1]) \
                                .then_inc(M["shift"], 1)
                            wait(act, "shift", n)
                            act.activation(rstd[:, 3:4], rstd[:, 2:3], ACT.Copy, scale=-1.0).then_inc(M["neg_shift"], 1)
                            wait(act, "neg_shift", n)
                            wait(act, "h_done", n - 1)
                            act.activation(xn[:], x4[:, k, :], ACT.Identity, scale=rstd[:, 0:1], bias=rstd[:, 3:4]) \
                                .then_inc(M["xn_done"], 1)
                        if act_on(c):
                            wait(act, "ss_done", c)
                            act.activation(sqk[:].rearrange("p m t -> p (m t)"), tbank[:, :], ACT.Ln,
                                           bias=zero[:]).then_inc(M["lnss_done"], 1)
                            wait(act, "lnss_done", c)
                            wait(act, "q_done", c - 1)
                            act.activation(inv_norm[:], sqk[:], ACT.Exp, scale=-0.5, bias=zero[:]) \
                                .then_inc(M["inv_done"], 1)
                        if act_on(o):
                            wait(act, "ms_done", o)
                            wait(act, "og_done", o - 1)
                            act.activation(o_sq[:], zbank[:, 128:128 + E], ACT.Ln, scale=1.0 / D ** 2, bias=eps_rms[:]) \
                                .then_inc(M["lnms_done"], 1)
                            wait(act, "lnms_done", o)
                            act.activation(o_r[:, 0, :], o_sq[:], ACT.Exp, scale=-0.5, bias=zero[:]) \
                                .then_inc(M["rms_done"], 1)
                        if act_on(c):
                            wait(act, "decay_steps", c, DECAY, DECAY)
                            wait(act, "ab_done", c - 1)
                            act.activation(decay_rep[:, 0], bcast(ser[:, 5, :].unsqueeze(2), [P, H, C]), ACT.Exp,
                                           bias=zero[:]).then_inc(M["alpha_done"], 1)
                            act.activation(decay_rep[:, 1], bcast(rec[:, H:].unsqueeze(2), [P, H, C]), ACT.Copy) \
                                .then_inc(M["beta_done"], 1)
                        if act_on(r):
                            for h_ in range(2):
                                wait(act, "sum_done", *half(r, h_))
                                wait(act, "sturn_done", *half(r - 1, h_))
                                pair(s_pair[:, units(h_)], os[:, units(h_), 0, :]).then_inc(M["spair_done"], 1)
                        if act_on(e):
                            wait(act, "h2t_mm", e)
                            wait(act, "rl_done", e - 1)
                            act.activation(h2T[:].rearrange("p k t -> p (k t)"), tbank[:, 0:E], ACT.Copy) \
                                .then_inc(M["h2T_done"], 1)
                        if act_on(n):
                            wait(act, "xt_done", n)
                            wait(act, "proj_done", n - 2)
                            act.activation(hT2[:, k % 2].rearrange("p k t -> p (k t)"), tbank[:, 0:E], ACT.Copy) \
                                .then_inc(M["hT_done"], 1)
                        if act_on(w):
                            wait(act, "st_done", w)
                            wait(act, "rl_done", e if act_on(e) else -1)
                            wait_ring(act, SO, w - 4, kw)
                            act.activation(scT4[:, kw, :], small_st, ACT.Copy).then_inc(M["scT_done"], 1)
                        if act_on(e):
                            wait(act, "rl_done", e)
                            wait(act, "expl_done", e - 1)
                            wait(act, "max_done", e - 1)
                            act.activation(logit[:], small_rl, ACT.Copy).then_inc(M["logit_done"], 1)
                        if act_on(c):
                            wait(act, "ab_done", c)
                            wait(act, "gam_done", c - 1)
                            ab = tbank[:, 0:2 * E].rearrange("p (a u i) -> p a u i", a=2, i=C)
                            act.activation(alpha0[:, :, 1:C], ab[:, 0, :, 1:C], ACT.Copy) \
                                .then_inc(M["alpha0_done"], 1)
                            act.activation(start0[:, :, 0:1], ab[:, 0, :, 0:1], ACT.Copy) \
                                .then_inc(M["start0_done"], 1)
                            act.activation(beta4[:, kc_], ab[:, 1], ACT.Copy).then_inc(M["beta_copied"], 1)
                        if act_on(c):
                            wait(act, "k_done", c)
                            wait(act, "kturn_done", c - 1)
                            pair(k_pair[:], mk4[:, kc_, :, KF, :]).then_inc(M["kpair_done"], 1)
                        if act_on(e):
                            wait(act, "max_done", e)
                            wait(act, "sc_done", e - 1)
                            act.activation(expl[:], logit[:], ACT.Exp, bias=nmax[:], accum_out=esum[:, 0:1]) \
                                .then_inc(M["expl_done"], 1)
                        if act_on(o):
                            wait(act, "mean2_done", o)
                            wait(act, "xn2_done", o - 1)
                            act.activation(rstd2[:, 1:2], mv2[:, 1:2], ACT.Ln, bias=eps_ln[:]) \
                                .then_inc(M["ln_rstd2"], 1)
                            wait(act, "ln_rstd2", o)
                            act.activation(rstd2[:, 0:1], rstd2[:, 1:2], ACT.Exp, scale=-0.5, bias=zero[:]) \
                                .then_inc(M["rstd2_done"], 1)
                            wait(act, "rstd2_done", o)
                            act.activation(rstd2[:, 2:3], mv2[:, 0:1], ACT.Copy, scale=rstd2[:, 0:1]) \
                                .then_inc(M["shift2"], 1)
                            wait(act, "shift2", o)
                            act.activation(rstd2[:, 3:4], rstd2[:, 2:3], ACT.Copy, scale=-1.0).then_inc(M["neg_shift2"], 1)
                            wait(act, "neg_shift2", o)
                            act.activation(xn2[:], x2_2[:, ko % 2, :], ACT.Identity, scale=rstd2[:, 0:1], bias=rstd2[:, 3:4]) \
                                .then_inc(M["xn2_done"], 1)
                    run(act, step)

                @block.vector
                def _(v):
                    count = [0]

                    def link(ins):
                        count[0] += 1
                        ins.then_inc(K["c_vec"], 1)
                        v.wait_ge(K["c_vec"], count[0])

                    v.wait_ge(K["c_pool"], SETUP_POOL)
                    v.wait_ge(K["c_in"], LOADS * 16)
                    link(v.tensor_reduce(ident_rep[:, 0, :], ident[:].rearrange("p (h r) -> p r h", r=D), AX.X, ALU.add))
                    link(v.tensor_copy(ident_rep[:, 1:, :], bcast(ident_rep[:, 0:1, :], [P, U - 1, C])))
                    link(v.tensor_reduce(head_side[:], head_mask[:].rearrange("p (a b) -> p b a", b=2), AX.X, ALU.add))
                    link(v.tensor_reduce(pair_mask[:], head_mask[:].rearrange("p (a b) -> p a b", b=2), AX.X, ALU.add))
                    link(v.memset(solved[:], 0.0))
                    for i in range(C):
                        link(v.memset(solved[:, i, :, i:i + 1], 1.0))
                    for g in range(HG):
                        link(v.tensor_scalar(w_out[:, g, :], w_out[:, g, :], rms_col[:, 0:1], D ** -0.5, ALU.mult, ALU.mult))
                    v.wait_ge(K["c_act"], 1)
                    link(v.tensor_scalar(x4[0:B, 1, :], x4[0:B, 0, :], 1.0, None, ALU.add))
                    link(v.reciprocal(x4[0:B, 2, :], x4[0:B, 1, :]))
                    link(v.tensor_tensor(out=x4[0:B, 3, :], in0=x4[0:B, 2, :], in1=h[0:B, :], op=ALU.mult))
                    v.wait_ge(K["c_pe"], 1)
                    for kc in range(KC):
                        link(v.tensor_copy(cT[:, kc, :].rearrange("p (b i) -> p b i", i=C),
                                           bcast(tbank[:, kc * P:kc * P + B].unsqueeze(2), [P, B, C])))
                        link(v.tensor_copy(router_t[:, kc, :], tbank[:, (2 + kc) * P:(2 + kc) * P + NE]))
                    v.wait_ge(K["c_act"], SETUP_ACT)
                    link(v.tensor_scalar(neg_rate[:], neg_rate[:], -1.0, None, ALU.mult))
                    for m in (CA, CB):
                        link(v.tensor_scalar(mod[:, m, :], mod[:, m, :], 1.0, None, ALU.add))
                    for m in (GA, GB):
                        link(v.tensor_scalar(xr2[:, 0, :], mod[:, m, :], 0.0, 2.0, ALU.is_ge, ALU.mult))
                        link(v.scalar_tensor_tensor(out=xr2[:, 1, :], in0=mod[:, m, :], scalar=-1.0,
                                                    in1=mod[:, m, :], op0=ALU.mult, op1=ALU.max))
                        link(v.tensor_scalar(xr2[:, 1, :], xr2[:, 1, :], 0.25, None, ALU.max))
                        link(v.scalar_tensor_tensor(out=mod[:, m, :], in0=xr2[:, 0, :], scalar=-1.0,
                                                    in1=xr2[:, 1, :], op0=ALU.add, op1=ALU.mult))
                    v.wait_ge(K["c_pe"], 4)
                    link(v.tensor_copy(gb_col[:], tbank[:, 0:2 * P].rearrange("p (k b i) -> p k b i", k=KC, i=C)[:, :, :, 0]))
                    assert count[0] == SETUP_VEC, count[0]

                    def solve_row(even, i, reduce=None):
                        if reduce is None:
                            solve_row(even, i, False)
                            solve_row(even, i, True)
                            return
                        base = LANES // 2 * even
                        a = low[:, 0, :].rearrange("p (i h l) -> p i h l", h=2, l=C)[:, i, :, 0:i]
                        t = solved[:, 0:i, :, 0:i].rearrange("p l h j -> p h j l")
                        pr = prod[:, 0:2 * i * i].rearrange("p (h j l) -> p h j l", h=2, l=i)
                        if not reduce:
                            v.wait_ge(M["lanes_steps"], base + 3 + 2 * (i - 1))
                            v.tensor_tensor(out=pr, in0=bcast(a.unsqueeze(2), [P, 2, i, i]), in1=t, op=ALU.mult) \
                                .then_inc(M["lanes_steps"], 1)
                            return
                        v.wait_ge(M["lanes_steps"], base + 4 + 2 * (i - 1))
                        v.tensor_reduce(solved[:, i, :, 0:i], pr, AX.X, ALU.add, negate=True) \
                            .then_inc(M["lanes_steps"], 1)

                    def lanes_in(even, s):
                        lane = low[:].rearrange("p a (i c) -> p a i c", c=32)
                        v.transpose(lane[:, 0].rearrange("p i (c u) -> p i c u", c=2),
                                    ap4[:, s:s + 2, :, 0, :].rearrange("p c u i -> p i c u")) \
                            .then_inc(M["lanes_steps"], 1)
                        v.transpose(lane[:, 1], beta4[:, s:s + 2].rearrange("p c u i -> p i (c u)")) \
                            .then_inc(M["lanes_steps"], 1)
                        v.wait_ge(M["lanes_steps"], LANES // 2 * even + 2)
                        v.tensor_tensor(out=low[:, 0, :], in0=low[:, 0, :], in1=low[:, 1, :], op=ALU.mult) \
                            .then_inc(M["lanes_steps"], 1)

                    def lanes_out(even, s):
                        v.wait_ge(M["lanes_steps"], LANES // 2 * even + 3 + 2 * (C - 1))
                        beta = low[:, 1, :].rearrange("p (j h r) -> p j h r", h=2, r=C)[:, :, :, 0] \
                            .rearrange("p j h -> p h j")
                        v.tensor_tensor(out=solved_b[:], in0=solved[:],
                                        in1=bcast(beta.unsqueeze(1), [P, C, 2, C]), op=ALU.mult) \
                            .then_inc(M["lanes_steps"], 1)
                        v.wait_ge(M["lanes_steps"], LANES // 2 * even + 4 + 2 * (C - 1))
                        wait(v, "tdiag_done", even + 1 - 4)
                        v.transpose(t2[:, s].rearrange("p c u i -> p i (c u)"),
                                    solved_b[:].rearrange("p i h j -> p i (h j)")).then_inc(M["t_done"], 2)

                    def decay_step(base, j):
                        last = 4 + len(LOG1P)
                        v.wait_ge(M["decay_steps"], base + (3 + j))
                        if j == 0:
                            ins = v.tensor_scalar(den[:, 0:H], u32[:, 0:H], 2.0, None, ALU.add)
                        elif j == 1:
                            ins = v.tensor_scalar(den[:, H:], u32[:, H:], 1.0, None, ALU.add)
                        elif j == 2:
                            ins = v.reciprocal(rec[:], den[:])
                        elif j == 3:
                            ins = v.tensor_tensor(out=ser[:, 0, :], in0=u32[:, 0:H], in1=rec[:, 0:H], op=ALU.mult)
                        elif j == 4:
                            ins = v.tensor_tensor(out=ser[:, 1, :], in0=ser[:, 0, :], in1=ser[:, 0, :], op=ALU.mult)
                        elif j == 5:
                            ins = v.tensor_scalar(ser[:, 2, :], ser[:, 1, :], LOG1P[0], None, ALU.mult)
                        elif j <= last:
                            m = j - 6
                            ins = v.scalar_tensor_tensor(out=ser[:, 3 - m % 2, :], in0=ser[:, 2 + m % 2, :],
                                                         scalar=LOG1P[m + 1], in1=ser[:, 1, :], op0=ALU.add, op1=ALU.mult)
                        elif j == last + 1:
                            ins = v.scalar_tensor_tensor(out=ser[:, 4, :], in0=ser[:, 3, :], scalar=1.0,
                                                         in1=ser[:, 0, :], op0=ALU.add, op1=ALU.mult)
                        elif j == last + 2:
                            ins = v.tensor_scalar(ser[:, 2, :], z32[:, 0:H], 0.0, None, ALU.max)
                        elif j == last + 3:
                            ins = v.scalar_tensor_tensor(out=ser[:, 3, :], in0=ser[:, 4, :], scalar=2.0,
                                                         in1=ser[:, 2, :], op0=ALU.mult, op1=ALU.add)
                        else:
                            ins = v.tensor_tensor(out=ser[:, 5, :], in0=ser[:, 3, :], in1=neg_rate[:], op=ALU.mult)
                        ins.then_inc(M["decay_steps"], 1)

                    def step(n, k):
                        r, kr = n - LAG_REC, slot(k, LAG_REC)
                        o, ko = n - LAG_OUT, slot(k, LAG_OUT)
                        g, kg = n - LAG_GRAM, slot(k, LAG_GRAM)
                        c, kc_ = n - LAG_PROJ, slot(k, LAG_PROJ)
                        e = n - LAG_ROUTE
                        w, kw = n - LAG_SCORE, slot(k, LAG_SCORE)
                        first = k % 2 == 1
                        lag = LAG_GRAM + 1 if first else LAG_GRAM + 2
                        even, ps = n - lag, slot(k, lag)
                        solving = act_on(even)


                        def half_rows(place, *parts):
                            row, end = ROWS[place][first]
                            for part in parts:
                                if solving and row + part // 2 < end:
                                    solve_row(even, row + part // 2, part % 2 == 1)

                        def rows_and_decays(place, j0, j1):
                            row, end = ROWS[place][first]
                            for j in range(j0, j1):
                                if act_on(c):
                                    decay_step(base, j)
                                i = row + (j - j0) // 2
                                if solving and i < end:
                                    solve_row(even, i, (j - j0) % 2 == 1)

                        base = c * DECAY if act_on(c) else None
                        if act_on(r):
                            for h_ in range(2):
                                wait(v, "read_mm", *half(r, h_))
                                wait(v, "vcopy_done", r)
                                wait(v, "rpair_done", *half(r - 1, h_))
                                v.tensor_tensor(out=rhs_f[:, units(h_)], in0=v4[:, kr, units(h_)], in1=banked(h_, KST),
                                                op=ALU.subtract).then_inc(M["rhsf_done"], 1)
                            for h_ in range(2):
                                wait(v, "rhsf_done", *half(r, h_))
                                wait(v, "rturn_done", *half(r - 1, h_))
                                v.tensor_tensor(out=r_pair[:, units(h_)],
                                                in0=bcast(rhs_f[:, units(h_)].unsqueeze(2), [P, HU, 2, C]),
                                                in1=bcast(head_side[:].unsqueeze(1).unsqueeze(3), [P, HU, 2, C]),
                                                op=ALU.mult).then_inc(M["rpair_done"], 1)
                            for h_ in range(2):
                                wait(v, "rpair_done", *half(r, h_))
                                wait(v, "rhs_done", *half(r - 1, h_))
                                v.transpose(r_turn[:, units(h_)].rearrange("p u s c -> p (u s c)"),
                                            r_pair[:, units(h_)].rearrange("p u s c -> p (u s c)")) \
                                    .then_inc(M["rturn_done"], 1)
                            for h_ in range(2):
                                wait(v, "rturn_done", *half(r, h_))
                                wait(v, "delta_mm", r - 1)
                                v.tensor_tensor(out=rhs[:, units(h_)], in0=r_turn[:, units(h_), 0, :],
                                                in1=r_turn[:, units(h_), 1, :], op=ALU.add) \
                                    .then_inc(M["rhs_done"], 1)
                        if act_on(n):
                            wait_ring(v, XS, n, k)
                            wait(v, "mean_done", n - 1)
                            v.bn_stats(stats[:], x4[:, k, :]).then_inc(M["stats_done"], 1)
                            wait(v, "rstd_done", n - 1)
                            wait(v, "xn_done", n - 1)
                            wait(v, "stats_done", n)
                            v.tensor_copy(tick[:, 0:1], zero[:])
                            v.bn_aggr(mv[:], stats[:]).then_inc(M["mean_done"], 1)
                        if act_on(c):
                            wait(v, "z_done", c)
                            wait(v, "expz_done", c - 1)
                            v.tensor_tensor(out=z32[:], in0=small_z, in1=dtb[:], op=ALU.add) \
                                .then_inc(M["decay_steps"], 1)
                            v.wait_ge(M["decay_steps"], base + 1)
                            v.scalar_tensor_tensor(out=w32[:, 0:H], in0=z32[:, 0:H], scalar=-1.0, in1=z32[:, 0:H],
                                                   op0=ALU.mult, op1=ALU.min) \
                                .then_inc(M["decay_steps"], 1)
                            v.tensor_scalar(w32[:, H:], z32[:, H:], -1.0, None, ALU.mult) \
                                .then_inc(M["decay_steps"], 1)
                        if act_on(c):
                            wait(v, "expz_done", c)
                            wait(v, "beta_done", c - 1)
                        rows_and_decays(0, 0, EARLY_DECAY)
                        if act_on(r):
                            wait(v, "delta_mm", r)
                            for h_ in range(2):
                                wait(v, "add_mm", *half(r - 1, h_))
                                d_unit = obank[:, 0, :].rearrange("p (u c) -> p u c", c=C)[:, units(h_)]
                                v.tensor_tensor(out=d_diag[:, units(h_)], in0=bcast(d_unit.unsqueeze(2), [P, HU, HP, C]),
                                                in1=bcast(head_mask[:].unsqueeze(1).unsqueeze(3), [P, HU, HP, C]),
                                                op=ALU.mult).then_inc(M["ddiag_done"], 1)
                        if act_on(c):
                            wait(v, "inv_done", c)
                            wait(v, "read_mm", c - 4, 2)
                            for m, name in ((1, "k_done"), (0, "q_done")):
                                v.scalar_tensor_tensor(
                                    out=mk4[:, kc_, :, (QF, KF)[m], :],
                                    in0=inv_norm[:, 2 * m:2 * m + 2, :].rearrange("p g (b i) -> p (g b) i", i=C),
                                    scalar=1e12,
                                    in1=qkbank[:, m * E:(m + 1) * E].rearrange("p (u i) -> p u i", i=C),
                                    op0=ALU.min, op1=ALU.mult).then_inc(M[name], 1)
                        rows_and_decays(1, EARLY_DECAY, DECAY - 3)
                        if act_on(r):
                            wait(v, "osq_done", r - 1)
                            wait(v, "og1_done", r - 1)
                            for h_ in range(2):
                                wait(v, "add_mm", *half(r, h_))
                                wait(v, "spair_done", *half(r - 1, h_))
                                v.tensor_tensor(out=os[:, units(h_)].rearrange("p u a c -> p u (a c)"),
                                                in0=held[:, units(h_)].rearrange("p u a c -> p u (a c)"),
                                                in1=banked(h_, ST, OT + 1), op=ALU.add).then_inc(M["sum_done"], 1)
                            for h_ in range(2):
                                wait(v, "spair_done", *half(r, h_))
                                wait(v, ("sdiag_done", "sdiag2_done")[h_], r - 1)
                                v.transpose(s_turn[:, units(h_)].rearrange("p u s c -> p (u s c)"),
                                            s_pair[:, units(h_)].rearrange("p u s c -> p (u s c)")) \
                                    .then_inc(M["sturn_done"], 1)
                            wait(v, "sturn_done", *half(r, 0))
                            wait(v, "read_mm", *half(r, 0))
                            state_diag(v, 0).then_inc(M["sdiag_done"], 1)
                        half_rows(2, 0)
                        if act_on(g):
                            wait(v, "kpair_done", g)
                            wait(v, "ktok_done", g - 1)
                            v.transpose(k_turn[:].rearrange("p u s c -> p (u s c)"),
                                        k_pair[:].rearrange("p u s c -> p (u s c)")).then_inc(M["kturn_done"], 1)
                        half_rows(2, 1)
                        if act_on(c):
                            wait(v, "gate_s", c)
                            wait(v, "vcopy_done", c)
                            wait(v, "og1_done", c - 8)
                            v.tensor_tensor(out=gate8[:, c % 8].rearrange("p g t -> p (g t)"), in0=vgbank[:, E:],
                                            in1=sig[:, 2, :], op=ALU.mult).then_inc(M["gate_done"], 1)
                        half_rows(2, 2)
                        if act_on(o):
                            wait(v, "y_done", o)
                            wait(v, "h2mul_done", o - 1)
                            v.tensor_tensor(out=xn2[:], in0=zbank[:, 128:128 + E], in1=mod[:, GA, :], op=ALU.mult) \
                                .then_inc(M["yga_done"], 1)
                        half_rows(2, 3)
                        if act_on(e):
                            wait(v, "logit_done", e)
                            v.tensor_reduce(nmax[:], logit[:], AX.X, ALU.max, negate=True).then_inc(M["max_done"], 1)
                        half_rows(2, *range(4, 2 * C))
                        if solving and not first:
                            lanes_out(even, ps // 2)
                        if act_on(c):
                            wait(v, "beta_copied", c)
                            for name in ("ap_done", "dk_done", "gi_done", "gq_done"):
                                wait(v, name, c - 4)
                            v.tensor_tensor_scan(dec4[:, kc_].rearrange("p u i -> p (u i)"),
                                                 alpha0[:].rearrange("p u i -> p (u i)"),
                                                 ident_rep[:].rearrange("p u i -> p (u i)"), 0.0, ALU.mult, ALU.add) \
                                .then_inc(M["dec_done"], 1)
                            v.tensor_tensor_scan(gam4[:, kc_].rearrange("p u i -> p (u i)"),
                                                 alpha0[:].rearrange("p u i -> p (u i)"),
                                                 start0[:].rearrange("p u i -> p (u i)"), 0.0, ALU.mult, ALU.add) \
                                .then_inc(M["gam_done"], 1)
                        if act_on(c):
                            wait(v, "gram_done", c)
                            wait(v, "dec_done", c)
                            wait(v, "add_mm", c - 4, 2)
                            v.tensor_tensor(out=ap4[:, kc_, :, 0:3:2, :], in0=gram[:].rearrange("p u (a i) -> p u a i", a=2),
                                            in1=bcast(dec4[:, kc_].unsqueeze(2), [P, U, 2, C]), op=ALU.mult) \
                                .then_inc(M["ap_done"], 1)
                        if act_on(o):
                            wait(v, "x2_done", o)
                            v.bn_stats(stats2[:], x2_2[:, ko % 2, :]).then_inc(M["stats2_done"], 1)
                            wait(v, "stats2_done", o)
                            wait(v, "xn2_done", o - 1)
                            v.tensor_copy(tick[:, 1:2], zero[:])
                            v.bn_aggr(mv2[:], stats2[:]).then_inc(M["mean2_done"], 1)
                        if act_on(e):
                            wait(v, "expl_done", e)
                            v.reciprocal(esum[:, 1:2], esum[:, 0:1]).then_inc(M["esum_done"], 1)
                            wait(v, "esum_done", e)
                            wait(v, "st_done", e - 1)
                            v.tensor_scalar(sc[:], expl[:], esum[:, 1:2], None, ALU.mult).then_inc(M["sc_done"], 1)
                        if not first and act_on(n - LAG_GRAM):
                            new, lane_slot = n - LAG_GRAM, slot(k, LAG_GRAM)
                            wait(v, "ap_done", new + 1)
                            wait(v, "beta_copied", new + 1)
                            wait(v, "t_done", new - 1)
                            lanes_in(new, lane_slot)
                    run(v, step)

                @block.tensor
                def _(pe):
                    pe.wait_ge(K["c_pool"], SETUP_POOL)
                    pe.wait_ge(K["c_in"], LOADS * 16)
                    pe.wait_ge(K["c_vec"], SILU_VEC)
                    for kc in range(KC):
                        pe.transpose(tbank[:, kc * P:kc * P + B], x4[0:B, 3, kc * P:(kc + 1) * P], ident[0:B, 0:B])
                    for kc in range(KC):
                        ins = pe.transpose(tbank[:, (2 + kc) * P:(2 + kc) * P + NE], xn[0:NE, kc * P:(kc + 1) * P],
                                           ident[0:NE, 0:NE])
                    ins.then_inc(K["c_pe"], 1)
                    pe.wait_ge(K["c_vec"], COND_VEC)
                    for m in range(3):
                        for kc in range(KC):
                            ins = pe.matmul([zbank, qkbank, vgbank][m][:, :], cT[:, kc, :],
                                            wm[:, kc, m * 512:(m + 1) * 512], start=(kc == 0), stop=(kc == KC - 1))
                    ins.then_inc(K["c_pe"], 2)
                    pe.wait_ge(K["c_vec"], SETUP_VEC - 1)
                    for kc in range(KC):
                        ins = pe.transpose(tbank[:, kc * P:(kc + 1) * P], mod[:, GB, kc * P:(kc + 1) * P], ident[:])
                    ins.then_inc(K["c_pe"], 1)
                    pe.wait_ge(K["c_vec"], SETUP_VEC)

                    o_units = obank[:].rearrange("p a (u c) -> p (a u) c", c=C)

                    def twice(h_, j):
                        return rec_block[h_][:, j:HU + 1:HU - j, :]

                    def repeated(ap):
                        return bcast(ap.unsqueeze(1), [P, WIDE // (3 * C), 3 * C])

                    def window(ap, u, end=None):
                        per = ap.shape[-1]
                        stop = u + WIDE // per
                        return ap[:, u:stop if end is None else min(stop, end)]

                    def step(n, k):
                        r, kr = n - LAG_REC, slot(k, LAG_REC)
                        o, ko = n - LAG_OUT, slot(k, LAG_OUT)
                        g, kg = n - LAG_GRAM, slot(k, LAG_GRAM)
                        c, kc_ = n - LAG_PROJ, slot(k, LAG_PROJ)
                        e, ke = n - LAG_ROUTE, slot(k, LAG_ROUTE)
                        w = n - LAG_SCORE
                        if act_on(r):
                            wait(pe, "gq_done", r)
                            wait(pe, "gi_done", r)
                            for h_ in range(2):
                                wait(pe, "sum_done", *half(r - 1, h_))
                                wait(pe, ("sdiag_done", "sdiag2_done")[h_], r - 1)
                                for j in range(HU):
                                    u = h_ * HU + j
                                    ins = pe.matmul(twice(h_, j), s_diag[:, u].rearrange("p g i -> p (g i)"),
                                                    repeated(mk4[:, kr, u, GK:GQ + 1, :].rearrange("p a i -> p (a i)")),
                                                    start=True, stop=True)
                                ins.then_inc(M["read_mm"], 1)
                        if act_on(c):
                            wait(pe, "hT_done", c)
                            wait(pe, "q_done", c - 1)
                            wait(pe, "gate_done", c - 1)
                            wait(pe, "vcopy_done", c - 1)
                            for m, name in enumerate("qkvg"):
                                bank = qkbank if m < 2 else vgbank
                                for hg in range(HG):
                                    for kc in range(KC):
                                        col = (m % 2) * E + hg * P
                                        ins = pe.matmul(bank[:, col:col + P], w_in[name][:, kc, hg * P:(hg + 1) * P],
                                                        hT2[:, kc_ % 2, kc, :], start=(kc == 0), stop=(kc == KC - 1))
                            ins.then_inc(M["proj_done"], 1)
                        if act_on(c):
                            wait(pe, "yga_done", o - 1)
                            for kc in range(KC):
                                ins = pe.matmul(small_z, hT2[:, kc_ % 2, kc, :], w_ab[:, kc, :],
                                                start=(kc == 0), stop=(kc == KC - 1))
                            ins.then_inc(M["z_done"], 1)
                        if act_on(r):
                            wait(pe, "tdiag_done", r)
                            wait(pe, "ddiag_done", r - 1, 2)
                            wait(pe, "logit_done", e - 1)
                            wait(pe, "scT_done", w - 1)
                            wait(pe, "rhs_done", r, 2)
                            for u in range(U):
                                ins = pe.matmul(window(o_units, u), t_diag2[:, kr % 2, u].rearrange("p g i -> p (g i)"),
                                                window(rhs, u), start=True, stop=True)
                            ins.then_inc(M["delta_mm"], 1)
                        if act_on(c):
                            wait(pe, "sq_done", c)
                            wait(pe, "beta_copied", c - 1)
                            pe.matmul(tbank[:, :], head_ones[:], sqk[:].rearrange("p m t -> p (m t)"),
                                      start=True, stop=True).then_inc(M["ss_done"], 1)
                        if act_on(o):
                            wait(pe, "osq_done", o)
                            wait(pe, "yga_done", o - 1)
                            if act_on(c):
                                wait(pe, "decay_steps", c, DECAY, 1)
                            pe.matmul(zbank[:, 128:128 + E], head_ones[:], o_sq[:], start=True, stop=True) \
                                .then_inc(M["ms_done"], 1)
                        if act_on(r):
                            wait(pe, "dk_done", r)
                            wait(pe, "ap_done", r)
                            wait(pe, "rhsf_done", r, 2)
                            for h_ in range(2):
                                wait(pe, "held_done", *half(r, h_))
                                wait(pe, "ddiag_done", *half(r, h_))
                                for j in range(HU):
                                    u = h_ * HU + j
                                    moving = ap4[:, kr, u].rearrange("p a i -> p (a i)")
                                    ins = pe.matmul(twice(h_, j), d_diag[:, u].rearrange("p g i -> p (g i)"),
                                                    repeated(moving), start=True, stop=True)
                                ins.then_inc(M["add_mm"], 1)
                        if act_on(e):
                            wait(pe, "h2_done", e)
                            wait(pe, "beta_copied", c - 1 if not isinstance(c, int) else min(c, NCH) - 1)
                            if act_on(c):
                                wait(pe, "lnss_done", c)
                            for kc in range(KC):
                                ins = pe.transpose(tbank[:, kc * P:(kc + 1) * P], h2_2[:, ke % 2, kc * P:(kc + 1) * P],
                                                   ident[:])
                            ins.then_inc(M["h2t_mm"], 1)
                        wait(pe, "ddiag_done", r if act_on(r) else -1, 2)
                        if act_on(w):
                            wait(pe, "sc_done", w)
                            pe.transpose(small_st, sc[:], ident[:]).then_inc(M["st_done"], 1)
                        if act_on(o):
                            wait(pe, "og_done", o)
                            wait(pe, "lnms_done", o)
                            for hg in range(HG):
                                ins = pe.matmul(zbank[:, 128:128 + E], og[:, ko % 2, hg, :], w_out[:, hg, :],
                                                start=(hg == 0), stop=(hg == HG - 1))
                            ins.then_inc(M["y_done"], 1)
                        if act_on(n):
                            wait(pe, "h_done", n)
                            if act_on(e):
                                wait(pe, "h2T_done", e)
                            if act_on(c):
                                wait(pe, "lnss_done", c)
                            for kc in range(KC):
                                ins = pe.transpose(tbank[:, kc * P:(kc + 1) * P], h[:, kc * P:(kc + 1) * P], ident[:])
                            ins.then_inc(M["xt_done"], 1)
                        if act_on(e):
                            wait(pe, "h2T_done", e)
                            wait(pe, "expl_done", e - 1)
                            for kc in range(KC):
                                ins = pe.matmul(small_rl, h2T[:, kc, :], router_t[:, kc, :],
                                                start=(kc == 0), stop=(kc == KC - 1))
                            ins.then_inc(M["rl_done"], 1)
                        if act_on(c):
                            wait(pe, "kdiag_done", c)
                            wait(pe, "q_done", c)
                            wait(pe, "ap_done", c - 1)
                            keys = mk4[:, kc_, :, KF:QF + 1, :].rearrange("p u a i -> p u (a i)")
                            for u in range(U):
                                ins = pe.matmul(window(gram, u, U), k_diag2[:, kc_ % 2, u].rearrange("p g i -> p (g i)"),
                                                window(keys, u, U), start=True, stop=True)
                            ins.then_inc(M["gram_done"], 1)
                        if act_on(c):
                            wait(pe, "alpha_done", c)
                            wait(pe, "beta_done", c)
                            wait(pe, "lnss_done", c)
                            if act_on(e):
                                wait(pe, "h2T_done", e)
                            if act_on(n):
                                wait(pe, "hT_done", n)
                            for a in range(2):
                                for hg in range(HG):
                                    src = decay_rep[:, a, hg * HP:(hg + 1) * HP, :].rearrange("p h r -> p (h r)")
                                    ins = pe.transpose(tbank[:, (2 * a + hg) * P:(2 * a + hg + 1) * P], src, ident[:])
                            ins.then_inc(M["ab_done"], 1)
                    run(pe, step)


        PAIRS = NE * B
        NT = 3
        TR = -(-CAP // NT)
        width = [min(TR, CAP - t * TR) for t in range(NT)]

        experts = ctx.enter_context(ExitStack())

        def eb(name, shape, dt=F32):
            return experts.enter_context(nc.sbuf_tensor(name, shape, dt))

        score = eb("score", [PAIRS, T])
        best = eb("best", [PAIRS, ROUNDS * 8])
        place = eb("place", [PAIRS, ROUNDS * 8])
        best8 = eb("best8", [PAIRS, 8])
        place8 = eb("place8", [PAIRS, 8], U32)
        batch_hot = eb("batch_hot", [PAIRS, B])
        batch_row = eb("batch_row", [P, B])
        batch_int = eb("batch_int", [P, B], U32)
        batch_base = eb("batch_base", [PAIRS, 1])
        gate_col = eb("gate_col", [TR, NT, PAIRS])
        row_col = eb("row_col", [TR, NT, PAIRS + 2], U32)
        b1_rows = eb("b1_rows", [NE * HID // P, P])
        b2_rows = eb("b2_rows", [NE * KC, P])
        b1_col = eb("b1_col", [P, NE * HID // P])
        b2_col = eb("b2_col", [P, NE * KC])
        w_raw = eb("w_raw", [P, 2, KC * HID])
        w_hi = eb("w_hi", [P, 2, 2, KC * HID])
        w_lo = eb("w_lo", [P, 2, 2, KC * HID])
        b1_now = eb("b1_now", [P, 2, HID // P])
        carry = eb("carry", [P, 128])
        from_row = eb("from_row", [TR, 2, NT], U32)
        to_row = eb("to_row", [TR, 2, NT], U32)
        tok2 = eb("tok2", [TR, 2, NT, E])
        tok_hi2 = eb("tok_hi2", [P, 2, KC, COLS])
        tok_lo2 = eb("tok_lo2", [P, 2, KC, COLS])
        act_full = eb("act_full", [P, HID // P, COLS])
        act_hi2 = eb("act_hi2", [P, 2, HID // P, COLS])
        act_lo2 = eb("act_lo2", [P, 2, HID // P, COLS])
        yT2 = eb("yT2", [P, 2, KC, COLS])
        ys2 = eb("ys2", [TR, 2, NT, E])

        N = sems("scores_in biases_in round_max round_place round_next round_kept best_ready place_ready hot_steps "
                 "lists_turned lists_ready rows_zeroed biases_turned biases_ready b1_picked from_picked to_picked tokT_mm "
                 "tokT_ready tokT_hi last_col_zeroed weights_in w_hi_done w1_lo_done w2_lo_done act_hi_done act_ready up_mm gelu_done down_mm yT_ready back_mm ys_ready")
        GATHERED = [sem(f"gathered{i}") for i in range(2)]
        ADDED = [sem(f"added{i}") for i in range(2)]
        HC = HID // P

        with nc.Block() as block:
            place_of = [-1]

            def settle(eng):
                place_of[0] += 1
                col = slice(place_of[0], place_of[0] + 1)
                if eng is nc.gpsimd:
                    eng.tensor_tensor(out=carry[:, col], in0=zero[:], in1=zero[:], op=ALU.add)
                elif eng is nc.scalar:
                    eng.activation(carry[:, col], zero[:], ACT.Copy)
                else:
                    eng.tensor_copy(carry[:, col], zero[:])

            def wait_added(eng, q, j):
                if isinstance(q, int) and q < 2:
                    return
                eng.wait_ge(ADDED[j], (q - j) * (8 * NT))

            def back(t):
                return [vgbank[0:width[0], 0:E], vgbank[0:width[1], E:2 * E], tbank[0:width[2], 0:E]][t]

            def chain_bank(kc):
                return [rec_banks[:, 0, :], obank[:].rearrange("p a c -> p (a c)")][kc][:, 0:COLS]

            def side_bank(j):
                return [gram[:].rearrange("p u c -> p (u c)"), rec_banks[:, 1, :]][j]

            def up_bank(m):
                return side_bank(m % 2)[:, 0:COLS]

            def each_unit(eng, unit, split=None):
                split = split or (lambda e, par: None)
                split(0, 0)
                split(1, 1)
                unit(0, 0, 0, 0, 0, finish=False)
                unit(1, 1, 0, 0, 1)

                def pairs(first, e, par, start=0):
                    with eng.Fori(start, B // 2) as b2_:
                        for j in range(2):
                            unit(b2_ * 2 + (first + j), b2_ * 2 + j, e, par, j)
                pairs(0, 0, 0, 1)
                split(2, 0)
                pairs(B, 1, 1)
                with eng.Fori(1, NE // 2 - 1) as e2:
                    for par in range(2):
                        split(e2 * 2 + (par + 1), (par + 1) % 2)
                        with eng.Fori(0, B // 2) as b2_:
                            for j in range(2):
                                unit(e2 * (2 * B) + b2_ * 2 + (par * B + j), b2_ * 2 + j, e2 * 2 + par, par, j)
                split(NE - 1, 1)
                pairs((NE - 2) * B, NE - 2, 0)
                pairs((NE - 1) * B, NE - 1, 1)

            def load_weights(sp, e):
                sp.dma_start(w_raw[:, 0, :].rearrange("p (k n) -> p k n", k=KC),
                             w1[e].rearrange("(k p) n -> p k n", p=P)).then_inc(N["weights_in"], 16)
                sp.dma_start(w_raw[:, 1, :].rearrange("p (j n) -> p j n", j=HC),
                             w2[e].rearrange("(j p) n -> p j n", p=P)).then_inc(N["weights_in"], 16)

            @block.sync
            def _(sp):
                sp.dma_start(score[:], score_dram.rearrange("e b t -> (e b) t")).then_inc(N["scores_in"], 16)
                sp.dma_start(b1_rows[:], b1.rearrange("e (j p) -> (e j) p", p=P)).then_inc(N["biases_in"], 16)
                sp.dma_start(b2_rows[:], b2.rearrange("e (k p) -> (e k) p", p=P)).then_inc(N["biases_in"], 16)
                load_weights(sp, 0)
                with sp.Fori(1, NE) as e:
                    sp.wait_ge(N["w1_lo_done"], e)
                    sp.wait_ge(N["w2_lo_done"], e)
                    load_weights(sp, e)

            @block.vector
            def _(v):
                steps = [0]

                def link(ins):
                    steps[0] += 1
                    ins.then_inc(N["hot_steps"], 1)
                    v.wait_ge(N["hot_steps"], steps[0])

                link(v.memset(row_col[:], 0))
                link(v.tensor_reduce(batch_hot[:], ident[0:PAIRS, 0:PAIRS].rearrange("p (e b) -> p b e", b=B),
                                     AX.X, ALU.add))
                v.wait_ge(N["rows_zeroed"], 1)
                link(v.tensor_copy(batch_row[:], batch_int[:]))
                link(v.tensor_tensor(out=batch_hot[:], in0=batch_hot[:], in1=batch_row[0:PAIRS, :], op=ALU.mult))
                link(v.tensor_reduce(batch_base[:], batch_hot[:], AX.X, ALU.add))
                v.wait_ge(N["scores_in"], 16)
                def best_eight(r):
                    if not isinstance(r, int):
                        v.wait_ge(N["round_next"], r)
                        v.wait_ge(N["round_kept"], r * 2)
                        settle(v)
                    v.max(best8[:], score[:]).then_inc(N["round_max"], 1)
                    v.wait_ge(N["round_max"], r + 1)
                    v.tensor_scalar(best[:, bass.ds(r * 8, 8)], best8[:], 1.0, None, ALU.mult) \
                        .then_inc(N["round_kept"], 1)
                    v.max_index(place8[:], best8[:], score[:]).then_inc(N["round_place"], 1)
                    v.wait_ge(N["round_place"], r + 1)
                    v.tensor_scalar(place[:, bass.ds(r * 8, 8)], place8[:], batch_base[:, 0:1], None, ALU.add) \
                        .then_inc(N["round_kept"], 1)
                    v.match_replace(score[:], best8[:], score[:], -1.0).then_inc(N["round_next"], 1)

                best_eight(0)
                with v.Fori(1, ROUNDS) as r:
                    best_eight(r)
                v.wait_ge(N["lists_turned"], 1)
                for src, dst in ((0, gate_col), (1, row_col)):
                    for t in range(NT):
                        w = width[t]
                        v.tensor_copy(dst[0:w, t, 0:PAIRS], side_bank(src)[0:w, t * PAIRS:(t + 1) * PAIRS]) \
                            .then_inc(N["lists_ready"], 1)
                v.wait_ge(N["biases_turned"], 1)
                v.tensor_copy(b1_col[:], rec_banks[:, 0, :][:, 0:NE * HC]) \
                    .then_inc(N["biases_ready"], 1)
                v.tensor_copy(b2_col[:], rec_banks[:, 0, :][:, P:P + NE * KC]) \
                    .then_inc(N["biases_ready"], 1)

                def split_tokens(q, j):
                    v.wait_ge(N["tokT_mm"], q + 1)
                    if not isinstance(q, int) or q >= 2:
                        settle(v)
                    for kc in range(KC):
                        turned = [zbank, qkbank][kc][:, 0:CAP]
                        v.tensor_copy(tok_hi2[:, j, kc, 0:CAP].bitcast(F32R), turned).then_inc(N["tokT_hi"], 1)
                    for kc in range(KC):
                        v.wait_ge(N["tokT_hi"], q * KC + (kc + 1))
                        v.tensor_tensor(out=tok_lo2[:, j, kc, 0:CAP].bitcast(F32R), in0=[zbank, qkbank][kc][:, 0:CAP],
                                        in1=tok_hi2[:, j, kc, 0:CAP], op=ALU.subtract).then_inc(N["tokT_ready"], 1)

                def unit(q, b, e, par, j, turn_next=True, finish=True, start=True):
                    if start:
                        if not isinstance(q, int) or q >= 2:
                            v.wait_ge(N["down_mm"], q - 1)
                            settle(v)
                        for t in range(HC // 2 + 1):
                            if t < HC // 2:
                                v.wait_ge(N["gelu_done"], q * HC + (2 * t + 2))
                                v.tensor_copy(act_hi2[:, j, 2 * t:2 * t + 2, :].bitcast(F32R),
                                              act_full[:, 2 * t:2 * t + 2, :]).then_inc(N["act_hi_done"], 1)
                            if t > 0:
                                v.wait_ge(N["act_hi_done"], q * (HC // 2) + t)
                                part = slice(2 * t - 2, 2 * t)
                                v.tensor_tensor(out=act_lo2[:, j, part, :].bitcast(F32R), in0=act_full[:, part, :],
                                                in1=act_hi2[:, j, part, :], op=ALU.subtract) \
                                    .then_inc(N["act_ready"], 1)
                    if turn_next:
                        split_tokens(q + 1, (j + 1) % 2)
                    if finish:
                        v.wait_ge(N["back_mm"], q)
                        wait_added(v, q - 1, (j + 1) % 2)
                        for t in range(NT):
                            col = gate_col[0:width[t], t, bass.ds(q - 1, 1)]
                            v.tensor_scalar(ys2[0:width[t], (j + 1) % 2, t, :], back(t), col, None, ALU.mult) \
                                .then_inc(N["ys_ready"], 1)
                    if start:
                        v.wait_ge(N["down_mm"], q + 1)
                        for kc in range(KC):
                            v.tensor_scalar(yT2[:, j, kc, :], chain_bank(kc), b2_col[:, bass.ds(e * KC + kc, 1)],
                                            gb_col[:, kc, bass.ds(b, 1)], ALU.add, ALU.mult) \
                                .then_inc(N["yT_ready"], 1)

                def split(e, par):
                    v.wait_ge(N["weights_in"], e * 32 + 32)
                    if not isinstance(e, int) or e >= 2:
                        v.wait_ge(N["down_mm"], (e - 1) * B)
                        settle(v)
                    for m in (1, 0):
                        v.tensor_copy(w_hi[:, par, m, :].bitcast(F32R), w_raw[:, m, :]).then_inc(N["w_hi_done"], 1)
                    v.wait_ge(N["w_hi_done"], e * 2 + 2)
                    if not isinstance(e, int):
                        settle(v)
                    v.tensor_tensor(out=w_lo[:, par, 0, :].bitcast(F32R), in0=w_raw[:, 0, :], in1=w_hi[:, par, 0, :],
                                    op=ALU.subtract).then_inc(N["w1_lo_done"], 1)
                    v.tensor_tensor(out=w_lo[:, par, 1, :].bitcast(F32R), in0=w_raw[:, 1, :], in1=w_hi[:, par, 1, :],
                                    op=ALU.subtract).then_inc(N["w2_lo_done"], 1)

                for part in (tok_hi2, tok_lo2):
                    for j in range(2):
                        for kc in range(KC):
                            v.tensor_copy(part[:, j, kc, CAP:COLS].bitcast(F32R), zero[:, 0:COLS - CAP]) \
                                .then_inc(N["last_col_zeroed"], 1)
                split_tokens(0, 0)
                each_unit(v, unit, split)
                unit(PAIRS, 0, 0, 0, 0, turn_next=False, start=False)

            @block.scalar
            def _(act):
                act.wait_ge(N["biases_ready"], 2)

                def unit(q, b, e, par, j, finish=True):
                    if not isinstance(q, int) or q >= 1:
                        act.wait_ge(N["act_ready"], q * (HC // 2))
                        settle(act)
                    act.activation(b1_now[:, j, :], b1_col[:, bass.ds(e * HC, HC)], ACT.Copy) \
                        .then_inc(N["b1_picked"], 1)
                    act.wait_ge(N["b1_picked"], q + 1)
                    for m in range(HC):
                        act.wait_ge(N["up_mm"], q * HC + (m + 1))
                        act.activation(act_full[:, m, :], up_bank(m), ACT.Gelu,
                                       bias=b1_now[:, j, m:m + 1]).then_inc(N["gelu_done"], 1)
                each_unit(act, unit)

            @block.tensor
            def _(pe):
                pe.wait_ge(N["biases_in"], 32)
                flat = rec_banks[:, 0, :]
                pe.transpose(flat[:, 0:NE * HC], b1_rows[:], ident[0:NE * HC, 0:NE * HC])
                pe.transpose(flat[:, P:P + NE * KC], b2_rows[:], ident[0:NE * KC, 0:NE * KC]) \
                    .then_inc(N["biases_turned"], 1)
                pe.wait_ge(N["round_kept"], ROUNDS * 2)
                for src, rows_ in ((0, best), (1, place)):
                    for t in range(NT):
                        ins = pe.transpose(side_bank(src)[0:width[t], t * PAIRS:(t + 1) * PAIRS],
                                           rows_[:, t * TR:t * TR + width[t]], ident[0:PAIRS, 0:PAIRS])
                ins.then_inc(N["lists_turned"], 1)

                def three_passes(out_, w_up, w_rest, x_up, x_rest, start, stop):
                    pe.matmul(out_, w_up.bitcast(F32R), x_up.bitcast(F32R), start=start, stop=False)
                    pe.matmul(out_, w_up.bitcast(F32R), x_rest.bitcast(F32R), start=False, stop=False)
                    return pe.matmul(out_, w_rest.bitcast(F32R), x_up.bitcast(F32R), start=False, stop=stop)

                def turn(q, j):
                    pe.wait_ge(GATHERED[j % 2], (q - j % 2) * (8 * NT) + 16 * NT)
                    if not isinstance(q, int) or q > 0:
                        pe.wait_ge(N["tokT_ready"], q * KC)
                    for kc in range(KC):
                        for t in range(NT):
                            ins = pe.transpose([zbank, qkbank][kc][:, t * TR:t * TR + width[t]],
                                               tok2[0:width[t], j, t, kc * P:(kc + 1) * P],
                                               ident[0:width[t], 0:width[t]])
                    ins.then_inc(N["tokT_mm"], 1)

                def back_rows(q, j):
                    pe.wait_ge(N["yT_ready"], q * KC + KC)
                    if not isinstance(q, int) or q > 0:
                        pe.wait_ge(N["ys_ready"], q * NT)
                    for t in range(NT):
                        for kc in range(KC):
                            ins = pe.transpose(back(t)[:, kc * P:(kc + 1) * P],
                                               yT2[:, j, kc, t * TR:t * TR + width[t]], ident[:])
                    ins.then_inc(N["back_mm"], 1)

                def unit(q, b, e, par, j, finish=True):
                    if j == 0:
                        pe.wait_ge(N["w1_lo_done"], e + 1)
                    pe.wait_ge(N["tokT_ready"], q * KC + KC)
                    for m in range(HC):
                        if m < 2 and isinstance(q, int) and q == 0:
                            pe.wait_ge(N["lists_ready"], 2 * NT)
                        else:
                            pe.wait_ge(N["gelu_done"], q * HC + (m - 1))
                        for kc in range(KC):
                            col = kc * HID + m * P
                            ins = three_passes(up_bank(m), w_hi[:, par, 0, col:col + P], w_lo[:, par, 0, col:col + P],
                                               tok_hi2[:, j, kc, :], tok_lo2[:, j, kc, :], kc == 0, kc == KC - 1)
                        ins.then_inc(N["up_mm"], 1)
                    turn(q + 1, (j + 1) % 2)
                    if finish:
                        back_rows(q - 1, (j + 1) % 2)
                    if not isinstance(q, int) or q > 0:
                        pe.wait_ge(N["yT_ready"], q * KC)
                    else:
                        pe.wait_ge(N["biases_ready"], 2)
                    if j == 0:
                        pe.wait_ge(N["w2_lo_done"], e + 1)
                    for kc in range(KC):
                        for m in range(HC):
                            if kc == 0 and m % 2 == 0:
                                pe.wait_ge(N["act_ready"], q * (HC // 2) + (m // 2 + 1))
                            col = m * E + kc * P
                            ins = three_passes(chain_bank(kc), w_hi[:, par, 1, col:col + P], w_lo[:, par, 1, col:col + P],
                                               act_hi2[:, j, m, :], act_lo2[:, j, m, :], m == 0, m == HC - 1)
                    ins.then_inc(N["down_mm"], 1)

                turn(0, 0)
                pe.wait_ge(N["last_col_zeroed"], 4 * KC)
                each_unit(pe, unit)
                back_rows(PAIRS - 1, 1)

            @block.gpsimd
            def _(pool):
                pool.iota(batch_int[:], pattern=[[T, B]], base=0, channel_multiplier=0).then_inc(N["rows_zeroed"], 1)
                pool.wait_ge(N["lists_ready"], 2 * NT)

                def gather(q, j):
                    if not isinstance(q, int) or q >= 2:
                        pool.wait_ge(N["tokT_mm"], q - 1)
                    settle(pool)
                    pool.tensor_copy(from_row[:, j, :], row_col[:, :, bass.ds(q, 1)].rearrange("p t o -> p (t o)")) \
                        .then_inc(N["from_picked"], 1)
                    pool.wait_ge(N["from_picked"], q + 1)
                    settle(pool)
                    for t in range(NT):
                        pool.indirect_dma_start(tok2[0:width[t], j, t, :], None, h2_dram,
                                                bass.IndirectOffsetOnAxis(ap=from_row[0:width[t], j, t:t + 1], axis=0)) \
                            .then_inc(GATHERED[j], 16)

                def scatter(q, j):
                    wait_added(pool, q, j)
                    settle(pool)
                    pool.tensor_copy(to_row[:, j, :], row_col[:, :, bass.ds(q, 1)].rearrange("p t o -> p (t o)")) \
                        .then_inc(N["to_picked"], 1)
                    pool.wait_ge(N["to_picked"], q + 1)
                    pool.wait_ge(N["ys_ready"], q * NT + NT)
                    if not isinstance(q, int) or q > 0:
                        other = (j + 1) % 2
                        pool.wait_ge(ADDED[other], (q - 1 - other) * (8 * NT) + 16 * NT)
                    settle(pool)
                    for t in range(NT):
                        pool.indirect_dma_start(out_rows, bass.IndirectOffsetOnAxis(ap=to_row[0:width[t], j, t:t + 1], axis=0),
                                                ys2[0:width[t], j, t, :], None, compute_op=ALU.add) \
                            .then_inc(ADDED[j], 16)

                out_rows = out.rearrange("b t e -> (b t) e")

                gather(0, 0)
                gather(1, 1)

                def unit(q, b, e, par, j, finish=True):
                    gather(q + 2, j)
                    scatter(q, j)
                each_unit(pool, unit)
                for j in range(2):
                    pool.wait_ge(ADDED[j], PAIRS * 8 * NT)
                    pool.wait_ge(GATHERED[j], (PAIRS + 2) * 8 * NT)


_INS = ["L0_attn_x", "L0_attn_Wq", "L0_attn_Wk", "L0_attn_Wv", "L0_attn_Walpha", "L0_attn_Wbeta", "L0_attn_A_log",
        "L0_attn_dt_bias", "L0_attn_Wgate", "L0_attn_Wout", "L0_attn_rms_w", "L0_ffn_router_w", "L0_ffn_w1",
        "L0_ffn_b1", "L0_ffn_w2", "L0_ffn_b2", "L0_c", "L0_wmod"]
_OUTS = [((B, T, E), "float32")]


def kernel(**inputs):
    import numpy as _np
    import concourse.bacc as _bacc
    from concourse import mybir as _mybir
    from concourse.bass_utils import run_bass_kernel_spmd as _run

    nc = _bacc.Bacc("TRN2", target_bir_lowering=False, num_devices=1)
    arrays, args = {}, []
    for name in _INS:
        a = _np.ascontiguousarray(inputs[name])
        arrays[f"in_{name}_dram"] = a
        args.append(nc.dram_tensor(f"in_{name}_dram", a.shape, _mybir.dt.from_np(a.dtype), kind="ExternalInput").ap())
    for i, (shape, dtype) in enumerate(_OUTS):
        dt = _mybir.dt.from_np(_np.dtype(dtype))
        args.append(nc.dram_tensor(f"out_{i}_dram", shape, dt, kind="ExternalOutput").ap())
    program(nc, *args)
    r = _run(nc, [arrays], core_ids=[0])
    got = tuple(r.results[0][f"out_{i}_dram"] for i in range(len(_OUTS)))
    return got[0]
```
